# Optimizing a Trainium2 kernel written in Bass

```python
import numpy as np
import jax
import jax.numpy as jnp

def _softmax(x, axis=-1):
    return jax.nn.softmax(x, axis=axis)

def _gelu(x):
    return jax.nn.gelu(x, approximate=True)

def _silu(x):
    return jax.nn.silu(x)

def _sigmoid(x):
    return jax.nn.sigmoid(x)

def _layernorm(x, axis=-1, eps=1e-05):
    m = jnp.mean(x, axis=axis, keepdims=True)
    v = jnp.var(x, axis=axis, keepdims=True)
    return (x - m) / jnp.sqrt(v + eps)

def _scatter_add(tgt, idx, src, axis=0):
    return tgt.at[idx].add(src)

def _segment_sum(src, seg, n):
    return jax.ops.segment_sum(src, seg, n)
kernel_name = 'mk_gps_d2_gnn_r16_e1eab3'

def setup_inputs(seed: int=0):
    np.random.seed(seed)
    _w = jnp.asarray

    def _rec_inputs():
        import jax
        import jax.numpy as jnp
        _gk = jax.random.key(seed)
        x = -0.0002117 + 1 * jax.random.normal(jax.random.fold_in(_gk, 1), (3125, 256), jnp.float32)
        src = jax.random.randint(jax.random.fold_in(_gk, 2), (50000,), 0, 3125, jnp.int32)
        dst = jnp.minimum((3125 * jax.random.uniform(jax.random.fold_in(_gk, 3), (50000,)) ** 2.0).astype(jnp.int32), 49999)
        _o = jnp.argsort(dst, stable=True)
        src = src[_o]
        dst = dst[_o]
        edge_weight = jax.random.uniform(jax.random.fold_in(_gk, 13), (50000,), jnp.float32, 0.0, 0.03125)
        return (x, src, dst, edge_weight)
    x, src, dst, edge_weight = _rec_inputs()

    def _L0_gnn_setup():
        import jax, jax.numpy as jnp
        import numpy as np
        N_NODES = 6250
        N_EDGES = 200000
        DIM = 256
        LEAKY_SLOPE = 0.2
        EPS = 1e-12
        key = jax.random.key(seed)
        ks = jax.random.split(key, 8)
        embeddings = jax.random.normal(ks[0], (N_NODES, DIM), dtype=jnp.float32)
        edge_src = jax.random.randint(ks[1], (N_EDGES,), 0, N_NODES, dtype=jnp.int32)
        edge_dst = jax.random.randint(ks[2], (N_EDGES,), 0, N_NODES, dtype=jnp.int32)
        edge_val = jax.random.uniform(ks[3], (N_EDGES,), dtype=jnp.float32) / 32.0
        scale = 1.0 / np.sqrt(DIM)
        W1 = jax.random.normal(ks[4], (DIM, DIM), dtype=jnp.float32) * scale
        b1 = jax.random.normal(ks[5], (DIM,), dtype=jnp.float32) * 0.01
        W2 = jax.random.normal(ks[6], (DIM, DIM), dtype=jnp.float32) * scale
        b2 = jax.random.normal(ks[7], (DIM,), dtype=jnp.float32) * 0.01
        return {'embeddings': embeddings, 'edge_src': edge_src, 'edge_dst': edge_dst, 'edge_val': edge_val, 'W1': W1, 'b1': b1, 'W2': W2, 'b2': b2}
    _L0_gnn_all = _L0_gnn_setup()
    _L0_gnn_in = {k: v for k, v in _L0_gnn_all.items() if k in ('W1', 'b1', 'W2', 'b2')}
    del _L0_gnn_all

    def _L0_mix_setup():
        import jax, jax.numpy as jnp
        import numpy as np
        C_CURV = 1.0
        MIN_NORM = 1e-15
        BALL_EPS = 1e-05
        ATT_EPS = 1e-15
        DIM = 32

        def _norm(x):
            return jnp.clip(jnp.linalg.norm(x, axis=-1, keepdims=True), MIN_NORM)

        def proj(x, c):
            maxnorm = (1.0 - BALL_EPS) / jnp.sqrt(c)
            n = _norm(x)
            return jnp.where(n > maxnorm, x / n * maxnorm, x)

        def expmap0(u, c):
            sc = jnp.sqrt(c)
            n = _norm(u)
            return jnp.tanh(sc * n) * u / (sc * n)

        def logmap0(p, c):
            sc = jnp.sqrt(c)
            n = _norm(p)
            return jnp.arctanh(jnp.clip(sc * n, -1.0 + 1e-07, 1.0 - 1e-07)) * p / (sc * n)

        def mobius_add(x, y, c):
            x2 = jnp.sum(x * x, -1, keepdims=True)
            y2 = jnp.sum(y * y, -1, keepdims=True)
            xy = jnp.sum(x * y, -1, keepdims=True)
            num = (1 + 2 * c * xy + c * y2) * x + (1 - c * x2) * y
            den = 1 + 2 * c * xy + c * c * x2 * y2
            return num / jnp.clip(den, MIN_NORM)

        def conv1d(x, w, pad, groups=1):
            return jax.lax.conv_general_dilated(x, w, (1,), [(pad, pad)], dimension_numbers=('NCH', 'OIH', 'NCH'), feature_group_count=groups)

        def batchnorm(x, gamma, beta):
            mean = jnp.mean(x, axis=(0, 2), keepdims=True)
            var = jnp.var(x, axis=(0, 2), keepdims=True)
            xn = (x - mean) * jax.lax.rsqrt(var + 1e-05)
            return gamma[None, :, None] * xn + beta[None, :, None]

        def _reference_tuple_inner(x, w_qkv, bn_gamma, bn_beta, w_dw, w_pw, w_res, b_res):
            c = C_CURV
            h = logmap0(proj(x, c), c)
            h = jnp.transpose(h, (1, 2, 0))
            h = conv1d(h, w_qkv, pad=2)
            h = batchnorm(h, bn_gamma, bn_beta)
            h = jax.nn.relu(jnp.transpose(h, (2, 0, 1)))
            qkv = proj(expmap0(h, c), c)
            t = jnp.transpose(logmap0(proj(qkv, c), c), (1, 2, 0))
            s = conv1d(t, w_dw, pad=2, groups=t.shape[1])
            s = conv1d(s, w_pw, pad=0, groups=t.shape[1] // DIM)
            cat = jnp.concatenate([t, s], axis=1)
            ai = proj(expmap0(jnp.transpose(cat, (2, 0, 1)), c), c)
            t2 = logmap0(proj(ai, c), c)
            L, N, C2 = t2.shape
            g = C2 // (3 * DIM)
            qkv3 = jnp.transpose(t2, (1, 2, 0)).reshape(N, g, 3 * DIM, L)
            q, k, v = jnp.split(qkv3, 3, axis=2)
            q = jax.nn.relu(q)
            k = jax.nn.relu(k)
            vk = jnp.einsum('ngdl,ngel->ngde', v, k)
            out = jnp.einsum('ngde,ngdl->ngdl', vk, q)
            out = out / (jnp.sum(v, -1, keepdims=True) + ATT_EPS)
            out = jnp.transpose(out.reshape(N, g * DIM, L), (2, 0, 1))
            fx_h = proj(expmap0(out, c), c)
            ft = jnp.transpose(logmap0(proj(fx_h, c), c), (1, 2, 0))
            ft = conv1d(ft, w_res, pad=0) + b_res[None, :, None]
            fx = proj(expmap0(jnp.transpose(ft, (2, 0, 1)), c), c)
            residual = mobius_add(fx, x, c)
            return (fx, residual)
        key = jax.random.key(seed)
        ks = jax.random.split(key, 6)
        L, N, C, TD = (128, 16, 256, 256)
        x = jax.random.normal(ks[0], (L, N, C), jnp.float32) * 0.05
        w_qkv = jax.random.normal(ks[1], (3 * TD, C, 5), jnp.float32) / np.sqrt(C * 5)
        bn_gamma = jnp.ones((3 * TD,), jnp.float32)
        bn_beta = jnp.zeros((3 * TD,), jnp.float32)
        w_dw = jax.random.normal(ks[2], (3 * TD, 1, 5), jnp.float32) / np.sqrt(5.0)
        w_pw = jax.random.normal(ks[3], (3 * TD, DIM, 1), jnp.float32) / np.sqrt(DIM)
        w_res = jax.random.normal(ks[4], (C, 2 * TD, 1), jnp.float32) / np.sqrt(2 * TD)
        b_res = jnp.zeros((C,), jnp.float32)
        return {'x': x, 'w_qkv': w_qkv, 'bn_gamma': bn_gamma, 'bn_beta': bn_beta, 'w_dw': w_dw, 'w_pw': w_pw, 'w_res': w_res, 'b_res': b_res}
    _L0_mix_all = _L0_mix_setup()
    _L0_mix_in = {k: v for k, v in _L0_mix_all.items() if k in ('w_qkv', 'bn_gamma', 'bn_beta', 'w_dw', 'w_pw', 'w_res', 'b_res')}
    del _L0_mix_all

    def _L0_ffn_setup():
        import math
        import jax, jax.numpy as jnp
        import numpy as np
        CAPACITY_FACTOR = 1.25
        TOP_K = 2
        LN_EPS = 1e-05

        def _layer_norm(x, gamma, beta):
            mu = jnp.mean(x, axis=-1, keepdims=True)
            var = jnp.var(x, axis=-1, keepdims=True)
            return (x - mu) * jax.lax.rsqrt(var + LN_EPS) * gamma + beta
        key = jax.random.key(seed)
        ks = jax.random.split(key, 4)
        B, S, D, F, E = (8, 256, 256, 512, 8)
        x = jax.random.normal(ks[0], (B, S, D), dtype=jnp.float32)
        Wr = jax.random.normal(ks[1], (D, E), dtype=jnp.float32) / np.sqrt(D)
        br = jnp.zeros((E,), jnp.float32)
        W1 = jax.random.normal(ks[2], (E, D, F), dtype=jnp.float32) / np.sqrt(D)
        b1 = jnp.zeros((E, F), jnp.float32)
        W2 = jax.random.normal(ks[3], (E, F, D), dtype=jnp.float32) / np.sqrt(F)
        b2 = jnp.zeros((E, D), jnp.float32)
        gamma = jnp.ones((D,), jnp.float32)
        beta = jnp.zeros((D,), jnp.float32)
        return {'x': x, 'Wr': Wr, 'br': br, 'W1': W1, 'b1': b1, 'W2': W2, 'b2': b2, 'gamma': gamma, 'beta': beta}
    _L0_ffn_all = _L0_ffn_setup()
    _L0_ffn_in = {k: v for k, v in _L0_ffn_all.items() if k in ('Wr', 'br', 'W1', 'b1', 'W2', 'b2', 'gamma', 'beta')}
    del _L0_ffn_all

    def _L1_gnn_setup():
        import jax, jax.numpy as jnp
        import numpy as np
        N_NODES = 3125
        N_EDGES = 100000
        IN_DIM, HID_DIM, OUT_DIM = (256, 1024, 256)
        key = jax.random.key(seed)
        k1, k2, k3, k4, k5, k6 = jax.random.split(key, 6)
        x = jax.random.normal(k1, (N_NODES, IN_DIM), dtype=jnp.float32)
        edge_index = jax.random.randint(k2, (2, N_EDGES), 0, N_NODES, dtype=jnp.int64)
        W1 = jax.random.normal(k3, (IN_DIM, HID_DIM), dtype=jnp.float32) / np.sqrt(IN_DIM)
        b1 = jax.random.normal(k4, (HID_DIM,), dtype=jnp.float32) * 0.01
        W2 = jax.random.normal(k5, (HID_DIM, OUT_DIM), dtype=jnp.float32) / np.sqrt(HID_DIM)
        b2 = jax.random.normal(k6, (OUT_DIM,), dtype=jnp.float32) * 0.01
        return {'x': x, 'edge_index': edge_index, 'W1': W1, 'b1': b1, 'W2': W2, 'b2': b2}
    _L1_gnn_all = _L1_gnn_setup()
    _L1_gnn_in = {k: v for k, v in _L1_gnn_all.items() if k in ('W1', 'b1', 'W2', 'b2')}
    del _L1_gnn_all

    def _L1_mix_setup():
        import jax, jax.numpy as jnp
        import numpy as np
        EPS = 1e-05

        def _layernorm(x, weight, bias):
            mean = jnp.mean(x, axis=-1, keepdims=True)
            std = jnp.std(x, axis=-1, keepdims=True, ddof=1)
            out = (x - mean) / (std + EPS)
            return weight * out + bias
        key = jax.random.key(seed)
        B, N, C = (4, 2048, 256)
        H, hc = (8, C // 8)
        kx, = jax.random.split(key, 1)
        x = jax.random.normal(kx, (B, N, C), dtype=jnp.float32)
        return {'x': x, 'kln_weight': jnp.ones((H, 1, hc), dtype=jnp.float32), 'kln_bias': jnp.zeros((H, 1, hc), dtype=jnp.float32), 'vln_weight': jnp.ones((H, 1, hc), dtype=jnp.float32), 'vln_bias': jnp.zeros((H, 1, hc), dtype=jnp.float32)}
    _L1_mix_all = _L1_mix_setup()
    _L1_mix_in = {k: v for k, v in _L1_mix_all.items() if k in ('kln_weight', 'kln_bias', 'vln_weight', 'vln_bias')}
    del _L1_mix_all

    def _L1_ffn_setup():
        import jax, jax.numpy as jnp
        import numpy as np
        B, S, H, F, E, K = (8, 256, 256, 512, 16, 2)
        EPS = 1e-05
        key = jax.random.key(seed)
        ks = jax.random.split(key, 9)
        sc = 0.02
        return {'x': jax.random.normal(ks[0], (B, S, H), dtype=jnp.float32), 'gate_w': jax.random.normal(ks[1], (H, E), dtype=jnp.float32) * sc, 'gate_b': jnp.zeros((E,), dtype=jnp.float32), 'w1': jax.random.normal(ks[2], (E, H, F), dtype=jnp.float32) * sc, 'b1': jnp.zeros((E, F), dtype=jnp.float32), 'w2': jax.random.normal(ks[3], (E, F, H), dtype=jnp.float32) * sc, 'b2': jnp.zeros((E, H), dtype=jnp.float32), 'gamma': jnp.ones((H,), dtype=jnp.float32), 'beta': jnp.zeros((H,), dtype=jnp.float32)}
    _L1_ffn_all = _L1_ffn_setup()
    _L1_ffn_in = {k: v for k, v in _L1_ffn_all.items() if k in ('gate_w', 'gate_b', 'w1', 'b1', 'w2', 'b2', 'gamma', 'beta')}
    del _L1_ffn_all
    return {'x': x, 'src': src, 'dst': dst, 'edge_weight': edge_weight, 'L0_gnn_W1': _L0_gnn_in['W1'], 'L0_gnn_b1': _L0_gnn_in['b1'], 'L0_gnn_W2': _L0_gnn_in['W2'], 'L0_gnn_b2': _L0_gnn_in['b2'], 'L0_mix_w_qkv': _L0_mix_in['w_qkv'], 'L0_mix_bn_gamma': _L0_mix_in['bn_gamma'], 'L0_mix_bn_beta': _L0_mix_in['bn_beta'], 'L0_mix_w_dw': _L0_mix_in['w_dw'], 'L0_mix_w_pw': _L0_mix_in['w_pw'], 'L0_mix_w_res': _L0_mix_in['w_res'], 'L0_mix_b_res': _L0_mix_in['b_res'], 'L0_ffn_Wr': _L0_ffn_in['Wr'], 'L0_ffn_br': _L0_ffn_in['br'], 'L0_ffn_W1': _L0_ffn_in['W1'], 'L0_ffn_b1': _L0_ffn_in['b1'], 'L0_ffn_W2': _L0_ffn_in['W2'], 'L0_ffn_b2': _L0_ffn_in['b2'], 'L0_ffn_gamma': _L0_ffn_in['gamma'], 'L0_ffn_beta': _L0_ffn_in['beta'], 'L1_gnn_W1': _L1_gnn_in['W1'], 'L1_gnn_b1': _L1_gnn_in['b1'], 'L1_gnn_W2': _L1_gnn_in['W2'], 'L1_gnn_b2': _L1_gnn_in['b2'], 'L1_mix_kln_weight': _L1_mix_in['kln_weight'], 'L1_mix_kln_bias': _L1_mix_in['kln_bias'], 'L1_mix_vln_weight': _L1_mix_in['vln_weight'], 'L1_mix_vln_bias': _L1_mix_in['vln_bias'], 'L1_ffn_gate_w': _L1_ffn_in['gate_w'], 'L1_ffn_gate_b': _L1_ffn_in['gate_b'], 'L1_ffn_w1': _L1_ffn_in['w1'], 'L1_ffn_b1': _L1_ffn_in['b1'], 'L1_ffn_w2': _L1_ffn_in['w2'], 'L1_ffn_b2': _L1_ffn_in['b2'], 'L1_ffn_gamma': _L1_ffn_in['gamma'], 'L1_ffn_beta': _L1_ffn_in['beta']}

def reference(x, src, dst, edge_weight, L0_gnn_W1, L0_gnn_b1, L0_gnn_W2, L0_gnn_b2, L0_mix_w_qkv, L0_mix_bn_gamma, L0_mix_bn_beta, L0_mix_w_dw, L0_mix_w_pw, L0_mix_w_res, L0_mix_b_res, L0_ffn_Wr, L0_ffn_br, L0_ffn_W1, L0_ffn_b1, L0_ffn_W2, L0_ffn_b2, L0_ffn_gamma, L0_ffn_beta, L1_gnn_W1, L1_gnn_b1, L1_gnn_W2, L1_gnn_b2, L1_mix_kln_weight, L1_mix_kln_bias, L1_mix_vln_weight, L1_mix_vln_bias, L1_ffn_gate_w, L1_ffn_gate_b, L1_ffn_w1, L1_ffn_b1, L1_ffn_w2, L1_ffn_b2, L1_ffn_gamma, L1_ffn_beta):
    import jax
    import jax.numpy as jnp

    def _L0_gnn_ref(embeddings, edge_src, edge_dst, edge_val, W1, b1, W2, b2):
        import jax, jax.numpy as jnp
        import numpy as np
        N_NODES = 6250
        N_EDGES = 200000
        DIM = 256
        LEAKY_SLOPE = 0.2
        EPS = 1e-12
        ego_emb = embeddings @ W1.T + b1
        messages = edge_val[:, None] * embeddings[edge_src]
        neighbor_emb = jax.ops.segment_sum(messages, edge_dst, num_segments=embeddings.shape[0])
        interaction_emb = neighbor_emb * embeddings
        side_emb = (neighbor_emb + interaction_emb) @ W2.T + b2
        out = ego_emb + side_emb
        out = jnp.where(out >= 0, out, LEAKY_SLOPE * out)
        norm = jnp.sqrt(jnp.sum(out * out, axis=1, keepdims=True))
        return out / jnp.maximum(norm, EPS)

    def _L0_mix_ref(x, w_qkv, bn_gamma, bn_beta, w_dw, w_pw, w_res, b_res):
        import jax, jax.numpy as jnp
        import numpy as np
        C_CURV = 1.0
        MIN_NORM = 1e-15
        BALL_EPS = 1e-05
        ATT_EPS = 1e-15
        DIM = 32

        def _norm(x):
            return jnp.clip(jnp.linalg.norm(x, axis=-1, keepdims=True), MIN_NORM)

        def proj(x, c):
            maxnorm = (1.0 - BALL_EPS) / jnp.sqrt(c)
            n = _norm(x)
            return jnp.where(n > maxnorm, x / n * maxnorm, x)

        def expmap0(u, c):
            sc = jnp.sqrt(c)
            n = _norm(u)
            return jnp.tanh(sc * n) * u / (sc * n)

        def logmap0(p, c):
            sc = jnp.sqrt(c)
            n = _norm(p)
            return jnp.arctanh(jnp.clip(sc * n, -1.0 + 1e-07, 1.0 - 1e-07)) * p / (sc * n)

        def mobius_add(x, y, c):
            x2 = jnp.sum(x * x, -1, keepdims=True)
            y2 = jnp.sum(y * y, -1, keepdims=True)
            xy = jnp.sum(x * y, -1, keepdims=True)
            num = (1 + 2 * c * xy + c * y2) * x + (1 - c * x2) * y
            den = 1 + 2 * c * xy + c * c * x2 * y2
            return num / jnp.clip(den, MIN_NORM)

        def conv1d(x, w, pad, groups=1):
            return jax.lax.conv_general_dilated(x, w, (1,), [(pad, pad)], dimension_numbers=('NCH', 'OIH', 'NCH'), feature_group_count=groups)

        def batchnorm(x, gamma, beta):
            mean = jnp.mean(x, axis=(0, 2), keepdims=True)
            var = jnp.var(x, axis=(0, 2), keepdims=True)
            xn = (x - mean) * jax.lax.rsqrt(var + 1e-05)
            return gamma[None, :, None] * xn + beta[None, :, None]

        def _reference_tuple_inner(x, w_qkv, bn_gamma, bn_beta, w_dw, w_pw, w_res, b_res):
            c = C_CURV
            h = logmap0(proj(x, c), c)
            h = jnp.transpose(h, (1, 2, 0))
            h = conv1d(h, w_qkv, pad=2)
            h = batchnorm(h, bn_gamma, bn_beta)
            h = jax.nn.relu(jnp.transpose(h, (2, 0, 1)))
            qkv = proj(expmap0(h, c), c)
            t = jnp.transpose(logmap0(proj(qkv, c), c), (1, 2, 0))
            s = conv1d(t, w_dw, pad=2, groups=t.shape[1])
            s = conv1d(s, w_pw, pad=0, groups=t.shape[1] // DIM)
            cat = jnp.concatenate([t, s], axis=1)
            ai = proj(expmap0(jnp.transpose(cat, (2, 0, 1)), c), c)
            t2 = logmap0(proj(ai, c), c)
            L, N, C2 = t2.shape
            g = C2 // (3 * DIM)
            qkv3 = jnp.transpose(t2, (1, 2, 0)).reshape(N, g, 3 * DIM, L)
            q, k, v = jnp.split(qkv3, 3, axis=2)
            q = jax.nn.relu(q)
            k = jax.nn.relu(k)
            vk = jnp.einsum('ngdl,ngel->ngde', v, k)
            out = jnp.einsum('ngde,ngdl->ngdl', vk, q)
            out = out / (jnp.sum(v, -1, keepdims=True) + ATT_EPS)
            out = jnp.transpose(out.reshape(N, g * DIM, L), (2, 0, 1))
            fx_h = proj(expmap0(out, c), c)
            ft = jnp.transpose(logmap0(proj(fx_h, c), c), (1, 2, 0))
            ft = conv1d(ft, w_res, pad=0) + b_res[None, :, None]
            fx = proj(expmap0(jnp.transpose(ft, (2, 0, 1)), c), c)
            residual = mobius_add(fx, x, c)
            return (fx, residual)
        return _reference_tuple_inner(x, w_qkv, bn_gamma, bn_beta, w_dw, w_pw, w_res, b_res)[0]

    def _L0_ffn_ref(x, Wr, br, W1, b1, W2, b2, gamma, beta):
        import math
        import jax, jax.numpy as jnp
        import numpy as np
        CAPACITY_FACTOR = 1.25
        TOP_K = 2
        LN_EPS = 1e-05

        def _layer_norm(x, gamma, beta):
            mu = jnp.mean(x, axis=-1, keepdims=True)
            var = jnp.var(x, axis=-1, keepdims=True)
            return (x - mu) * jax.lax.rsqrt(var + LN_EPS) * gamma + beta
        B, S, D = x.shape
        E = Wr.shape[1]
        N = B * S
        K = TOP_K
        logits = jnp.mean(x, axis=1) @ Wr + br
        routing_weights = jax.nn.softmax(logits, axis=-1)
        capacity = float(math.ceil(N * CAPACITY_FACTOR / E))
        expected_loads = routing_weights.sum(axis=0) * (N / B)
        scale = jnp.where(expected_loads > capacity, capacity / expected_loads, 1.0)
        routing_weights = jax.nn.softmax(routing_weights * scale, axis=-1)
        rw_tok = jnp.broadcast_to(routing_weights[:, None, :], (B, S, E)).reshape(N, E)
        top_w, top_i = jax.lax.top_k(rw_tok, K)
        top_w = jax.nn.softmax(top_w, axis=-1)
        xf = x.reshape(N, D)
        h = jax.nn.gelu(jnp.einsum('nd,edf->enf', xf, W1) + b1[:, None, :], approximate=False)
        y = jnp.einsum('enf,efd->end', h, W2) + b2[:, None, :]
        w_dense = jnp.zeros((N, E), x.dtype).at[jnp.arange(N)[:, None], top_i].add(top_w)
        out = jnp.einsum('ne,end->nd', w_dense, y).reshape(B, S, D)
        out = _layer_norm(out + x, gamma, beta)
        return out

    def _L1_gnn_ref(x, edge_index, W1, b1, W2, b2):
        import jax, jax.numpy as jnp
        import numpy as np
        N_NODES = 3125
        N_EDGES = 100000
        IN_DIM, HID_DIM, OUT_DIM = (256, 1024, 256)
        num_nodes = x.shape[0]
        src, dst = (edge_index[0], edge_index[1])
        deg = jax.ops.segment_sum(jnp.ones_like(dst, dtype=x.dtype), dst, num_segments=num_nodes)
        dinv = jnp.where(deg > 0, jax.lax.rsqrt(jnp.maximum(deg, 1e-12)), 0.0)
        edge_weight = dinv[src] * dinv[dst]
        msg = edge_weight[:, None] * x[src]
        agg = jax.ops.segment_sum(msg, dst, num_segments=num_nodes)
        h = jax.nn.gelu(agg @ W1 + b1, approximate=False)
        out = h @ W2 + b2
        return out

    def _L1_mix_ref(x, kln_weight, kln_bias, vln_weight, vln_bias):
        import jax, jax.numpy as jnp
        import numpy as np
        EPS = 1e-05

        def _layernorm(x, weight, bias):
            mean = jnp.mean(x, axis=-1, keepdims=True)
            std = jnp.std(x, axis=-1, keepdims=True, ddof=1)
            out = (x - mean) / (std + EPS)
            return weight * out + bias
        B, N, C = x.shape
        H = kln_weight.shape[0]
        hc = C // H
        qkv = x.reshape(B, N, H, hc).transpose(0, 2, 1, 3)
        q = qkv
        k = _layernorm(qkv, kln_weight, kln_bias)
        v = _layernorm(qkv, vln_weight, vln_bias)
        kv = jnp.einsum('bhnd,bhne->bhde', k, v) / N
        out = jnp.einsum('bhnd,bhde->bhne', q, kv)
        out = out.transpose(0, 2, 1, 3).reshape(B, N, C)
        return out + x

    def _L1_ffn_ref(x, gate_w, gate_b, w1, b1, w2, b2, gamma, beta):
        import jax, jax.numpy as jnp
        import numpy as np
        B, S, H, F, E, K = (8, 256, 256, 512, 16, 2)
        EPS = 1e-05
        gate_logits = x @ gate_w + gate_b
        topk_vals, topk_idx = jax.lax.top_k(gate_logits, K)
        topk_w = jax.nn.softmax(topk_vals, axis=-1)
        h = jax.nn.relu(jnp.einsum('bsh,ehf->bsef', x, w1) + b1)
        expert_out = jnp.einsum('bsef,efh->bseh', h, w2) + b2
        sel = jnp.take_along_axis(expert_out, topk_idx[:, :, :, None], axis=2)
        moe = jnp.sum(topk_w[..., None] * sel, axis=2)
        y = x + moe
        mu = jnp.mean(y, axis=-1, keepdims=True)
        var = jnp.var(y, axis=-1, keepdims=True)
        return (y - mu) / jnp.sqrt(var + EPS) * gamma + beta
    edge_index = jnp.stack([src, dst])
    xn = _layernorm(x, axis=-1)
    x = x + _L0_gnn_ref(xn, src, dst, edge_weight, L0_gnn_W1, L0_gnn_b1, L0_gnn_W2, L0_gnn_b2) + _L0_mix_ref(xn[None], L0_mix_w_qkv, L0_mix_bn_gamma, L0_mix_bn_beta, L0_mix_w_dw, L0_mix_w_pw, L0_mix_w_res, L0_mix_b_res)[0]
    x = x + _L0_ffn_ref(_layernorm(x, axis=-1)[None], L0_ffn_Wr, L0_ffn_br, L0_ffn_W1, L0_ffn_b1, L0_ffn_W2, L0_ffn_b2, L0_ffn_gamma, L0_ffn_beta)[0]
    xn = _layernorm(x, axis=-1)
    x = x + _L1_gnn_ref(xn, edge_index, L1_gnn_W1, L1_gnn_b1, L1_gnn_W2, L1_gnn_b2) + _L1_mix_ref(xn[None], L1_mix_kln_weight, L1_mix_kln_bias, L1_mix_vln_weight, L1_mix_vln_bias)[0]
    x = x + _L1_ffn_ref(_layernorm(x, axis=-1)[None], L1_ffn_gate_w, L1_ffn_gate_b, L1_ffn_w1, L1_ffn_b1, L1_ffn_w2, L1_ffn_b2, L1_ffn_gamma, L1_ffn_beta)[0]
    return x

_drawn_inputs = setup_inputs


def setup_inputs(seed=0):
    import zlib

    import numpy as np

    out = dict(_drawn_inputs(seed))
    spreads = {'L0_mix_bn_gamma': (1.0, 0.6),
     'L0_mix_bn_beta': (0.0, 1.46),
     'L0_mix_b_res': (0.0, 0.33),
     'L0_ffn_br': (0.0, 0.8),
     'L0_ffn_b1': (0.0, 0.333),
     'L0_ffn_b2': (0.0, 0.1),
     'L0_ffn_gamma': (1.0, 0.2),
     'L0_ffn_beta': (0.0, 0.1),
     'L1_mix_kln_weight': (1.0, 0.2),
     'L1_mix_kln_bias': (0.0, 0.394),
     'L1_mix_vln_weight': (1.0, 0.2),
     'L1_mix_vln_bias': (0.0, 0.356),
     'L1_ffn_gate_b': (0.0, 0.663),
     'L1_ffn_b1': (0.0, 0.8),
     'L1_ffn_b2': (0.0, 0.557),
     'L1_ffn_gamma': (1.0, 0.2),
     'L1_ffn_beta': (0.0, 0.425)}
    factors = {'edge_weight': 8.0,
     'L0_gnn_b1': 200.0,
     'L0_gnn_W2': 8.0,
     'L0_gnn_b2': 200.0,
     'L0_mix_w_dw': 6.669,
     'L0_mix_w_pw': 6.479,
     'L0_ffn_Wr': 8.0,
     'L1_gnn_b1': 29.766,
     'L1_gnn_b2': 8.0,
     'L1_ffn_gate_w': 2.965,
     'L1_ffn_w1': 4.629,
     'L1_ffn_w2': 3.682,
     'L0_gnn_W1': 3.245}
    for name, (base, spread) in spreads.items():
        noise = np.random.default_rng([zlib.crc32(name.encode()), seed]).standard_normal(out[name].shape)
        drawn = base * np.exp(spread * noise) if base else spread * noise
        out[name] = jnp.asarray(drawn.astype(out[name].dtype))
    for name, factor in factors.items():
        out[name] = (out[name] * factor).astype(out[name].dtype)
    return out
```

```python
import math
from contextlib import ExitStack

import numpy as np
import concourse.bass as bass
from concourse import mybir

F32 = mybir.dt.float32
I32 = mybir.dt.int32
U32 = mybir.dt.uint32
BF16 = mybir.dt.bfloat16
ALU = mybir.AluOpType
ACT = mybir.ActivationFunctionType
AX = mybir.AxisListType
ds = bass.ds

P = 128
N = 3125
D = 256
KD = D // P
E = 50000
U = 5
T = -(-N // P)
NP = T * P
NI = T // U
TAIL = N - (T - 1) * P
assert T % U == 0

C = 4
GE = C * P
B = 4
G = -(-E // (GE * B)) * B
GB = G // B
W = 96
MAXR = -(-N // W)
NA = NP + P
BIG = 16384.0

CH = U * P
HALF = CH // 2
NCH = NP // CH
TD = 3 * D
KQ = TD // P
HID1 = 1024
F0, E0 = 512, 8
F1, E1 = 512, 16
TOPK = 2
HC = 32
HEADS = D // HC
CAPACITY = float(math.ceil(N * 1.25 / E0))

MAXNORM = float(np.float32(1.0 - 1e-5))
ATANH_MAX = math.atanh(MAXNORM)
TINY = 1e-30


class Asked:

    def __init__(self, engine, asked, answered):
        self.engine, self.asked, self.answered, self.n = engine, asked, answered, 0

    def ask(self, instruction):
        self.n += 1
        instruction.then_inc(self.asked, 1)
        self.engine.wait_ge(self.answered, self.n)

    def take(self):
        self.n += 1
        self.engine.wait_ge(self.asked, self.n)

    def give(self, instruction):
        instruction.then_inc(self.answered, 1)


class Chain:

    def __init__(self, engine, semaphore):
        self.engine, self.semaphore = engine, semaphore
        self.before, self.n, self.base = 0, 0, None

    def __call__(self, instruction):
        instruction.then_inc(self.semaphore, 1)
        self.n += 1
        at = self.before + self.n
        self.engine.wait_ge(self.semaphore, at if self.base is None else self.base + at)

    def enter(self, i, per):
        self.before, self.n, self.per, self.base = self.before + self.n, 0, per, i * per

    def leave(self, times):
        assert self.n == self.per, (self.n, self.per)
        self.before, self.n, self.base = self.before + self.per * times, 0, None


def bass_gps_kernel(nc, A, out):
    with ExitStack() as ctx:
        def sb(name, shape, dt=F32):
            return ctx.enter_context(nc.sbuf_tensor(name, shape, dt))

        semaphores = {}

        def S(name):
            if name not in semaphores:
                semaphores[name] = ctx.enter_context(nc.semaphore(name))
            return semaphores[name]

        X = sb("X", [P, T, D])
        XNT = sb("XNT", [P, KD, NP])
        ACC = sb("ACC", [P, KD + 1, NA])
        MB = sb("MB", [P, T, D])
        ident = sb("ident", [P, P])
        iota = sb("iota", [P, W])
        ones = sb("ones", [P, P])
        zeros = sb("zeros", [P, P])
        ones16 = sb("ones16", [P, P], BF16)
        blockones = sb("blockones", [P, P])
        idx = sb("idx", [P, G, C], I32)
        rel0 = sb("rel0", [P, G, C])
        rel = sb("rel", [P, G + 1, C])
        ewt = sb("ewt", [P, G + 1, C])
        base0 = sb("base0", [1, G], I32)
        base = sb("base", [1, G], I32)
        rounds = sb("rounds", [1, 1], I32)
        farthest = sb("farthest", [1, 1])
        idxs = sb("idxs", [P, B, C], I32)
        gath = sb("gath", [P, B, C, D])
        oh = sb("oh", [P, 2, C, W])
        oh16 = sb("oh16", [P, 2, C, W], BF16)
        st = sb("st", [P, T, 6])
        mv = sb("mv", [P, T, 2])
        rs = sb("rs", [P, T])
        nm = sb("nm", [P, T])
        sc = sb("sc", [P, 8, T])
        valid = sb("valid", [P, T])
        dinvc = sb("dinvc", [P, T])
        NWORK = 14720
        work = sb("work", [P, NWORK])
        PS = ctx.enter_context(nc.psum_tensor("PS", [P, 8, 512], F32))
        xn_dram = nc.dram_tensor("xn_table", (NP, D), F32).ap()
        xs_dram = nc.dram_tensor("xs_table", (NP, D), F32).ap()

        def areas(*sizes, start=0):
            at, found = start, []
            for n in sizes:
                found.append(work[:, at:at + n])
                at += n
            assert at <= NWORK, at
            return found

        def v3(ap, b):
            return ap.rearrange("p (a b) -> p a b", b=b)

        gflat = gath[:, :, :, :].rearrange("p s c d -> p (s c d)")
        xb = v3(gflat[:, 0:U * D], D)
        hb = v3(gflat[:, U * D:2 * U * D], D)
        mflat = MB[:, :, :].rearrange("p t d -> p (t d)")

        srow = mflat[0:G, 0:GE].bitcast(I32)
        drow = mflat[0:G, GE:2 * GE].bitcast(I32)
        wrow = mflat[0:G, 2 * GE:3 * GE]
        sf, df, rf, mf = (mflat[0:G, k * GE:(k + 1) * GE] for k in range(3, 7))
        gb2 = mflat[0:G, 7 * GE:7 * GE + 4]

        H0T_, wc_, bd_, wres_, hh_, ks_, hsq_, ssq_, osq_, oo_, ff_, dw_, bn_, bres_ = areas(
            KD * NP, KD * TD, KQ * P, 4 * D, 10 * P, 2 * P, KQ * P, KQ * P, 4 * P, 4 * P, 3 * P, KQ, 6 * KQ, D)
        H0T, wc, bd, wres = v3(H0T_, NP), v3(wc_, TD), v3(bd_, P), v3(wres_, D)
        hh = v3(hh_, P)
        ks, hsq, ssq, osq, oo, ff, bn = (v3(a, P) for a in (ks_, hsq_, ssq_, osq_, oo_, ff_, bn_)) if False else (
            v3(ks_, P), v3(hsq_, P), v3(ssq_, P), v3(osq_, P), v3(oo_, P), v3(ff_, P), v3(bn_, KQ))
        rr = v3(ssq_[:, 0:4 * P], P)
        bng, bnb, bns, bnt, bnu, bnm = (bn[:, i, :] for i in range(6))
        gram = v3(hh_[:, 0:KD * D], D)
        zz, = areas(KD * TD, start=KD * NP + KD * TD + KQ * P + 4 * D + 10 * P)
        zz = v3(zz, TD)
        msum = dw_[:, 0:0]
        w1t_, w2t_, stg_, ust_, brow_ = areas(KD * D, KD * D, U * D, U * D, 3 * D)
        w1t, w2t = v3(w1t_, D), v3(w2t_, D)
        stg = stg_.rearrange("p (u k n) -> p u k n", u=U, k=KD)
        ust = ust_.rearrange("p (u k n) -> p u k n", u=U, k=KD)
        f0w1_, f0w2_, f0h_, f0b1_, f0row_, gb0_, f0r_ = areas(
            TOPK * KD * F0, TOPK * 4 * D, TOPK * 4 * CH, TOPK * 4, 3 * D, 2 * D, 200)
        f0w1 = f0w1_.rearrange("p (e k f) -> p e k f", e=TOPK, k=KD)
        f0w2 = f0w2_.rearrange("p (e k f) -> p e k f", e=TOPK, k=4)
        f0h = f0h_.rearrange("p (e k f) -> p e k f", e=TOPK, k=4)
        gb0 = v3(gb0_, D)
        wr = v3(f0r_[:, 0:KD * E0], E0)
        r0 = v3(f0r_[:, KD * E0:KD * E0 + 10 * E0], E0)
        ysum = f0r_[:, 120:122]
        wexp = f0r_[:, 122:124]
        g1w1_, g1w2_, g1h_, g1b1_, g1row_, kvp_, vwb_, kwc_, z_, = areas(
            KD * HID1, 8 * D, 8 * CH, 8, D, 4 * D, 2 * D, 8, 4 * D)
        g1w1, g1w2, g1h = v3(g1w1_, HID1), v3(g1w2_, D), v3(g1h_, CH)
        zb, csq = z_[:, 0:D], z_[:, D:2 * D]
        hst = v3(z_[:, 2 * D:2 * D + 4 * HEADS], HEADS)
        kv = v3(kvp_[:, 0:D], P)
        kt1, kt2 = v3(kvp_[:, D:2 * D], P), v3(kvp_[:, 2 * D:3 * D], P)
        vwb, vbb = v3(vwb_[:, 0:D], P), v3(vwb_[:, D:2 * D], P)
        stg1 = gflat[:, 0:U * D].rearrange("p (u k n) -> p u k n", u=U, k=KD)
        stg2 = gflat[:, 2 * U * D:3 * U * D].rearrange("p (u k n) -> p u k n", u=U, k=KD)
        e_w1_, e_w2_, e_h_, e_b1_, e_b2_, gb1_, gate_, grow_, lg_, wt_, top_, topi_, kwc_s = areas(
            2 * KD * F1, 2 * 4 * D, 4 * CH, 4 * E1, D, 2 * D, KD * E1, E1, T * E1, T * E1, T * 8, T * 8, 8)
        e_w1 = e_w1_.rearrange("p (s k f) -> p s k f", s=2, k=KD)
        e_w2 = e_w2_.rearrange("p (s k f) -> p s k f", s=2, k=4)
        e_h, gb1, gate = v3(e_h_, CH), v3(gb1_, D), v3(gate_, E1)
        lg, wt, top, topi = v3(lg_, E1), v3(wt_, E1), v3(top_, 8), v3(topi_, 8).bitcast(U32)

        block = ctx.enter_context(nc.Block())

        def stage_end(eng, k):
            eng.drain().then_inc(S("stages"), 1)
            eng.wait_ge(S("stages"), 5 * k)

        def col(ap, t):
            return ap[:, ds(t, 1)]

        def tile_of(ap, t):
            return ap[:, ds(t, 1), :].rearrange("p a b -> p (a b)")

        def row(ap):
            return ap.rearrange("(a n) -> a n", a=1)

        full_groups, last_group = E // GE, E % GE

        def ln_stats(v, ch, root, src, eps):
            with v.Fori(0, NI) as i:
                for u in range(U):
                    ins = nc.vector.bn_stats(tile_of(st, i * U + u), tile_of(src, i * U + u))
                ch.enter(i, 1)
                ch(ins)
            ch.leave(NI)
            for t in range(T):
                ins = nc.vector.bn_aggr(mv[:, t, :], st[:, t, :])
            ch(ins)
            root.ask(nc.vector.tensor_scalar(rs[:, :], mv[:, :, 1], eps, None, ALU.add))
            ch(nc.vector.reciprocal(rs[:, :], rs[:, :]))
            ch(nc.vector.scalar_tensor_tensor(out=nm[:, :], in0=mv[:, :, 0], scalar=-1.0, in1=rs[:, :],
                                              op0=ALU.mult, op1=ALU.mult))

        def root_of(fn, ap, scale=1.0):
            fn.take()
            fn.give(nc.scalar.activation(ap, ap, ACT.Sqrt, scale=scale))

        def ln_tiles_dve(v, s, scaled=None, extra=None):
            with v.Fori(0, NI) as i:
                for u in range(U):
                    t = i * U + u
                    v.wait_ge(S(s + "_tp"), t + 1)
                    nc.vector.tensor_scalar(xb[:, u, :], tile_of(X, t), col(rs, t), col(nm, t),
                                            ALU.mult, ALU.add).then_inc(S(s + "_xb"), 1)
                    if scaled is not None:
                        v.wait_ge(S(s + "_xb"), t + 1)
                        nc.vector.tensor_scalar(hb[:, u, :], xb[:, u, :], col(scaled, t), None,
                                                ALU.mult).then_inc(S(s + "_hb"), 1)
                if extra is not None:
                    for u in range(U):
                        extra(i, u, i * U + u)

        def ln_tiles_pe(pe, s, scaled=False, after=None):
            nc.tensor.sem_inc(S(s + "_tp"), U)
            with pe.Fori(0, NI) as i:
                for u in range(U):
                    t = i * U + u
                    pe.wait_ge(S(s + "_xb"), t + 1)
                    pe.wait_ge(S(s + "_free"), t + 1)
                    for k in range(KD):
                        ins = nc.tensor.transpose(PS[:, u, k * P:(k + 1) * P], xb[:, u, k * P:(k + 1) * P], ident[:, :])
                    if scaled:
                        pe.wait_ge(S(s + "_hb"), t + 1)
                        for k in range(KD):
                            ins = nc.tensor.transpose(PS[:, u, D + k * P:D + (k + 1) * P],
                                                      hb[:, u, k * P:(k + 1) * P], ident[:, :])
                        for m in range(KD):
                            nc.tensor.matmul(PS[:, 5 + m, 0:D], hb[:, u, m * P:(m + 1) * P], hb[:, u, :],
                                             start=False, stop=False, skip_group_check=True)
                            ins = nc.tensor.matmul(PS[:, 7, m:m + 1], hb[:, u, m * P:(m + 1) * P], ones[:, 0:1],
                                                   start=False, stop=False, skip_group_check=True)
                    ins.then_inc(S(s + "_tp"), 1)
                if after is not None:
                    for u in range(U):
                        after(i, u, i * U + u)

        def ln_tiles_act(act, s, table=None, scaled=False, free=None):
            nc.scalar.sem_inc(S(s + "_free"), U)
            if table is None:
                act.wait_ge(S(s + "_nm"), 1)
            with act.Fori(0, NI) as i:
                for u in range(U):
                    t = i * U + u
                    a, b = (rs, nm) if table is None else table
                    nc.scalar.activation(tile_of(MB, t), tile_of(X, t), ACT.Identity, bias=col(b, t),
                                         scale=col(a, t)).then_inc(S(s + "_mb"), 1)
                for u in range(U):
                    t = i * U + u
                    act.wait_ge(S(s + "_tp"), t + 1 + U)
                    ins = nc.scalar.activation(XNT[:, :, ds(t * P, P)], v3(PS[:, u, 0:D], P), ACT.Copy)
                    if scaled:
                        ins = nc.scalar.activation(H0T[:, :, ds(t * P, P)], v3(PS[:, u, D:2 * D], P), ACT.Copy)
                    ins.then_inc(S(s + "_free"), 1)

        def table_store(sp, s, dram):
            with sp.Fori(0, NI) as i:
                sp.wait_ge(S(s + "_mb"), i * U + U)
                sp.dma_start(dram.rearrange("(t p) d -> p t d", p=P)[:, ds(i * U, U), :],
                             MB[:, ds(i * U, U), :]).then_inc(S(s + "_table"), 16)
            sp.wait_ge(S(s + "_table"), 16 * NI)

        def gather_pool(pool, s, dram, n0, b):
            for q in range(B):
                n = n0 + q
                pool.wait_ge(S(s + "_sum"), n + 1)
                nc.gpsimd.tensor_copy(idxs[:, q, :], tile_of(idx, b * B + q)).then_inc(S(s + "_idxs"), 1)
                pool.wait_ge(S(s + "_idxs"), n + 1)
                nc.gpsimd.sem_inc(S("idxs_seen"), 1)
                for j in range(C):
                    nc.gpsimd.indirect_dma_start(
                        out=gath[:, q, j, :], out_offset=None, in_=dram,
                        in_offset=bass.IndirectOffsetOnAxis(ap=idxs[:, q, j:j + 1], axis=0),
                    ).then_inc(S(f"{s}_rows{q}"), 16)

        def gather_pe(pe, s, r, b, q, degrees):
            n = r * G + b * B + q
            h = q % 2
            pe.wait_ge(S(s + "_oh"), r * (G + 1) + b * B + q + 1)
            pe.wait_ge(S(f"{s}_rows{q}"), (r * GB + b + 1) * (16 * C))
            pe.wait_ge(S(s + "_added"), n + 1)
            for k in range(KD):
                for j in range(C):
                    ins = nc.tensor.matmul(PS[:, 5 + h, k * W:(k + 1) * W], gath[:, q, j, k * P:(k + 1) * P],
                                           oh[:, h, j, :], start=j == 0, stop=j == C - 1)
            if degrees:
                for j in range(C):
                    ins = nc.tensor.matmul(PS[:, 5 + h, KD * W:(KD + 1) * W], ones16[:, :], oh16[:, h, j, :],
                                           start=j == 0, stop=j == C - 1)
            ins.then_inc(S(s + "_sum"), 1)

        def windows(s, g, h, weighted):
            for j in range(C):
                at = rel[:, ds(g, 1), j:j + 1].rearrange("p a c -> p (a c)")
                wt_j = ewt[:, ds(g, 1), j:j + 1].rearrange("p a c -> p (a c)")
                if weighted:
                    nc.vector.tensor_scalar(oh16[:, h, j, :], iota[:, :], at, None, ALU.is_equal)
                    ins = nc.vector.tensor_scalar(oh[:, h, j, :], iota[:, :], at, wt_j, ALU.is_equal, ALU.mult)
                else:
                    ins = nc.vector.tensor_scalar(oh[:, h, j, :], iota[:, :], at, None, ALU.is_equal)
            ins.then_inc(S(s + "_oh"), 1)

        def gather_dve(v, s, r, b, q, weighted):
            g = b * B + q
            planes = KD + 1 if weighted else KD
            windows(s, g + 1, (q + 1) % 2, weighted)
            v.wait_ge(S(s + "_sum"), r * G + g + 1 + B)
            start = v.value_load(base[0:1, ds(g, 1)], min_val=0, max_val=N)
            into = ACC[:, 0:planes, ds(start, W)]
            nc.vector.tensor_tensor(into, into, v3(PS[:, 5 + q % 2, 0:planes * W], W), ALU.add)\
                .then_inc(S(s + "_added"), 1)
            v.wait_ge(S(s + "_added"), r * G + g + 1 + 2)

        def next_round(v, s, r):
            nc.vector.tensor_scalar(rel[:, 0:G, :], rel[:, 0:G, :], -float(W), None, ALU.add)\
                .then_inc(S(s + "_round"), 1)
            nc.vector.tensor_scalar(base[:, :], base[:, :], float(W), float(N), ALU.add, ALU.min)\
                .then_inc(S(s + "_round"), 1)
            v.wait_ge(S(s + "_round"), r * 2 + 2)

        def gather_pool_all(pool, s, dram):
            with pool.Fori(0, GB) as b:
                gather_pool(pool, s, dram, b * B, b)
            more = pool.value_load(rounds[0:1, 0:1], min_val=1, max_val=MAXR)
            with pool.If(more > 1):
                with pool.Fori(1, more) as r:
                    with pool.Fori(0, GB) as b:
                        gather_pool(pool, s, dram, r * G + b * B, b)

        def gather_pe_all(pe, s, degrees, step):
            nc.tensor.sem_inc(S(s + "_sum"), B)
            with pe.Fori(0, GB) as b:
                for q in range(B):
                    gather_pe(pe, s, 0, b, q, degrees)
                    step(b, q)
            more = pe.value_load(rounds[0:1, 0:1], min_val=1, max_val=MAXR)
            with pe.If(more > 1):
                with pe.Fori(1, more) as r:
                    with pe.Fori(0, GB) as b:
                        for q in range(B):
                            gather_pe(pe, s, r, b, q, degrees)

        def gather_dve_all(v, s, weighted, step):
            nc.vector.sem_inc(S(s + "_added"), 2)
            windows(s, 0, 0, weighted)
            with v.Fori(0, GB) as b:
                for q in range(B):
                    gather_dve(v, s, 0, b, q, weighted)
                    step(b, q)
            next_round(v, s, 0)
            more = v.value_load(rounds[0:1, 0:1], min_val=1, max_val=MAXR)
            with v.If(more > 1):
                with v.Fori(1, more) as r:
                    windows(s, 0, 0, weighted)
                    with v.Fori(0, GB) as b:
                        for q in range(B):
                            gather_dve(v, s, r, b, q, weighted)
                    next_round(v, s, r)

        def slot(u):
            return PS[:, u % 4, 0:D]

        def slot_free(t, u):
            return t + 1 + {0: 4, 4: 1}.get(u, 0)

        def bank(u):
            return PS[:, u, 0:D]

        def up_pe(pe, s, c, weights, rhs, at0, units):
            for m, w in enumerate(weights):
                for h in range(2):
                    n = m * 2 + h
                    pe.wait_ge(S(s + "_upfree"), at0 + n + 1)
                    for k in range(KD):
                        ins = nc.tensor.matmul(PS[:, 4 + n % 4, 0:HALF], w[k], rhs(k, c * CH + h * HALF),
                                               start=k == 0, stop=k == KD - 1)
                    ins.then_inc(S(s + "_up"), 1)

        def up_act(act, s, c, units, at0, func, bias, into):
            for m in range(units // 2):
                for h in range(2):
                    n = m * 2 + h
                    act.wait_ge(S(s + "_up"), at0 + n + 1)
                    nc.scalar.activation(into(m)[:, h * HALF:(h + 1) * HALF], PS[:, 4 + n % 4, 0:HALF], func,
                                         bias=bias(m)).then_inc(S(s + "_upfree"), 1)

        def epilogue_act(act, s):
            act.wait_ge(S(s + "_nm"), 1)
            with act.Fori(0, NI) as i:
                for u in range(U):
                    t = i * U + u
                    nc.scalar.activation(tile_of(MB, t), tile_of(MB, t), ACT.Identity, bias=col(nm, t),
                                         scale=col(rs, t)).then_inc(S(s + "_mbn"), 1)

        def epilogue_dve(v, ch, s, gb):
            with v.Fori(0, NI) as i:
                ch.enter(i, 3)
                v.wait_ge(S(s + "_mbn"), i * U + U)
                mb = MB[:, ds(i * U, U), :]
                xx = X[:, ds(i * U, U), :]
                ch(nc.vector.tensor_tensor(mb, mb, gb[:, 0:1, :].to_broadcast((P, U, D)), ALU.mult))
                ch(nc.vector.tensor_tensor(mb, mb, gb[:, 1:2, :].to_broadcast((P, U, D)), ALU.add))
                ch(nc.vector.tensor_tensor(xx, xx, mb, ALU.add))
                v.sem_inc(S(s + "_x"), 1)
            ch.leave(NI)

        @block.sync
        def _(sp):
            def load(dst, src, name):
                sp.dma_start(dst, src).then_inc(S(name), 16)

            sp.wait_ge(S("padded"), 4)
            load(X[:, 0:T - 1, :], A["x"][0:(T - 1) * P, :].rearrange("(t p) d -> p t d", p=P), "x_in")
            load(X[0:TAIL, T - 1, :], A["x"][(T - 1) * P:N, :], "x_in")
            for dst, src in ((srow, A["src"]), (drow, A["dst"]), (wrow, A["edge_weight"])):
                load(dst[0:full_groups, :], src[0:full_groups * GE].rearrange("(g e) -> g e", e=GE), "edges")
                load(dst[full_groups:full_groups + 1, 0:last_group], row(src[full_groups * GE:E]), "edges")
            load(wc, A["wc"].rearrange("(k p) o -> p k o", p=P), "w_conv")
            load(bng, A["bn_gamma"], "w_conv")
            load(bnb, A["bn_beta"], "w_conv")
            load(wres, A["w_res"].rearrange("(k p) o -> p k o", p=P), "w_mix")
            sp.wait_ge(S("bd_zero"), 1)
            for q in range(4):
                load(bd[32 * q:32 * q + 32, :, 32 * q:32 * q + 32],
                     A["w_pw"].rearrange("(j p) o -> p j o", p=P)[32 * q:32 * q + 32, :, :], "w_mix")
            load(dw_, A["w_dw"], "w_mix")
            load(bres_, A["b_res"].partition_broadcast(P), "w_mix")
            stage_end(sp, 1)
            table_store(sp, "l0", xn_dram)
            stage_end(sp, 2)
            stage_end(sp, 3)
            load(w1t, A["g0_w1"].rearrange("(k p) o -> p k o", p=P), "w_g0")
            load(w2t, A["g0_w2"].rearrange("(k p) o -> p k o", p=P), "w_g0")
            load(brow_[0:1, 0:D], row(A["g0_b1"]), "w_g0")
            load(brow_[0:1, D:2 * D], row(A["g0_b2"]), "w_g0")
            stage_end(sp, 4)
            load(wr, A["f0_wr"].rearrange("(k p) e -> p k e", p=P), "w_router")
            load(r0[0:1, 0, :], row(A["f0_br"]), "w_router")
            load(gb0[:, 0, :], A["f0_gamma"].partition_broadcast(P), "w_f0n")
            load(gb0[:, 1, :], A["f0_beta"].partition_broadcast(P), "w_f0n")
            sp.wait_ge(S("routed"), 1)
            for k in range(TOPK):
                e = sp.value_load(r0[0:1, 9, k:k + 1].bitcast(I32), min_val=0, max_val=E0 - 1)
                load(f0w1[:, k, :, :], A["f0_w1"].rearrange("e (k p) f -> e p k f", p=P)[ds(e, 1), :, :, :]
                     .rearrange("a p k f -> (a p) k f"), "w_f0")
                load(f0w2[:, k, :, :], A["f0_w2"].rearrange("e (k p) f -> e p k f", p=P)[ds(e, 1), :, :, :]
                     .rearrange("a p k f -> (a p) k f"), "w_f0")
                load(f0b1_[:, 4 * k:4 * k + 4], A["f0_b1"][ds(e, 1), :, :]
                     .rearrange("a p m -> (a p) m"), "w_f0")
                load(f0row_[0:1, k * D:(k + 1) * D], A["f0_b2"][ds(e, 1), :], "w_f0")
            stage_end(sp, 5)
            table_store(sp, "l1", xs_dram)
            stage_end(sp, 6)
            load(g1w1, A["g1_w1"].rearrange("(k p) o -> p k o", p=P), "w_g1")
            load(g1w2, A["g1_w2"].rearrange("(k p) o -> p k o", p=P), "w_g1")
            load(g1b1_, A["g1_b1"], "w_g1")
            load(g1row_[0:1, :], row(A["g1_b2"]), "w_g1")
            load(kwc_[:, 0:2], A["m1_kw"], "w_m1")
            load(kwc_[:, 2:4], A["m1_kb"], "w_m1")
            load(vwb_[:, 0:D], A["m1_vw"].partition_broadcast(P), "w_m1")
            load(vwb_[:, D:2 * D], A["m1_vb"].partition_broadcast(P), "w_m1")
            stage_end(sp, 7)
            stage_end(sp, 8)
            load(gate, A["f1_wg"].rearrange("(k p) e -> p k e", p=P), "w_gate")
            load(grow_[0:1, :], row(A["f1_bg"]), "w_gate")
            load(e_b1_, A["f1_b1"], "w_f1")
            load(e_b2_[0:E1, :], A["f1_b2"], "w_f1")
            load(gb1[:, 0, :], A["f1_gamma"].partition_broadcast(P), "w_f1")
            load(gb1[:, 1, :], A["f1_beta"].partition_broadcast(P), "w_f1")
            with sp.Fori(0, E1 // 2) as i:
                for k in range(2):
                    e = i * 2 + k
                    sp.wait_ge(S("f1_wfree"), e + 1)
                    load(e_w1[:, k, :, :], A["f1_w1"].rearrange("e (k p) f -> e p k f", p=P)[ds(e, 1), :, :, :]
                         .rearrange("a p k f -> (a p) k f"), f"f1_w{k}")
                    load(e_w2[:, k, :, :], A["f1_w2"].rearrange("e (k p) f -> e p k f", p=P)[ds(e, 1), :, :, :]
                         .rearrange("a p k f -> (a p) k f"), f"f1_w{k}")
            with sp.Fori(0, NI - 1) as i:
                sp.wait_ge(S("f1z_x"), i + 1)
                sp.dma_start(out[0:(T - U) * P, :].rearrange("(t p) d -> p t d", p=P)[:, ds(i * U, U), :],
                             X[:, ds(i * U, U), :]).then_inc(S("out"), 16)
            sp.wait_ge(S("f1z_x"), NI)
            sp.dma_start(out[(T - U) * P:(T - 1) * P, :].rearrange("(t p) d -> p t d", p=P),
                         X[:, T - U:T - 1, :]).then_inc(S("out"), 16)
            sp.dma_start(out[(T - 1) * P:N, :], X[0:TAIL, T - 1, :]).then_inc(S("out"), 16)
            sp.wait_ge(S("out"), 16 * (NI + 1))

        @block.gpsimd
        def _(pool):
            nc.gpsimd.memset(srow, 0).then_inc(S("padded"), 1)
            nc.gpsimd.memset(drow, int(BIG)).then_inc(S("padded"), 1)
            nc.gpsimd.memset(wrow, 0.0).then_inc(S("padded"), 1)
            nc.gpsimd.memset(X[:, T - 1, :], 0.0).then_inc(S("padded"), 1)
            nc.gpsimd.memset(bd_, 0.0).then_inc(S("bd_zero"), 1)
            nc.gpsimd.memset(ident[:, :], 0.0).then_inc(S("pool_set"), 1)
            nc.gpsimd.memset(valid[:, :], 1.0).then_inc(S("pool_set"), 1)
            nc.gpsimd.memset(blockones[:, :], 0.0).then_inc(S("pool_set"), 1)
            pool.wait_ge(S("pool_set"), 3)
            nc.gpsimd.affine_select(out=ident[:, :], in_=ident[:, :], compare_op=ALU.not_equal, fill=1.0,
                                    base=0, pattern=[[-1, P]], channel_multiplier=1).then_inc(S("consts"), 1)
            nc.gpsimd.affine_select(out=valid[:, :], in_=valid[:, :], compare_op=ALU.is_ge, fill=0.0,
                                    base=N - 1, pattern=[[-P, T]], channel_multiplier=-1).then_inc(S("consts"), 1)
            for q in range(4):
                pool.wait_ge(S("consts"), q + 2)
                nc.gpsimd.memset(blockones[32 * q:32 * q + 32, 32 * q:32 * q + 32], 1.0).then_inc(S("consts"), 1)
            pool.wait_ge(S("consts"), 6)
            nc.gpsimd.memset(ones[:, :], 1.0).then_inc(S("consts"), 1)
            nc.gpsimd.memset(zeros[:, :], 0.0).then_inc(S("consts"), 1)
            nc.gpsimd.memset(ones16[:, :], 1.0).then_inc(S("consts"), 1)
            nc.gpsimd.iota(iota[:, :], pattern=[[1, W]], base=0, channel_multiplier=0,
                           allow_small_or_imprecise_dtypes=True).then_inc(S("consts"), 1)
            nc.gpsimd.memset(rel[:, :, :], -1.0).then_inc(S("consts"), 1)
            nc.gpsimd.memset(ewt[:, :, :], 0.0).then_inc(S("consts"), 1)
            nc.gpsimd.memset(ACC[:, :, :], 0.0).then_inc(S("consts"), 1)
            stage_end(pool, 1)
            stage_end(pool, 2)
            gather_pool_all(pool, "g0", xn_dram)
            stage_end(pool, 3)
            stage_end(pool, 4)
            nc.gpsimd.memset(ACC[:, 0:KD, :], 0.0)
            stage_end(pool, 5)
            stage_end(pool, 6)
            gather_pool_all(pool, "g1", xs_dram)
            stage_end(pool, 7)
            stage_end(pool, 8)

        @block.scalar
        def _(act):
            fn = Asked(act, S("asked"), S("answered"))
            root_of(fn, rs[:, :])
            fn.take()
            fn.give(nc.scalar.activation(sc[:, 1, :], sc[:, 0, :], ACT.Sqrt))
            fn.take()
            fn.give(nc.scalar.activation(sc[:, 4, :], sc[:, 3, :], ACT.Ln))
            stage_end(act, 1)
            ln_tiles_act(act, "l0", scaled=True)
            act.wait_ge(S("gram"), 1)
            nc.scalar.activation(gram, PS[:, 5:7, 0:D], ACT.Copy).then_inc(S("gram_sb"), 1)
            root_of(fn, bnu)
            stage_end(act, 2)
            nc.scalar.sem_inc(S("mix_ready"), 1)
            with act.Fori(0, T) as t:
                act.wait_ge(S("mix_conv"), t + 1)
                act.wait_ge(S("mix_o"), t + 1)
                for j in range(KQ):
                    nc.scalar.activation(hh[:, 2 + j, :], PS[:, j // 4, (j % 4) * P:(j % 4 + 1) * P], ACT.Relu,
                                         bias=bnt[:, j:j + 1], scale=bns[:, j:j + 1]).then_inc(S("mix_h"), 1)
                act.wait_ge(S("mix_h"), t * KQ + KQ)
                nc.scalar.activation(hsq, hh[:, 2:8, :], ACT.Square).then_inc(S("mix_hsq"), 1)
                act.wait_ge(S("mix_s"), t + 1)
                psf = PS[:, :, :].rearrange("p b n -> p (b n)")[:, 1024:1024 + TD]
                nc.scalar.activation(ks_, psf[:, 2 * P:4 * P], ACT.Relu)
                nc.scalar.activation(ssq_, psf, ACT.Square).then_inc(S("mix_ssq"), 1)
                nc.scalar.activation(hh_[:, 0:2 * P], psf[:, 0:2 * P], ACT.Relu)
                nc.scalar.activation(hh_[:, 8 * P:10 * P], psf[:, 4 * P:6 * P], ACT.Copy).then_inc(S("mix_qv"), 1)
                act.wait_ge(S("mix_f"), t + 1)
                nc.scalar.activation(ff[:, 2, :], ff[:, 1, :], ACT.Sqrt, scale=1e-30).then_inc(S("mix_eps"), 1)
                act.wait_ge(S("mix_o"), t + 1 + 1)
                nc.scalar.activation(osq_, oo_, ACT.Square).then_inc(S("mix_osq"), 1)
            stage_end(act, 3)
            root_of(fn, sc[:, 0, :])
            with act.Fori(0, NI) as i:
                for u in range(U):
                    t = i * U + u
                    act.wait_ge(S("m0_ft"), t + 1)
                    nc.scalar.activation(ust_[:, 0:D], tile_of(MB, t), ACT.Square, accum_out=col(sc[:, 1, :], t))\
                        .then_inc(S("m0_sq"), 1)
                    act.wait_ge(S("m0_sq"), t + 1)
            fn.take()
            nc.scalar.activation(sc[:, 2, :], sc[:, 1, :], ACT.Sqrt).then_inc(S("m0_n4"), 1)
            act.wait_ge(S("m0_n4"), 1)
            fn.give(nc.scalar.activation(sc[:, 3, :], sc[:, 2, :], ACT.Tanh))
            act.wait_ge(S("m0_done"), 1)
            nc.scalar.sem_inc(S("n0_ps_free"), U)
            with act.Fori(0, NI) as i:
                for u in range(U):
                    t = i * U + u
                    act.wait_ge(S("n0_mm"), t + 1)
                    nc.scalar.activation(stg[:, u, :, :], XNT[:, :, ds(t * P, P)], ACT.Copy)\
                        .then_inc(S("n0_stg"), 1)
                for u in range(U):
                    t = i * U + u
                    act.wait_ge(S("n0_y"), t + 1)
                    nc.scalar.activation(brow_[:, 0:D] if False else hb[:, u, :], tile_of(MB, t), ACT.Square,
                                         accum_out=col(sc[:, 1, :], t)).then_inc(S("n0_ss"), 1)
            root_of(fn, sc[:, 1, :])
            stage_end(act, 4)
            root_of(fn, rs[:, :])
            ln_tiles_act(act, "f0")
            for k in range(TOPK + 1):
                fn.take()
                n = E0 if k < 2 else 1
                fn.give(nc.scalar.activation(r0[0:1, 2, 0:n], r0[0:1, 1, 0:n], ACT.Exp))
            nc.scalar.sem_inc(S("f0_upfree"), 4)
            act.wait_ge(S("w_f0"), 16 * 8)
            with act.Fori(0, NCH) as c:
                act.wait_ge(S("f0_dn"), c * U + U)
                for e in range(TOPK):
                    up_act(act, "f0", c, 8, c * 16 + 8 * e, ACT.Gelu,
                           lambda m: f0b1_[:, 4 * e + m:4 * e + m + 1], lambda m: f0h[:, e, m, :])
            root_of(fn, rs[:, :])
            epilogue_act(act, "f0z")
            stage_end(act, 5)
            root_of(fn, ACC[:, KD, 0:NP])
            root_of(fn, rs[:, :])
            act.wait_ge(S("l1_tab"), 1)
            ln_tiles_act(act, "l1", table=(sc[:, 0, :], sc[:, 1, :]))
            stage_end(act, 6)
            with act.Fori(0, T) as t:
                act.wait_ge(S("m1_c"), t + 1)
                nc.scalar.activation(csq, zb, ACT.Square).then_inc(S("m1_sq"), 1)
                act.wait_ge(S("m1_ss"), t + 1)
                nc.scalar.activation(hst[:, 2, :], hst[:, 1, :], ACT.Sqrt, scale=1.0 / (HC - 1))\
                    .then_inc(S("m1_std"), 1)
            stage_end(act, 7)
            nc.scalar.sem_inc(S("g1_upfree"), 4)
            act.wait_ge(S("w_g1"), 16 * 4)
            with act.Fori(0, NCH) as c:
                act.wait_ge(S("g1_dn"), c * U + U)
                up_act(act, "g1", c, 16, c * 16, ACT.Gelu, lambda m: g1b1_[:, m:m + 1], lambda m: g1h[:, m, :])
            stage_end(act, 8)
            root_of(fn, rs[:, :])
            ln_tiles_act(act, "f1")
            fn.take()
            fn.give(nc.scalar.activation(sc[:, 1, :], sc[:, 0, :], ACT.Exp))
            act.wait_ge(S("w_f1"), 16 * 4)
            nc.scalar.sem_inc(S("f1_upfree"), 4)
            with act.Fori(0, E1 // 2) as i:
                for k in range(2):
                    b1s = kwc_s[:, 4 * k:4 * k + 4]
                    nc.scalar.activation(b1s, e_b1_[:, ds((i * 2 + k) * 4, 4)], ACT.Copy).then_inc(S("f1_b1s"), 1)
                    act.wait_ge(S("f1_b1s"), i * 2 + k + 1)
                    act.sem_inc(S("f1_b1_seen"), 1)
                    with act.Fori(0, NCH) as c:
                        n = (i * 2 + k) * NCH + c
                        act.wait_ge(S("f1_dn"), n * U + U)
                        up_act(act, "f1", c, 8, n * 8, ACT.Relu,
                               lambda m: b1s[:, m:m + 1], lambda m: e_h[:, m, :])
            root_of(fn, rs[:, :])
            epilogue_act(act, "f1z")

        @block.tensor
        def _(pe):
            pe.wait_ge(S("consts"), 13)
            for q, rows in enumerate((sf, rf, wrow)):
                pe.wait_ge(S("tab_rows"), q + 1)
                for j in range(C):
                    ins = nc.tensor.transpose(PS[:, q, j * P:j * P + G], rows[:, j * P:(j + 1) * P], ident[0:G, 0:G])
                ins.then_inc(S("tab_t"), 1)
            pe.wait_ge(S("tab_rows"), 4)
            nc.tensor.transpose(PS[0:1, 3, 0:G], gb2[:, 0:1], ident[0:G, 0:G])
            nc.tensor.transpose(PS[0:1, 3, P:P + G], gb2[:, 1:2], ident[0:G, 0:G]).then_inc(S("tab_t"), 1)
            stage_end(pe, 1)
            for m in range(KD):
                nc.tensor.matmul(PS[:, 5 + m, 0:P], zeros[:, :], ident[:, :], start=True, stop=False, skip_group_check=True)
                nc.tensor.matmul(PS[:, 5 + m, P:D], zeros[:, :], ident[:, :], start=False, stop=False, skip_group_check=True)
            nc.tensor.matmul(PS[:, 7, 0:KD], zeros[:, :], ident[:, 0:KD], start=True, stop=False, skip_group_check=True)
            ln_tiles_pe(pe, "l0", scaled=True)
            for m in range(KD):
                nc.tensor.matmul(PS[:, 5 + m, 0:P], zeros[:, :], ident[:, :], start=False, stop=True, skip_group_check=True)
            nc.tensor.matmul(PS[:, 7, 0:KD], zeros[:, :], ident[:, 0:KD], start=False, stop=True,
                             skip_group_check=True).then_inc(S("gram"), 1)
            pe.wait_ge(S("w_conv"), 16 * 3)
            pe.wait_ge(S("gram_sb"), 2)
            pe.wait_ge(S("l0_free"), T + U)
            for m in range(KD):
                for h in range(2):
                    for k in range(KD):
                        ins = nc.tensor.matmul(PS[:, 2 * m + h, 0:TD // 2], gram[:, k, m * P:(m + 1) * P],
                                               wc[:, k, h * (TD // 2):(h + 1) * (TD // 2)], start=k == 0, stop=k == KD - 1)
            ins.then_inc(S("bn_cw"), 1)
            for j in range(KQ):
                for k in range(KD):
                    nc.tensor.matmul(PS[:, 7, 8 + j:9 + j], wc[:, k, j * P:(j + 1) * P], sc[:, 7, k:k + 1],
                                     start=k == 0, stop=k == KD - 1)
            pe.wait_ge(S("bn_zz"), 1)
            for j in range(KQ):
                for k in range(KD):
                    ins = nc.tensor.matmul(PS[:, 7, 16 + j:17 + j], zz[:, k, j * P:(j + 1) * P], ones[:, 0:1],
                                           start=k == 0, stop=k == KD - 1)
            ins.then_inc(S("bn_sums"), 1)
            stage_end(pe, 2)

            def mixer_pe(t, q):
                if q == 0:
                    pe.wait_ge(S("mix_read"), t + 1)
                    for j in range(KQ):
                        for k in range(KD):
                            ins = nc.tensor.matmul(PS[:, j // 4, (j % 4) * P:(j % 4 + 1) * P],
                                                   wc[:, k, j * P:(j + 1) * P], H0T[:, k, ds(t * P, P)],
                                                   start=k == 0, stop=k == KD - 1)
                    ins.then_inc(S("mix_conv"), 1)
                elif q == 1:
                    pe.wait_ge(S("mix_h"), t * KQ + KQ)
                    for j in range(KQ):
                        ins = nc.tensor.matmul(PS[:, 2 + j // 4, (j % 4) * P:(j % 4 + 1) * P], bd[:, j, :],
                                               hh[:, 2 + j, :], start=True, stop=True)
                    ins.then_inc(S("mix_s"), 1)
                    for j in range(2):
                        nc.tensor.matmul(PS[:, 4, j * P:(j + 1) * P], blockones[:, :], hh[:, 4 + j, :],
                                         start=True, stop=True)
                    pe.wait_ge(S("mix_hsq"), t + 1)
                    for j in range(KQ):
                        nc.tensor.matmul(PS[:, 7, 0:P], ones[:, :], hsq[:, j, :], start=j == 0, stop=j == KQ - 1)
                elif q == 2:
                    pe.wait_ge(S("mix_ssq"), t + 1)
                    for j in range(KQ):
                        ins = nc.tensor.matmul(PS[:, 7, P:2 * P], ones[:, :], ssq[:, j, :], start=j == 0, stop=j == KQ - 1)
                    for j in range(2):
                        ins = nc.tensor.matmul(PS[:, 4, (2 + j) * P:(3 + j) * P], blockones[:, :], ks[:, j, :],
                                               start=True, stop=True)
                    ins.then_inc(S("mix_sums"), 1)
                else:
                    pe.wait_ge(S("mix_o"), t + 1 + 1)
                    for j in range(4):
                        nc.tensor.matmul(PS[:, 7, D:2 * D], oo[:, j, :], wres[:, j, :], start=j == 0, stop=j == 3)
                    pe.wait_ge(S("mix_osq"), t + 1)
                    for j in range(4):
                        ins = nc.tensor.matmul(PS[:, 1, D:D + 1], osq[:, j, :], ones[:, 0:1], start=j == 0, stop=j == 3)
                    ins.then_inc(S("mix_ft"), 1)

            gather_pe_all(pe, "g0", True, mixer_pe)
            stage_end(pe, 3)
            nc.tensor.sem_inc(S("n0_mm"), U)
            pe.wait_ge(S("w_g0"), 16 * 4)
            pe.wait_ge(S("n0_brow"), 1)
            with pe.Fori(0, NI) as i:
                for u in range(U):
                    t = i * U + u
                    pe.wait_ge(S("n0_stg"), t + 1)
                    pe.wait_ge(S("n0_u"), t + 1)
                    pe.wait_ge(S("n0_y"), t + 1 - U) if False else None
                    pe.wait_ge(S("n0_ps"), t + 1)
                    nc.tensor.matmul(bank(u), ones[0:1, :], brow_[0:1, 2 * D:3 * D], start=True, stop=False)
                    for k in range(KD):
                        nc.tensor.matmul(bank(u), stg[:, u, k, :], w1t[:, k, :], start=False, stop=False)
                    for k in range(KD):
                        ins = nc.tensor.matmul(bank(u), ust[:, u, k, :], w2t[:, k, :], start=False, stop=k == KD - 1)
                    ins.then_inc(S("n0_mm"), 1)
            stage_end(pe, 4)
            ln_tiles_pe(pe, "f0")
            pe.wait_ge(S("f0_ysum"), 1)
            pe.wait_ge(S("w_router"), 32)
            for k in range(KD):
                ins = nc.tensor.matmul(PS[0:1, 5, 0:E0], ysum[:, k:k + 1], wr[:, k, :], start=k == 0, stop=k == KD - 1)
            ins.then_inc(S("route_mm"), 1)
            pe.wait_ge(S("routed"), 1)
            nc.tensor.matmul(PS[:, 3, 0:TOPK], ones[0:1, :], r0[0:1, 8, 0:TOPK], start=True, stop=True)\
                .then_inc(S("route_mm"), 1)
            nc.tensor.sem_inc(S("f0_dn"), U)
            pe.wait_ge(S("w_f0"), 16 * 8)
            with pe.Fori(0, NCH) as c:
                for e in range(TOPK):
                    up_pe(pe, "f0", c, [[f0w1[:, e, k, m * P:(m + 1) * P] for k in range(KD)] for m in range(4)],
                          lambda k, at: XNT[:, k, ds(at, HALF)], c * 16 + 8 * e, 8)
                pe.wait_ge(S("f0_upfree"), c * 16 + 16 + 4)
                pe.wait_ge(S("f0_w2s"), 1)
                for u in range(U):
                    pe.wait_ge(S("f0_dfree"), slot_free(c * U + u, u))
                    nc.tensor.matmul(slot(u), ones[0:1, :], f0row_[0:1, 2 * D:3 * D], start=True, stop=False)
                    for e in range(TOPK):
                        for k in range(4):
                            ins = nc.tensor.matmul(slot(u), f0h[:, e, k, u * P:(u + 1) * P], f0w2[:, e, k, :],
                                                   start=False, stop=(e, k) == (TOPK - 1, 3))
                    ins.then_inc(S("f0_dn"), 1)
            stage_end(pe, 5)
            ln_tiles_pe(pe, "l1")
            stage_end(pe, 6)
            for at in range(0, D, P):
                nc.tensor.matmul(PS[:, 0, at:at + P], zeros[:, :], ident[:, :], start=at == 0, stop=False, skip_group_check=True)
                nc.tensor.matmul(PS[:, 1, at:at + P], zeros[:, :], ident[:, :], start=at == 0, stop=False, skip_group_check=True)
            nc.tensor.matmul(PS[:, 2, 0:KD], zeros[:, :], ident[:, 0:KD], start=True, stop=False, skip_group_check=True)
            nc.tensor.sem_inc(S("m1_mm"), 1)

            def mixer1_pe(t, q):
                if q == 3:
                    pe.wait_ge(S("m1_z"), t + 1)
                    for m in range(KD):
                        nc.tensor.matmul(PS[:, 0, m * P:(m + 1) * P], zb[:, m * P:(m + 1) * P], zb[:, m * P:(m + 1) * P],
                                         start=False, stop=False, skip_group_check=True)
                        nc.tensor.matmul(PS[:, 2, m:m + 1], zb[:, m * P:(m + 1) * P], ones[:, 0:1],
                                         start=False, stop=False, skip_group_check=True)
                    nc.tensor.matmul(PS[:, 1, 0:D], ones[:, :], zb[:, 0:D],
                                     start=False, stop=False, skip_group_check=True).then_inc(S("m1_mm"), 1)

            gather_pe_all(pe, "g1", False, mixer1_pe)
            for b in range(2):
                nc.tensor.matmul(PS[:, b, 0:P], zeros[:, :], ident[:, :], start=False, stop=True, skip_group_check=True)
            nc.tensor.matmul(PS[:, 2, 0:KD], zeros[:, :], ident[:, 0:KD], start=False, stop=True, skip_group_check=True)
            stage_end(pe, 7)
            nc.tensor.sem_inc(S("g1_dn"), U)
            pe.wait_ge(S("w_g1"), 16 * 4)
            pe.wait_ge(S("agg"), 1)
            with pe.Fori(0, NCH) as c:
                up_pe(pe, "g1", c, [[g1w1[:, k, m * P:(m + 1) * P] for k in range(KD)] for m in range(8)],
                      lambda k, at: ACC[:, k, ds(at, HALF)], c * 16, 16)
                pe.wait_ge(S("g1_upfree"), c * 16 + 16 + 4)
                for u in range(U):
                    pe.wait_ge(S("g1_dfree"), slot_free(c * U + u, u))
                    pe.wait_ge(S("g1_stg"), c * U + u + 1)
                    nc.tensor.matmul(slot(u), ones[0:1, :], g1row_[0:1, :], start=True, stop=False)
                    for m in range(KD):
                        nc.tensor.matmul(slot(u)[:, m * P:(m + 1) * P], stg1[:, u, m, :], kv[:, m, :], start=False, stop=False)
                    for k in range(8):
                        ins = nc.tensor.matmul(slot(u), g1h[:, k, u * P:(u + 1) * P], g1w2[:, k, :],
                                               start=False, stop=k == 7)
                    ins.then_inc(S("g1_dn"), 1)
            stage_end(pe, 8)
            nc.tensor.sem_inc(S("f1_gate"), U)
            pe.wait_ge(S("w_gate"), 32)

            def gate_pe(i, u, t):
                pe.wait_ge(S("f1_stg"), t + 1)
                ins = nc.tensor.matmul(PS[:, u, D:D + E1], ones[0:1, :], grow_[0:1, :], start=True, stop=False)
                for k in range(KD):
                    ins = nc.tensor.matmul(PS[:, u, D:D + E1], stg2[:, u, k, :], gate[:, k, :],
                                           start=False, stop=k == KD - 1)
                ins.then_inc(S("f1_gate"), 1)

            ln_tiles_pe(pe, "f1", after=gate_pe)
            nc.tensor.sem_inc(S("f1_b"), U)
            pe.wait_ge(S("f1_wt"), 1)
            pe.wait_ge(S("w_f1"), 64)
            with pe.Fori(0, NI) as i:
                for u in range(U):
                    pe.wait_ge(S("f1_wts"), i * U + u + 1)
                    nc.tensor.transpose(PS[0:E1, 6, 0:P], hb[:, u, 0:E1], ident[:, :]).then_inc(S("f1_wT"), 1)
                    pe.wait_ge(S("f1_wTs"), i * U + u + 1)
                    pe.wait_ge(S("f1_b0"), i * U + u + 1)
                    nc.tensor.matmul(bank(u), stg2[0:E1, u, 0, :], e_b2_[0:E1, :], start=True, stop=True)\
                        .then_inc(S("f1_b"), 1)
            pe.wait_ge(S("f1_b0"), T + U)
            nc.tensor.sem_inc(S("f1_dn"), U)
            nc.tensor.sem_inc(S("f1_wfree"), 2)
            with pe.Fori(0, E1 // 2) as i:
                for s in range(2):
                    pe.wait_ge(S(f"f1_w{s}"), i * 32 + 32)
                    pe.sem_inc(S("f1_w_seen"), 1)
                    with pe.Fori(0, NCH) as c:
                        n = (i * 2 + s) * NCH + c
                        up_pe(pe, "f1", c, [[e_w1[:, s, k, m * P:(m + 1) * P] for k in range(KD)] for m in range(4)],
                              lambda k, at: XNT[:, k, ds(at, HALF)], n * 8, 8)
                        pe.wait_ge(S("f1_upfree"), n * 8 + 8 + 4)
                        for u in range(U):
                            pe.wait_ge(S("f1_dfree"), slot_free(n * U + u, u))
                            for k in range(4):
                                ins = nc.tensor.matmul(slot(u), e_h[:, k, u * P:(u + 1) * P], e_w2[:, s, k, :],
                                                       start=k == 0, stop=k == 3)
                            ins.then_inc(S("f1_dn"), 1)
                    pe.drain().then_inc(S("f1_wfree"), 1)

        @block.vector
        def _(v):
            ch = Chain(v, S("dve"))
            fn = Asked(v, S("asked"), S("answered"))
            v.wait_ge(S("edges"), 16 * 6)
            nc.vector.tensor_copy(sf, srow).then_inc(S("tab_rows"), 1)
            ch(nc.vector.tensor_copy(df, drow))
            ch(nc.vector.tensor_reduce(out=gb2[:, 0:1], in_=df, axis=AX.X, op=ALU.min))
            ch(nc.vector.tensor_scalar(rf, df, gb2[:, 0:1], None, ALU.subtract))
            ch(nc.vector.scalar_tensor_tensor(out=mf, in0=df, scalar=BIG / 2, in1=rf, op0=ALU.is_lt, op1=ALU.mult))
            v.sem_inc(S("tab_rows"), 2)
            ch(nc.vector.tensor_reduce(out=gb2[:, 1:2], in_=mf, axis=AX.X, op=ALU.max))
            ch(nc.vector.tensor_scalar(gb2[:, 0:1], gb2[:, 0:1], float(N), None, ALU.min))
            v.sem_inc(S("tab_rows"), 1)
            v.wait_ge(S("tab_t"), 4)
            v.wait_ge(S("consts"), 13)
            for q, table in enumerate((idx[:, :, :], rel0[:, :, :], ewt[:, 0:G, :])):
                ch(nc.vector.tensor_copy(table.rearrange("p g c -> p c g"), v3(PS[:, q, :], P)[:, :, 0:G]))
            ch(nc.vector.tensor_copy(rel[:, 0:G, :], rel0[:, :, :]))
            ch(nc.vector.tensor_copy(base0[:, :], PS[0:1, 3, 0:G]))
            ch(nc.vector.tensor_copy(base[:, :], base0[:, :]))
            ch(nc.vector.tensor_reduce(out=farthest[:, :], in_=PS[0:1, 3, P:P + G], axis=AX.X, op=ALU.max))
            ch(nc.vector.tensor_scalar(rounds[:, :], farthest[:, :], 1.0 / W, 1.0 - (W - 1) / 2 / W, ALU.mult, ALU.add))
            v.wait_ge(S("x_in"), 32)
            ln_stats(v, ch, fn, X, 1e-5)
            n2, n, lo, hi, ln, fac = (sc[:, k, :] for k in range(6))
            ch(nc.vector.tensor_tensor(n2, rs[:, :], rs[:, :], ALU.mult))
            ch(nc.vector.tensor_tensor(n2, n2, mv[:, :, 1], ALU.mult))
            fn.ask(nc.vector.tensor_scalar(n2, n2, float(D), TINY, ALU.mult, ALU.max))
            ch(nc.vector.tensor_scalar(lo, n, MAXNORM, None, ALU.min))
            ch(nc.vector.tensor_scalar(hi, lo, 1.0, None, ALU.add))
            ch(nc.vector.tensor_scalar(lo, lo, -1.0, 1.0, ALU.mult, ALU.add))
            ch(nc.vector.reciprocal(lo, lo))
            fn.ask(nc.vector.tensor_tensor(hi, hi, lo, ALU.mult))
            ch(nc.vector.reciprocal(lo, n))
            ch(nc.vector.scalar_tensor_tensor(out=fac, in0=ln, scalar=0.5, in1=lo, op0=ALU.mult, op1=ALU.mult))
            ch(nc.vector.tensor_scalar(lo, n2, 1.0 / 7, 1.0 / 5, ALU.mult, ALU.add))
            ch(nc.vector.tensor_tensor(lo, lo, n2, ALU.mult))
            ch(nc.vector.tensor_scalar(lo, lo, 1.0 / 3, None, ALU.add))
            ch(nc.vector.tensor_tensor(lo, lo, n2, ALU.mult))
            ch(nc.vector.scalar_tensor_tensor(out=lo, in0=lo, scalar=1.0, in1=fac, op0=ALU.add, op1=ALU.subtract))
            ch(nc.vector.scalar_tensor_tensor(out=lo, in0=n, scalar=0.05, in1=lo, op0=ALU.is_lt, op1=ALU.mult))
            ch(nc.vector.tensor_tensor(fac, fac, lo, ALU.add))
            v.sem_inc(S("l0_nm"), 1)
            stage_end(v, 1)
            ln_tiles_dve(v, "l0", scaled=fac)
            v.wait_ge(S("gram"), 1)
            nc.vector.tensor_scalar(sc[:, 7, 0:KD], PS[:, 7, 0:KD], 1.0 / N, None, ALU.mult).then_inc(S("gram_sb"), 1)
            v.wait_ge(S("bn_cw"), 1)
            v.wait_ge(S("w_conv"), 48)
            for m in range(KD):
                ch(nc.vector.tensor_tensor(zz[:, m, :].rearrange("p (h o) -> p h o", h=2),
                                           wc[:, m, :].rearrange("p (h o) -> p h o", h=2),
                                           PS[:, 2 * m:2 * m + 2, 0:TD // 2], ALU.mult))
            v.sem_inc(S("bn_zz"), 1)
            v.wait_ge(S("bn_sums"), 1)
            ch(nc.vector.tensor_copy(bnm, PS[:, 7, 8:8 + KQ]))
            ch(nc.vector.tensor_tensor(bns, bnm, bnm, ALU.mult))
            ch(nc.vector.scalar_tensor_tensor(out=bnu, in0=PS[:, 7, 16:16 + KQ], scalar=1.0 / N, in1=bns,
                                              op0=ALU.mult, op1=ALU.subtract))
            fn.ask(nc.vector.tensor_scalar(bnu, bnu, 0.0, 1e-5, ALU.max, ALU.add))
            ch(nc.vector.reciprocal(bnu, bnu))
            ch(nc.vector.tensor_tensor(bns, bng, bnu, ALU.mult))
            ch(nc.vector.tensor_tensor(bnm, bnm, bns, ALU.mult))
            ch(nc.vector.tensor_tensor(bnt, bnb, bnm, ALU.subtract))
            v.wait_ge(S("w_mix"), 16 * 7)
            ch(nc.vector.tensor_tensor(bd, bd, dw_.rearrange("p (j a) -> p j a", a=1).to_broadcast((P, KQ, P)), ALU.mult))
            stage_end(v, 2)

            A2 = ATANH_MAX * ATANH_MAX
            cm = Chain(v, S("dve_mix"))

            def mixer_dve(t, q):
                if q == 0:
                    cm.enter(t, 12)
                elif q == 2:
                    v.wait_ge(S("mix_sums"), t + 1)
                    f2, g2, ep = ff[:, 0, :], ff[:, 1, :], ff[:, 2, :]
                    cm(nc.vector.tensor_scalar(f2, PS[:, 7, 0:P], TINY, None, ALU.max))
                    cm(nc.vector.reciprocal(f2, f2))
                    cm(nc.vector.tensor_scalar(f2, f2, A2, 1.0, ALU.mult, ALU.min))
                    cm(nc.vector.tensor_copy(g2, PS[:, 7, P:2 * P]))
                    cm(nc.vector.tensor_tensor(g2, g2, PS[:, 7, 0:P], ALU.add))
                    cm(nc.vector.tensor_tensor(g2, g2, f2, ALU.mult))
                    cm(nc.vector.tensor_scalar(g2, g2, TINY, None, ALU.max))
                    cm(nc.vector.reciprocal(g2, g2))
                    cm(nc.vector.tensor_scalar(g2, g2, A2, 1.0, ALU.mult, ALU.min))
                    cm(nc.vector.tensor_tensor(f2, f2, g2, ALU.mult))
                    nc.vector.reciprocal(g2, f2).then_inc(S("mix_f"), 1)
                    v.wait_ge(S("mix_eps"), t + 1)
                    v.wait_ge(S("mix_qv"), t + 1)
                    vv4 = hh[:, 6:10, :]
                    cm(nc.vector.tensor_tensor(rr, vv4, ff[:, 2:3, :].to_broadcast((P, 4, P)), ALU.add))
                    cm(nc.vector.reciprocal(rr, rr))
                    nc.vector.tensor_tensor(rr, rr, vv4, ALU.mult).then_inc(S("mix_r"), 1)
                    v.wait_ge(S("mix_r"), t * 3 + 1)
                    nc.vector.tensor_tensor(rr, rr, PS[:, 4, :].rearrange("p (j n) -> p j n", n=P), ALU.mult)\
                        .then_inc(S("mix_r"), 1)
                    v.wait_ge(S("mix_r"), t * 3 + 2)
                    nc.vector.tensor_tensor(rr, rr, ff[:, 0:1, :].to_broadcast((P, 4, P)), ALU.mult)\
                        .then_inc(S("mix_r"), 1)
                    v.wait_ge(S("mix_r"), t * 3 + 3)
                    nc.vector.tensor_tensor(oo[:, 0:2, :], rr[:, 0:2, :], hh[:, 2:4, :], ALU.mult)
                    nc.vector.tensor_tensor(oo[:, 2:4, :], rr[:, 2:4, :], hh[:, 0:2, :], ALU.mult)\
                        .then_inc(S("mix_o"), 1)
                elif q == 3:
                    v.wait_ge(S("mix_ft"), t + 1)
                    nc.vector.tensor_copy(tile_of(MB, t), PS[:, 7, D:2 * D])
                    nc.vector.tensor_copy(col(sc[:, 0, :], t), PS[:, 1, D:D + 1]).then_inc(S("mix_read"), 1)

            nc.vector.sem_inc(S("mix_o"), 1)
            nc.vector.sem_inc(S("mix_read"), 1)
            gather_dve_all(v, "g0", True, mixer_dve)
            cm.base = None
            stage_end(v, 3)
            a, b, c4, th, f = (sc[:, k, :] for k in range(5))
            fn.ask(nc.vector.tensor_scalar(a, a, TINY, None, ALU.max))
            ch(nc.vector.reciprocal(a, a))
            ch(nc.vector.tensor_scalar(a, a, ATANH_MAX, 1.0, ALU.mult, ALU.min))
            with v.Fori(0, NI) as i:
                for u in range(U):
                    t = i * U + u
                    nc.vector.scalar_tensor_tensor(out=tile_of(MB, t), in0=tile_of(MB, t), scalar=col(a, t), in1=bres_,
                                                   op0=ALU.mult, op1=ALU.add).then_inc(S("m0_ft"), 1)
            v.wait_ge(S("m0_sq"), T)
            fn.ask(nc.vector.tensor_scalar(b, b, TINY, None, ALU.max))
            ch(nc.vector.reciprocal(f, c4))
            ch(nc.vector.scalar_tensor_tensor(out=f, in0=th, scalar=MAXNORM, in1=f, op0=ALU.min, op1=ALU.mult))
            with v.Fori(0, NI) as i:
                for u in range(U):
                    t = i * U + u
                    ins = nc.vector.scalar_tensor_tensor(out=tile_of(X, t), in0=tile_of(MB, t), scalar=col(f, t),
                                                         in1=tile_of(X, t), op0=ALU.mult, op1=ALU.add)
                ch.enter(i, 1)
                ch(ins)
            ch.leave(NI)
            v.sem_inc(S("m0_done"), 1)
            v.wait_ge(S("w_g0"), 64)
            nc.vector.tensor_tensor(brow_[0:1, 2 * D:3 * D], brow_[0:1, 0:D], brow_[0:1, D:2 * D], ALU.add)\
                .then_inc(S("n0_brow"), 1)
            nc.vector.sem_inc(S("n0_ps"), U)
            with v.Fori(0, NI) as i:
                for u in range(U):
                    t = i * U + u
                    v.wait_ge(S("n0_mm"), t + 1)
                    nc.vector.scalar_tensor_tensor(out=ust[:, u, :, :], in0=XNT[:, :, ds(t * P, P)], scalar=1.0,
                                                   in1=ACC[:, 0:KD, ds(t * P, P)], op0=ALU.add, op1=ALU.mult)\
                        .then_inc(S("n0_u"), 1)
                for u in range(U):
                    t = i * U + u
                    v.wait_ge(S("n0_mm"), t + 1 + U)
                    nc.vector.tensor_copy(tile_of(MB, t), bank(u)).then_inc(S("n0_ps"), 1)
                    v.wait_ge(S("n0_ps"), t + 1 + U)
                    nc.vector.scalar_tensor_tensor(out=tile_of(MB, t), in0=tile_of(MB, t), scalar=0.2,
                                                   in1=tile_of(MB, t), op0=ALU.mult, op1=ALU.max).then_inc(S("n0_y"), 1)
            v.wait_ge(S("n0_ss"), T)
            fn.ask(nc.vector.tensor_scalar(b, b, 1e-24, None, ALU.max))
            ch(nc.vector.reciprocal(b, b))
            with v.Fori(0, NI) as i:
                for u in range(U):
                    t = i * U + u
                    ins = nc.vector.scalar_tensor_tensor(out=tile_of(X, t), in0=tile_of(MB, t), scalar=col(b, t),
                                                         in1=tile_of(X, t), op0=ALU.mult, op1=ALU.add)
                ch.enter(i, 1)
                ch(ins)
            ch.leave(NI)
            stage_end(v, 4)
            ln_stats(v, ch, fn, X, 1e-5)
            v.sem_inc(S("f0_nm"), 1)
            ln_tiles_dve(v, "f0")
            v.wait_ge(S("f0_free"), T + U)
            ch(nc.vector.tensor_reduce(out=ysum, in_=XNT[:, :, 0:N], axis=AX.X, op=ALU.add))
            nc.vector.tensor_scalar(ysum, ysum, 1.0 / N, None, ALU.mult).then_inc(S("f0_ysum"), 1)
            v.wait_ge(S("route_mm"), 1)
            v.wait_ge(S("w_router"), 32)
            R = lambda k, n=E0: r0[0:1, k, 0:n]
            ch(nc.vector.tensor_tensor(R(3), R(0), PS[0:1, 5, 0:E0], ALU.add))
            for k in range(2):
                ch(nc.vector.tensor_reduce(out=R(5, 1), in_=R(3), axis=AX.X, op=ALU.max))
                fn.ask(nc.vector.tensor_scalar(R(1), R(3), R(5, 1), None, ALU.subtract))
                ch(nc.vector.tensor_reduce(out=R(5, 1), in_=R(2), axis=AX.X, op=ALU.add))
                ch(nc.vector.reciprocal(R(5, 1), R(5, 1)))
                ch(nc.vector.tensor_scalar(R(4), R(2), R(5, 1), None, ALU.mult))
                if k == 0:
                    ch(nc.vector.tensor_scalar(R(6), R(4), float(N), TINY, ALU.mult, ALU.max))
                    ch(nc.vector.reciprocal(R(6), R(6)))
                    ch(nc.vector.tensor_scalar(R(6), R(6), CAPACITY, 1.0, ALU.mult, ALU.min))
                    ch(nc.vector.tensor_tensor(R(3), R(4), R(6), ALU.mult))
            ch(nc.vector.max(out=R(7), in_=R(4)))
            ch(nc.vector.max_index(out=R(9).bitcast(U32), in_max=R(7), in_values=R(4)))
            fn.ask(nc.vector.tensor_tensor(R(1, 1), r0[0:1, 7, 1:2], r0[0:1, 7, 0:1], ALU.subtract))
            ch(nc.vector.tensor_scalar(R(6, 1), R(2, 1), 1.0, None, ALU.add))
            ch(nc.vector.reciprocal(r0[0:1, 8, 0:1], R(6, 1)))
            ch(nc.vector.tensor_tensor(r0[0:1, 8, 1:2], r0[0:1, 8, 0:1], R(2, 1), ALU.mult))
            v.sem_inc(S("routed"), 1)
            v.wait_ge(S("route_mm"), 2)
            ch(nc.vector.tensor_copy(wexp, PS[:, 3, 0:TOPK]))
            v.wait_ge(S("w_f0"), 16 * 8)
            for e in range(TOPK):
                ch(nc.vector.tensor_scalar(f0w2[:, e, :, :], f0w2[:, e, :, :], wexp[:, e:e + 1], None, ALU.mult))
            ch(nc.vector.tensor_scalar(f0row_[0:1, 2 * D:3 * D], f0row_[0:1, 0:D], wexp[0:1, 0:1], None, ALU.mult))
            ch(nc.vector.scalar_tensor_tensor(out=f0row_[0:1, 2 * D:3 * D], in0=f0row_[0:1, D:2 * D],
                                              scalar=wexp[0:1, 1:2], in1=f0row_[0:1, 2 * D:3 * D],
                                              op0=ALU.mult, op1=ALU.add))
            v.sem_inc(S("f0_w2s"), 1)
            nc.vector.sem_inc(S("f0_dfree"), U)
            with v.Fori(0, NCH) as c:
                for u in range(U):
                    t = c * U + u
                    v.wait_ge(S("f0_dn"), t + 1 + U)
                    nc.vector.tensor_tensor(tile_of(MB, t), tile_of(MB, t), slot(u), ALU.add)\
                        .then_inc(S("f0_dfree"), 1)
            v.wait_ge(S("f0_dfree"), T + U)
            ln_stats(v, ch, fn, MB, 1e-5)
            v.sem_inc(S("f0z_nm"), 1)
            v.wait_ge(S("w_f0n"), 32)
            epilogue_dve(v, ch, "f0z", gb0)
            stage_end(v, 5)
            nc.vector.tensor_scalar(rel[:, 0:G, :], rel0[:, :, :], 0.0, None, ALU.add)
            nc.vector.tensor_copy(base[:, :], base0[:, :])
            deg = ACC[:, KD, 0:NP]
            pos = mflat[:, 0:NP]
            ch(nc.vector.tensor_scalar(pos, deg, 0.0, None, ALU.is_gt))
            fn.ask(nc.vector.tensor_scalar(deg, deg, 1e-12, None, ALU.max))
            ch(nc.vector.reciprocal(deg, deg))
            ch(nc.vector.tensor_tensor(deg, deg, pos, ALU.mult))
            diag = v3(pos, P)
            ch(nc.vector.tensor_tensor(diag, v3(deg, P), ident[:, :].rearrange("p (a n) -> p a n", a=1)
                                       .to_broadcast((P, T, P)), ALU.mult))
            ch(nc.vector.tensor_reduce(out=dinvc[:, :], in_=diag, axis=AX.X, op=ALU.add))
            ln_stats(v, ch, fn, X, 1e-5)
            ch(nc.vector.tensor_tensor(sc[:, 0, :], rs[:, :], dinvc[:, :], ALU.mult))
            ch(nc.vector.tensor_tensor(sc[:, 1, :], nm[:, :], dinvc[:, :], ALU.mult))
            v.sem_inc(S("l1_tab"), 1)
            ln_tiles_dve(v, "l1")
            stage_end(v, 6)

            c1 = Chain(v, S("dve_mix1"))

            def mixer1_dve(t, q):
                z8 = v3(zb, HC)
                if q == 0:
                    c1.enter(t, 3)
                    v.wait_ge(S("m1_mm"), t + 1)
                    c1(nc.vector.tensor_scalar(zb, tile_of(X, t), col(rs, t), col(nm, t), ALU.mult, ALU.add))
                    c1(nc.vector.tensor_reduce(out=hst[:, 0, :], in_=z8, axis=AX.X, op=ALU.add))
                    c1(nc.vector.tensor_scalar(hst[:, 0, :], hst[:, 0, :], 1.0 / HC, None, ALU.mult))
                    mean = hst[:, 0, :].rearrange("p (h a) -> p h a", a=1).to_broadcast((P, HEADS, HC))
                    nc.vector.tensor_tensor(z8, z8, mean, ALU.subtract).then_inc(S("m1_c"), 1)
                elif q == 1:
                    v.wait_ge(S("m1_sq"), t + 1)
                    nc.vector.tensor_reduce(out=hst[:, 1, :], in_=v3(csq, HC), axis=AX.X, op=ALU.add)\
                        .then_inc(S("m1_ss"), 1)
                elif q == 2:
                    v.wait_ge(S("m1_std"), t + 1)
                    nc.vector.tensor_scalar(hst[:, 2, :], hst[:, 2, :], 1e-5, None, ALU.add).then_inc(S("m1_r"), 1)
                    v.wait_ge(S("m1_r"), t * 3 + 1)
                    nc.vector.reciprocal(hst[:, 3, :], hst[:, 2, :]).then_inc(S("m1_r"), 1)
                    v.wait_ge(S("m1_r"), t * 3 + 2)
                    nc.vector.tensor_scalar(hst[:, 3, :], hst[:, 3, :], col(valid, t), None, ALU.mult)\
                        .then_inc(S("m1_r"), 1)
                    v.wait_ge(S("m1_r"), t * 3 + 3)
                    inv = hst[:, 3, :].rearrange("p (h a) -> p h a", a=1).to_broadcast((P, HEADS, HC))
                    nc.vector.tensor_tensor(z8, z8, inv, ALU.mult).then_inc(S("m1_z"), 1)

            gather_dve_all(v, "g1", False, mixer1_dve)
            stage_end(v, 7)
            v.wait_ge(S("w_m1"), 64)
            for m in range(KD):
                zcol = sc[:, 2, m:m + 1]
                ch(nc.vector.tensor_copy(zcol, PS[:, 2, m:m + 1]))
                ch(nc.vector.tensor_tensor(kt1[:, m, :], vwb[:, m, :], PS[:, 0, m * P:(m + 1) * P], ALU.mult))
                ch(nc.vector.scalar_tensor_tensor(out=kt1[:, m, :], in0=vbb[:, m, :], scalar=zcol, in1=kt1[:, m, :],
                                                  op0=ALU.mult, op1=ALU.add))
                ch(nc.vector.tensor_scalar(kt1[:, m, :], kt1[:, m, :], kwc_[:, m:m + 1], None, ALU.mult))
                ch(nc.vector.tensor_tensor(kt2[:, m, :], vwb[:, m, :], PS[:, 1, m * P:(m + 1) * P], ALU.mult))
                ch(nc.vector.scalar_tensor_tensor(out=kt2[:, m, :], in0=vbb[:, m, :], scalar=float(N), in1=kt2[:, m, :],
                                                  op0=ALU.mult, op1=ALU.add))
                ch(nc.vector.scalar_tensor_tensor(out=kv[:, m, :], in0=kt2[:, m, :], scalar=kwc_[:, 2 + m:3 + m],
                                                  in1=kt1[:, m, :], op0=ALU.mult, op1=ALU.add))
                ch(nc.vector.scalar_tensor_tensor(out=kv[:, m, :], in0=kv[:, m, :], scalar=1.0 / N, in1=blockones[:, :],
                                                  op0=ALU.mult, op1=ALU.mult))
                ch(nc.vector.tensor_tensor(kv[:, m, :], kv[:, m, :], ident[:, :], ALU.add))
            for k in range(KD):
                ch(nc.vector.tensor_tensor(ACC[:, k, 0:NP], ACC[:, k, 0:NP], deg, ALU.mult))
            v.sem_inc(S("agg"), 1)
            nc.vector.sem_inc(S("g1_dfree"), U)
            with v.Fori(0, NCH) as c:
                for u in range(U):
                    t = c * U + u
                    v.wait_ge(S("g1_dn"), t + 1)
                    nc.vector.tensor_copy(stg1[:, u, :, :], XNT[:, :, ds(t * P, P)]).then_inc(S("g1_stg"), 1)
                for u in range(U):
                    t = c * U + u
                    v.wait_ge(S("g1_dn"), t + 1 + U)
                    nc.vector.tensor_tensor(tile_of(X, t), tile_of(X, t), slot(u), ALU.add)\
                        .then_inc(S("g1_dfree"), 1)
            stage_end(v, 8)
            ln_stats(v, ch, fn, X, 1e-5)
            v.sem_inc(S("f1_nm"), 1)

            def gate_dve(i, u, t):
                v.wait_ge(S("f1_free"), t + 1 + U)
                v.wait_ge(S("f1_gate"), t + 1)
                nc.vector.tensor_copy(stg2[:, u, :, :], XNT[:, :, ds(t * P, P)]).then_inc(S("f1_stg"), 1)
                v.wait_ge(S("f1_gate"), t + 1 + U)
                nc.vector.tensor_copy(tile_of(lg, t), PS[:, u, D:D + E1]).then_inc(S("f1_lg"), 1)

            ln_tiles_dve(v, "f1", extra=gate_dve)
            v.wait_ge(S("f1_lg"), T)
            for t in range(T):
                ins = nc.vector.max(out=top[:, t, :], in_=lg[:, t, :])
            ch(ins)
            for t in range(T):
                ins = nc.vector.max_index(out=topi[:, t, :], in_max=top[:, t, :], in_values=lg[:, t, :])
            ch(ins)
            p1, p2, i1, i2 = (sc[:, k, :] for k in (2, 3, 4, 5))
            fn.ask(nc.vector.tensor_tensor(sc[:, 0, :], top[:, :, 1], top[:, :, 0], ALU.subtract))
            ch(nc.vector.tensor_scalar(p1, sc[:, 1, :], 1.0, None, ALU.add))
            ch(nc.vector.reciprocal(p1, p1))
            ch(nc.vector.tensor_tensor(p2, p1, sc[:, 1, :], ALU.mult))
            ch(nc.vector.tensor_copy(i1, topi[:, :, 0]))
            ch(nc.vector.tensor_copy(i2, topi[:, :, 1]))

            def over_experts(ap):
                return ap.rearrange("p (t a) -> p t a", a=1).to_broadcast((P, T, E1))

            io = iota[:, 0:E1].rearrange("p (a e) -> p a e", a=1).to_broadcast((P, T, E1))
            ch(nc.vector.tensor_tensor(wt, io, over_experts(i1), ALU.is_equal))
            ch(nc.vector.tensor_tensor(wt, wt, over_experts(p1), ALU.mult))
            ch(nc.vector.tensor_tensor(lg, io, over_experts(i2), ALU.is_equal))
            ch(nc.vector.tensor_tensor(lg, lg, over_experts(p2), ALU.mult))
            ch(nc.vector.tensor_tensor(wt, wt, lg, ALU.add))
            v.sem_inc(S("f1_wt"), 1)
            nc.vector.sem_inc(S("f1_b0"), U)
            with v.Fori(0, NI) as i:
                for u in range(U):
                    t = i * U + u
                    v.wait_ge(S("f1_b"), t + 1)
                    nc.vector.tensor_copy(hb[:, u, 0:E1], tile_of(wt, t)).then_inc(S("f1_wts"), 1)
                    v.wait_ge(S("f1_wT"), t + 1)
                    nc.vector.tensor_copy(stg2[0:E1, u, 0, :], PS[0:E1, 6, 0:P]).then_inc(S("f1_wTs"), 1)
                for u in range(U):
                    t = i * U + u
                    v.wait_ge(S("f1_b"), t + 1 + U)
                    nc.vector.tensor_tensor(tile_of(MB, t), tile_of(MB, t), bank(u), ALU.add).then_inc(S("f1_b0"), 1)
            v.wait_ge(S("f1_b0"), T + U)
            nc.vector.sem_inc(S("f1_dfree"), U)
            with v.Fori(0, E1 // 2) as i:
                for s in range(2):
                    with v.Fori(0, NCH) as c:
                        for u in range(U):
                            t = c * U + u
                            n = (i * 2 + s) * T + t
                            v.wait_ge(S("f1_dn"), n + 1 + U)
                            nc.vector.scalar_tensor_tensor(
                                out=tile_of(MB, t), in0=slot(u),
                                scalar=wt[:, ds(t, 1), ds(i * 2 + s, 1)].rearrange("p a b -> p (a b)"),
                                in1=tile_of(MB, t), op0=ALU.mult, op1=ALU.add).then_inc(S("f1_dfree"), 1)
            v.wait_ge(S("f1_dfree"), E1 * T + U)
            ln_stats(v, ch, fn, MB, 1e-5)
            v.sem_inc(S("f1z_nm"), 1)
            v.wait_ge(S("w_f1"), 64)
            epilogue_dve(v, ch, "f1z", gb1)


def kernel(**inputs):
    import concourse.bacc as bacc
    from concourse.bass_utils import run_bass_kernel_spmd

    a = {k: np.asarray(v) for k, v in inputs.items()}
    channels = np.arange(TD).reshape(HEADS, 3, HC).transpose(1, 0, 2).reshape(-1)
    pointwise = a["L0_mix_w_pw"][channels, :, 0].reshape(TD // HC, HC, HC).transpose(0, 2, 1).reshape(TD, HC)

    def by_partition(v):
        return np.swapaxes(v.reshape(*v.shape[:-1], -1, P), -1, -2)

    laid = {
        "x": a["x"], "src": a["src"], "dst": a["dst"], "edge_weight": a["edge_weight"],
        "g0_w1": a["L0_gnn_W1"].T, "g0_b1": a["L0_gnn_b1"], "g0_w2": a["L0_gnn_W2"].T, "g0_b2": a["L0_gnn_b2"],
        "wc": a["L0_mix_w_qkv"][channels, :, 2].T,
        "bn_gamma": by_partition(a["L0_mix_bn_gamma"][channels]), "bn_beta": by_partition(a["L0_mix_bn_beta"][channels]),
        "w_dw": by_partition(a["L0_mix_w_dw"][channels, 0, 2]), "w_pw": pointwise,
        "w_res": a["L0_mix_w_res"][:, :, 0].T, "b_res": a["L0_mix_b_res"],
        "f0_wr": a["L0_ffn_Wr"], "f0_br": a["L0_ffn_br"], "f0_w1": a["L0_ffn_W1"], "f0_b1": by_partition(a["L0_ffn_b1"]),
        "f0_w2": a["L0_ffn_W2"], "f0_b2": a["L0_ffn_b2"], "f0_gamma": a["L0_ffn_gamma"], "f0_beta": a["L0_ffn_beta"],
        "g1_w1": a["L1_gnn_W1"], "g1_b1": by_partition(a["L1_gnn_b1"]), "g1_w2": a["L1_gnn_W2"], "g1_b2": a["L1_gnn_b2"],
        "m1_kw": by_partition(a["L1_mix_kln_weight"].reshape(-1)), "m1_kb": by_partition(a["L1_mix_kln_bias"].reshape(-1)),
        "m1_vw": a["L1_mix_vln_weight"].reshape(-1), "m1_vb": a["L1_mix_vln_bias"].reshape(-1),
        "f1_wg": a["L1_ffn_gate_w"], "f1_bg": a["L1_ffn_gate_b"], "f1_w1": a["L1_ffn_w1"], "f1_b1": by_partition(a["L1_ffn_b1"].reshape(-1)),
        "f1_w2": a["L1_ffn_w2"], "f1_b2": a["L1_ffn_b2"], "f1_gamma": a["L1_ffn_gamma"], "f1_beta": a["L1_ffn_beta"],
    }
    laid = {k: np.ascontiguousarray(v) for k, v in laid.items()}
    nc = bacc.Bacc("TRN2", target_bir_lowering=False, num_devices=1)
    dram = {k: nc.dram_tensor(f"in_{k}", v.shape, mybir.dt.from_np(v.dtype), kind="ExternalInput").ap()
            for k, v in laid.items()}
    out = nc.dram_tensor("out_x", (N, D), F32, kind="ExternalOutput").ap()
    bass_gps_kernel(nc, dram, out)
    got = run_bass_kernel_spmd(nc, [{f"in_{k}": v for k, v in laid.items()}], core_ids=[0])
    return got.results[0]["out_x"]
```

```python
import math
from contextlib import ExitStack

import numpy as np
import concourse.bass as bass
from concourse import mybir

F32 = mybir.dt.float32
I32 = mybir.dt.int32
U32 = mybir.dt.uint32
BF16 = mybir.dt.bfloat16
ALU = mybir.AluOpType
ACT = mybir.ActivationFunctionType
AX = mybir.AxisListType
ds = bass.ds

P = 128
N = 3125
D = 256
KD = D // P
E = 50000
U = 5
T = -(-N // P)
NP = T * P
NI = T // U
TAIL = N - (T - 1) * P
assert T % U == 0

C = 4
GE = C * P
B = 4
G = -(-E // (GE * B)) * B
GB = G // B
W = 96
MAXR = -(-N // W)
NA = NP + P
BIG = 16384.0

CH = U * P
HALF = CH // 2
NCH = NP // CH
TD = 3 * D
KQ = TD // P
HID1 = 1024
F0, E0 = 512, 8
F1, E1 = 512, 16
TOPK = 2
TILES1 = (TOPK * N + E1 * (P - 1)) // P
PAIRS = -(-TILES1 // 2)
SLOTS = 2 * PAIRS * P
HC = 32
HEADS = D // HC
CAPACITY = float(math.ceil(N * 1.25 / E0))

NORMS = ("l0", "f0", "f0z", "l1", "f1", "f1z")

MAXNORM = float(np.float32(1.0 - 1e-5))
ATANH_MAX = math.atanh(MAXNORM)
TINY = 1e-30


class Asked:

    def __init__(self, engine, asked, answered):
        self.engine, self.asked, self.answered, self.n = engine, asked, answered, 0

    def ask(self, instruction):
        self.n += 1
        instruction.then_inc(self.asked, 1)
        self.engine.wait_ge(self.answered, self.n)

    def take(self):
        self.n += 1
        self.engine.wait_ge(self.asked, self.n)

    def give(self, instruction):
        instruction.then_inc(self.answered, 1)


class Chain:

    def __init__(self, engine, semaphore):
        self.engine, self.semaphore = engine, semaphore
        self.before, self.n, self.base = 0, 0, None

    def __call__(self, instruction):
        instruction.then_inc(self.semaphore, 1)
        self.n += 1
        at = self.before + self.n
        self.engine.wait_ge(self.semaphore, at if self.base is None else self.base + at)

    def enter(self, i, per):
        self.before, self.n, self.per, self.base = self.before + self.n, 0, per, i * per

    def leave(self, times):
        assert self.n == self.per, (self.n, self.per)
        self.before, self.n, self.base = self.before + self.per * times, 0, None


def bass_gps_kernel(nc, A, out):
    with ExitStack() as ctx:
        def sb(name, shape, dt=F32):
            return ctx.enter_context(nc.sbuf_tensor(name, shape, dt))

        semaphores = {}

        def S(name):
            if name not in semaphores:
                semaphores[name] = ctx.enter_context(nc.semaphore(name))
            return semaphores[name]

        X = sb("X", [P, T, D])
        big = sb("big", [P, KD * NP + (KD + 1) * NA])
        XNT = big[:, 0:KD * NP].rearrange("p (k n) -> p k n", k=KD)
        ACC = big[:, KD * NP:KD * NP + (KD + 1) * NA].rearrange("p (k n) -> p k n", k=KD + 1)
        MB = sb("MB", [P, T, D])
        ident = sb("ident", [P, P])
        iota = sb("iota", [P, W])
        ones = sb("ones", [P, P])
        zeros = sb("zeros", [P, P])
        ones16 = sb("ones16", [P, P], BF16)
        blockones = sb("blockones", [P, P])
        before = sb("before", [P, P])
        pcol = sb("pcol", [P, 2])
        tables = sb("tables", [P, 4, (G + 1) * C])

        def table(k):
            return tables[:, k, :].rearrange("p (g c) -> p g c", c=C)

        idx = table(0).bitcast(I32)
        rel0 = table(1)[:, 0:G, :]
        rel = table(2)
        ewt = table(3)
        base0 = sb("base0", [1, G], I32)
        base = sb("base", [1, G], I32)
        rounds = sb("rounds", [1, 1], I32)
        farthest = sb("farthest", [1, 1])
        idxs = sb("idxs", [P, U, C], I32)
        st = sb("st", [P, T, 6])
        mv = sb("mv", [P, T, 2])
        rs = sb("rs", [P, T])
        nm = sb("nm", [P, T])
        sc = sb("sc", [P, 8, T])
        valid = sb("valid", [P, T])
        dinvc = sb("dinvc", [P, T])
        NWORK = 20640
        work = sb("work", [P, NWORK])
        PS = ctx.enter_context(nc.psum_tensor("PS", [P, 8, 512], F32))
        xn_dram = nc.dram_tensor("xn_table", (NP, D), F32).ap()
        xe_dram = nc.dram_tensor("expert_rows", (SLOTS + TOPK * P, D), F32).ap()
        xs_dram = nc.dram_tensor("xs_table", (NP, D), F32).ap()

        def areas(*sizes, start=0):
            at, found = start, []
            for n in sizes:
                found.append(work[:, at:at + n])
                at += n
            assert at <= NWORK, at
            return found

        def v3(ap, b):
            return ap.rearrange("p (a b) -> p a b", b=b)

        gflat, oh_, oh16_ = areas(B * C * D, 2 * C * W, C * W)
        gath = gflat.rearrange("p (s c d) -> p s c d", s=B, c=C)
        oh = oh_.rearrange("p (s c w) -> p s c w", s=2, c=C)
        oh16 = oh16_.bitcast(BF16).rearrange("p (s c w) -> p s c w", s=2, c=C)
        GATHER = B * C * D + 3 * C * W
        xb = v3(gflat[:, 0:U * D], D)
        hb = v3(gflat[:, U * D:2 * U * D], D)
        mflat = MB[:, :, :].rearrange("p t d -> p (t d)")

        srow = mflat[0:G, 0:GE].bitcast(I32)
        drow = mflat[0:G, GE:2 * GE].bitcast(I32)
        wrow = mflat[0:G, 2 * GE:3 * GE]
        sf, df, rf, mf = (mflat[0:G, k * GE:(k + 1) * GE] for k in range(3, 7))
        gb2 = mflat[0:G, 7 * GE:7 * GE + 4]

        H0T_, wc_, bd_, wres_, hh_, ks_, hsq_, ssq_, osq_, oo_, ff_, dw_, bn_, bres_ = areas(
            KD * (NP + P), KD * TD, KQ * P, 4 * D, 10 * P, 2 * P, KQ * P, KQ * P, 4 * P, 4 * P, 3 * P, KQ, 6 * KQ, D, start=GATHER)
        H0T, wc, bd, wres = v3(H0T_, NP + P), v3(wc_, TD), v3(bd_, P), v3(wres_, D)
        hh = v3(hh_, P)
        ks, hsq, ssq, osq, oo, ff, bn = (
            v3(ks_, P), v3(hsq_, P), v3(ssq_, P), v3(osq_, P), v3(oo_, P), v3(ff_, P), v3(bn_, KQ))
        rr = v3(ssq_[:, 0:4 * P], P)
        bng, bnb, bns, bnt, bnu, bnm = (bn[:, i, :] for i in range(6))
        gram = v3(hh_[:, 0:KD * D], D)
        zz, = areas(KD * TD, start=GATHER + KD * (NP + P) + KD * TD + KQ * P + 4 * D + 10 * P)
        zz = v3(zz, TD)
        msum = dw_[:, 0:0]
        w1t_, w2t_, stg_, ust_, brow_ = areas(KD * D, KD * D, U * D, U * D, 3 * D, start=GATHER)
        w1t, w2t = v3(w1t_, D), v3(w2t_, D)
        stg = stg_.rearrange("p (u k n) -> p u k n", u=U, k=KD)
        ust = ust_.rearrange("p (u k n) -> p u k n", u=U, k=KD)
        f0w1_, f0w2_, f0h_, f0b1_, f0row_, gb0_, f0r_ = areas(
            TOPK * KD * F0, TOPK * 4 * D, TOPK * 4 * CH, TOPK * 4, 3 * D, 2 * D, 200, start=GATHER)
        f0w1 = f0w1_.rearrange("p (e k f) -> p e k f", e=TOPK, k=KD)
        f0w2 = f0w2_.rearrange("p (e k f) -> p e k f", e=TOPK, k=4)
        f0h = f0h_.rearrange("p (e k f) -> p e k f", e=TOPK, k=4)
        gb0 = v3(gb0_, D)
        wr = v3(f0r_[:, 0:KD * E0], E0)
        r0 = v3(f0r_[:, KD * E0:KD * E0 + 10 * E0], E0)
        ysum = f0r_[:, 120:122]
        wexp = f0r_[:, 122:124]
        g1w1_, g1w2_, g1h_, g1b1_, g1row_, kvp_, vwb_, kwc_, z_, = areas(
            KD * HID1, 8 * D, 8 * CH, 8, D, 4 * D, 2 * D, 8, 4 * D, start=GATHER)
        g1w1, g1w2, g1h = v3(g1w1_, HID1), v3(g1w2_, D), v3(g1h_, CH)
        zb, csq = z_[:, 0:D], z_[:, D:2 * D]
        hst = v3(z_[:, 2 * D:2 * D + 4 * HEADS], HEADS)
        kv = v3(kvp_[:, 0:D], P)
        kt1, kt2 = v3(kvp_[:, D:2 * D], P), v3(kvp_[:, 2 * D:3 * D], P)
        vwb, vbb = v3(vwb_[:, 0:D], P), v3(vwb_[:, D:2 * D], P)
        stg1 = gflat[:, 0:U * D].rearrange("p (u k n) -> p u k n", u=U, k=KD)
        stg2 = gflat[:, 2 * U * D:3 * U * D].rearrange("p (u k n) -> p u k n", u=U, k=KD)
        e_w1 = big[:, 0:E1 * KD * F1].rearrange("p (e k f) -> p e k f", e=E1, k=KD)
        e_w2_, = areas(E1 * 4 * D)
        e_w2 = e_w2_.rearrange("p (e k f) -> p e k f", e=E1, k=4)
        FREE1 = E1 * 4 * D
        WAIT = -(-(GATHER + (KD + 1) * E1) // (4 * D))
        gate_, grow_ = areas(KD * E1, E1, start=GATHER)
        gate = v3(gate_, E1)
        lg_, o1_, o2_, cnt_, rk_, top_, topi_ = areas(*[T * E1] * 5, T * 8, T * 8, start=FREE1)
        lg, o1, o2, cnt, rk = (v3(a, E1) for a in (lg_, o1_, o2_, cnt_, rk_))
        top, topi = v3(top_, 8), v3(topi_, 8).bitcast(U32)
        sct_, = areas(U * D, start=FREE1 + 2048)
        sct = v3(sct_, D)
        NTILE = 2 * PAIRS
        xs_, w1s_, ht_, b3_, sel_, eji_, slots_, b1s_, b1t_ = areas(
            2 * D, 2 * KD * F1, 2 * 4 * P, D // 2, P, NTILE + 2, 2 * T, 8, 4 * E1, start=FREE1)
        tflat = tables[:, :, :].rearrange("p a b -> p (a b)")
        b2f, b2g = tflat[:, 0:D], tflat[:, D:2 * D]
        ej_ = tflat[:, 2 * D:2 * D + NTILE + 2]
        xt_, ys_ = tflat[:, 0:2 * D], tflat[:, 2 * D + NTILE + 2:4 * D + NTILE + 2]
        xs, xt, ys = v3(xs_, D), xt_.rearrange("p (s k n) -> p s k n", s=2, k=KD), v3(ys_, D)
        w1s, ht = w1s_.rearrange("p (s k f) -> p s k f", s=2, k=KD), ht_.rearrange("p (s m n) -> p s m n", s=2, m=4)
        b1s, b1t = v3(b1s_, 4), v3(b1t_, 4)
        b3 = b3_.bitcast(BF16)
        sel = v3(sel_.bitcast(BF16), P)
        eji = eji_.bitcast(I32)
        slots = v3(slots_.bitcast(I32), T)
        wide = v3(w1s_[:, 0:(NTILE + 2) * E1], E1)
        nt_, ts_, te_ = (st[:, :, :].rearrange("p a b -> p (a b)")[:, k * E1:(k + 1) * E1] for k in range(3))
        cmb_, gb1_ = areas(U * TOPK * D, 2 * D)
        cmb = cmb_.rearrange("p (u k d) -> p u k d", u=U, k=TOPK)
        gb1 = v3(gb1_, D)

        block = ctx.enter_context(nc.Block())

        def stage_end(eng, k):
            eng.drain().then_inc(S("stages"), 1)
            eng.wait_ge(S("stages"), 5 * k)

        def col(ap, t):
            return ap[:, ds(t, 1)]

        def tile_of(ap, t):
            return ap[:, ds(t, 1), :].rearrange("p a b -> p (a b)")

        def row(ap):
            return ap.rearrange("(a n) -> a n", a=1)

        full_groups, last_group = E // GE, E % GE

        def ln_stats(v, ch, root, src, eps):
            with v.Fori(0, NI) as i:
                for u in range(U):
                    ins = nc.vector.bn_stats(tile_of(st, i * U + u), tile_of(src, i * U + u))
                ch.enter(i, 1)
                ch(ins)
            ch.leave(NI)
            for t in range(T):
                ins = nc.vector.bn_aggr(mv[:, t, :], st[:, t, :])
            ch(ins)
            root.ask(nc.vector.tensor_scalar(rs[:, :], mv[:, :, 1], eps, None, ALU.add))
            ch(nc.vector.reciprocal(rs[:, :], rs[:, :]))
            ch(nc.vector.scalar_tensor_tensor(out=nm[:, :], in0=mv[:, :, 0], scalar=-1.0, in1=rs[:, :],
                                              op0=ALU.mult, op1=ALU.mult))

        def root_of(fn, ap, scale=1.0):
            fn.take()
            fn.give(nc.scalar.activation(ap, ap, ACT.Sqrt, scale=scale))

        def ln_tiles_dve(v, s, scaled=None, extra=None):
            with v.Fori(0, NI) as i:
                for u in range(U):
                    t = i * U + u
                    v.wait_ge(S(s + "_tp"), t + 1)
                    nc.vector.tensor_scalar(xb[:, u, :], tile_of(X, t), col(rs, t), col(nm, t),
                                            ALU.mult, ALU.add).then_inc(S(s + "_xb"), 1)
                    if scaled is not None:
                        v.wait_ge(S(s + "_xb"), t + 1)
                        nc.vector.tensor_scalar(hb[:, u, :], xb[:, u, :], col(scaled, t), None,
                                                ALU.mult).then_inc(S(s + "_hb"), 1)
                if extra is not None:
                    for u in range(U):
                        extra(i, u, i * U + u)

        def ln_tiles_pe(pe, s, scaled=False, after=None):
            nc.tensor.sem_inc(S(s + "_tp"), U)
            with pe.Fori(0, NI) as i:
                for u in range(U):
                    t = i * U + u
                    pe.wait_ge(S(s + "_xb"), t + 1)
                    pe.wait_ge(S(s + "_free"), t + 1)
                    for k in range(KD):
                        ins = nc.tensor.transpose(PS[:, u, k * P:(k + 1) * P], xb[:, u, k * P:(k + 1) * P], ident[:, :])
                    if scaled:
                        pe.wait_ge(S(s + "_hb"), t + 1)
                        for k in range(KD):
                            ins = nc.tensor.transpose(PS[:, u, D + k * P:D + (k + 1) * P],
                                                      hb[:, u, k * P:(k + 1) * P], ident[:, :])
                        for m in range(KD):
                            nc.tensor.matmul(PS[:, 5 + m, 0:D], hb[:, u, m * P:(m + 1) * P], hb[:, u, :],
                                             start=False, stop=False, skip_group_check=True)
                            ins = nc.tensor.matmul(PS[:, 7, m:m + 1], hb[:, u, m * P:(m + 1) * P], ones[:, 0:1],
                                                   start=False, stop=False, skip_group_check=True)
                    ins.then_inc(S(s + "_tp"), 1)
                if after is not None:
                    for u in range(U):
                        after(i, u, i * U + u)

        def ln_tiles_act(act, s, table=None, scaled=False, free=None):
            nc.scalar.sem_inc(S(s + "_free"), U)
            if table is None:
                act.wait_ge(S("norms"), NORMS.index(s) + 1)
            with act.Fori(0, NI) as i:
                for u in range(U):
                    t = i * U + u
                    a, b = (rs, nm) if table is None else table
                    nc.scalar.activation(tile_of(MB, t), tile_of(X, t), ACT.Identity, bias=col(b, t),
                                         scale=col(a, t)).then_inc(S(s + "_mb"), 1)
                for u in range(U):
                    t = i * U + u
                    act.wait_ge(S(s + "_tp"), t + 1 + U)
                    ins = nc.scalar.activation(XNT[:, :, ds(t * P, P)], v3(PS[:, u, 0:D], P), ACT.Copy)
                    if scaled:
                        ins = nc.scalar.activation(H0T[:, :, ds(t * P, P)], v3(PS[:, u, D:2 * D], P), ACT.Copy)
                    ins.then_inc(S(s + "_free"), 1)

        def table_store(sp, s, dram):
            with sp.Fori(0, NI) as i:
                sp.wait_ge(S(s + "_mb"), i * U + U)
                sp.dma_start(dram.rearrange("(t p) d -> p t d", p=P)[:, ds(i * U, U), :],
                             MB[:, ds(i * U, U), :]).then_inc(S(s + "_table"), 16)
            sp.wait_ge(S(s + "_table"), 16 * NI)

        def gather_pool(pool, s, dram, r, b):
            for q in range(B):
                n = r * G + b * B + q
                nxt = (q + 1) % B
                pool.wait_ge(S(f"{s}_rows{nxt}"), (r * GB + b + (q + 1) // B) * (16 * C))
                nc.gpsimd.tensor_copy(idxs[:, nxt, :], tile_of(idx, b * B + q + 1)).then_inc(S(s + "_idxs"), 1)
                pool.wait_ge(S(s + "_sum"), n + 1)
                pool.wait_ge(S(s + "_idxs"), n + r + 1)
                nc.gpsimd.sem_inc(S("idxs_seen"), 1)
                for j in range(C):
                    nc.gpsimd.indirect_dma_start(
                        out=gath[:, q, j, :], out_offset=None, in_=dram,
                        in_offset=bass.IndirectOffsetOnAxis(ap=idxs[:, q, j:j + 1], axis=0),
                    ).then_inc(S(f"{s}_rows{q}"), 16)

        def first_indices(pool, s, r):
            if not isinstance(r, int):
                pool.wait_ge(S(s + "_idxs"), r * (G + 1))
                pool.sem_inc(S("idxs_seen"), 1)
            nc.gpsimd.tensor_copy(idxs[:, 0, :], tile_of(idx, 0)).then_inc(S(s + "_idxs"), 1)

        def gather_pe(pe, s, r, b, q, degrees):
            n = r * G + b * B + q
            h = q % 2
            pe.wait_ge(S(s + "_oh"), r * (G + 1) + b * B + q + 1)
            pe.wait_ge(S(f"{s}_rows{q}"), (r * GB + b + 1) * (16 * C))
            pe.wait_ge(S(s + "_added"), n + 1)
            for k in range(KD):
                for j in range(C):
                    ins = nc.tensor.matmul(PS[:, 5 + h, k * W:(k + 1) * W], gath[:, q, j, k * P:(k + 1) * P],
                                           oh[:, h, j, :], start=j == 0, stop=j == C - 1)
            if degrees:
                for j in range(C):
                    ins = nc.tensor.matmul(PS[:, 5 + h, KD * W:(KD + 1) * W], ones16[:, :], oh16[:, h, j, :],
                                           start=j == 0, stop=j == C - 1)
            ins.then_inc(S(s + "_sum"), 1)

        def windows(s, g, h, weighted):
            for j in range(C):
                at = rel[:, ds(g, 1), j:j + 1].rearrange("p a c -> p (a c)")
                wt_j = ewt[:, ds(g, 1), j:j + 1].rearrange("p a c -> p (a c)")
                if weighted:
                    nc.vector.tensor_scalar(oh16[:, h, j, :], iota[:, :], at, None, ALU.is_equal)
                    ins = nc.vector.tensor_scalar(oh[:, h, j, :], iota[:, :], at, wt_j, ALU.is_equal, ALU.mult)
                else:
                    ins = nc.vector.tensor_scalar(oh[:, h, j, :], iota[:, :], at, None, ALU.is_equal)
            ins.then_inc(S(s + "_oh"), 1)

        def gather_dve(v, s, r, b, q, weighted, step=None):
            g = b * B + q
            planes = KD + 1 if weighted else KD
            windows(s, g + 1, (q + 1) % 2, weighted)
            if step:
                step(b, q)
            v.wait_ge(S(s + "_sum"), r * G + g + 1 + B)
            start = v.value_load(base[0:1, ds(g, 1)], min_val=0, max_val=N)
            into = ACC[:, 0:planes, ds(start, W)]
            nc.vector.tensor_tensor(into, into, v3(PS[:, 5 + q % 2, 0:planes * W], W), ALU.add)\
                .then_inc(S(s + "_added"), 1)
            v.wait_ge(S(s + "_added"), r * G + g + 1 + 2)

        def next_round(v, s, r):
            nc.vector.tensor_scalar(rel[:, 0:G, :], rel[:, 0:G, :], -float(W), None, ALU.add)\
                .then_inc(S(s + "_round"), 1)
            nc.vector.tensor_scalar(base[:, :], base[:, :], float(W), float(N), ALU.add, ALU.min)\
                .then_inc(S(s + "_round"), 1)
            v.wait_ge(S(s + "_round"), r * 2 + 2)

        def gather_pool_all(pool, s, dram):
            first_indices(pool, s, 0)
            with pool.Fori(0, GB) as b:
                gather_pool(pool, s, dram, 0, b)
            more = pool.value_load(rounds[0:1, 0:1], min_val=1, max_val=MAXR)
            with pool.If(more > 1):
                with pool.Fori(1, more) as r:
                    first_indices(pool, s, r)
                    with pool.Fori(0, GB) as b:
                        gather_pool(pool, s, dram, r, b)

        def gather_pe_all(pe, s, degrees, step):
            nc.tensor.sem_inc(S(s + "_sum"), B)
            with pe.Fori(0, GB) as b:
                for q in range(B):
                    gather_pe(pe, s, 0, b, q, degrees)
                    step(b, q)
            more = pe.value_load(rounds[0:1, 0:1], min_val=1, max_val=MAXR)
            with pe.If(more > 1):
                with pe.Fori(1, more) as r:
                    with pe.Fori(0, GB) as b:
                        for q in range(B):
                            gather_pe(pe, s, r, b, q, degrees)

        def gather_dve_all(v, s, weighted, step):
            nc.vector.sem_inc(S(s + "_added"), 2)
            windows(s, 0, 0, weighted)
            with v.Fori(0, GB) as b:
                for q in range(B):
                    gather_dve(v, s, 0, b, q, weighted, step)
            next_round(v, s, 0)
            more = v.value_load(rounds[0:1, 0:1], min_val=1, max_val=MAXR)
            with v.If(more > 1):
                with v.Fori(1, more) as r:
                    windows(s, 0, 0, weighted)
                    with v.Fori(0, GB) as b:
                        for q in range(B):
                            gather_dve(v, s, r, b, q, weighted)
                    next_round(v, s, r)

        def slot(u):
            return PS[:, u % 4, 0:D]

        def slot_free(t, u):
            return t + 1 + {0: 4, 4: 1}.get(u, 0)

        def bank(u):
            return PS[:, u, 0:D]

        def up_pe(pe, s, c, weights, rhs, at0, units):
            for m, w in enumerate(weights):
                for h in range(2):
                    n = m * 2 + h
                    pe.wait_ge(S(s + "_upfree"), at0 + n + 1)
                    for k in range(KD):
                        ins = nc.tensor.matmul(PS[:, 4 + n % 4, 0:HALF], w[k], rhs(k, c * CH + h * HALF),
                                               start=k == 0, stop=k == KD - 1)
                    ins.then_inc(S(s + "_up"), 1)

        def up_act(act, s, c, units, at0, func, bias, into):
            for m in range(units // 2):
                for h in range(2):
                    n = m * 2 + h
                    act.wait_ge(S(s + "_up"), at0 + n + 1)
                    nc.scalar.activation(into(m)[:, h * HALF:(h + 1) * HALF], PS[:, 4 + n % 4, 0:HALF], func,
                                         bias=bias(m)).then_inc(S(s + "_upfree"), 1)

        def epilogue_act(act, s):
            act.wait_ge(S("norms"), NORMS.index(s) + 1)
            with act.Fori(0, NI) as i:
                for u in range(U):
                    t = i * U + u
                    nc.scalar.activation(tile_of(MB, t), tile_of(MB, t), ACT.Identity, bias=col(nm, t),
                                         scale=col(rs, t)).then_inc(S("mbn"), 1)

        def epilogue_dve(v, ch, s, gb):
            with v.Fori(0, NI) as i:
                ch.enter(i, 3)
                v.wait_ge(S("mbn"), i * U + U + (0 if s == "f0z" else T))
                mb = MB[:, ds(i * U, U), :]
                xx = X[:, ds(i * U, U), :]
                ch(nc.vector.tensor_tensor(mb, mb, gb[:, 0:1, :].to_broadcast((P, U, D)), ALU.mult))
                ch(nc.vector.tensor_tensor(mb, mb, gb[:, 1:2, :].to_broadcast((P, U, D)), ALU.add))
                ch(nc.vector.tensor_tensor(xx, xx, mb, ALU.add))
                if s == "f1z":
                    v.sem_inc(S("x_final"), 1)
            ch.leave(NI)

        @block.sync
        def _(sp):
            def load(dst, src, name):
                sp.dma_start(dst, src).then_inc(S(name), 16)

            sp.wait_ge(S("padded"), 4)
            load(X[:, 0:T - 1, :], A["x"][0:(T - 1) * P, :].rearrange("(t p) d -> p t d", p=P), "x_in")
            load(X[0:TAIL, T - 1, :], A["x"][(T - 1) * P:N, :], "x_in")
            for dst, src in ((srow, A["src"]), (drow, A["dst"]), (wrow, A["edge_weight"])):
                load(dst[0:full_groups, :], src[0:full_groups * GE].rearrange("(g e) -> g e", e=GE), "edges")
                load(dst[full_groups:full_groups + 1, 0:last_group], row(src[full_groups * GE:E]), "edges")
            load(wc, A["wc"].rearrange("(k p) o -> p k o", p=P), "w_conv")
            load(bng, A["bn_gamma"], "w_conv")
            load(bnb, A["bn_beta"], "w_conv")
            load(wres, A["w_res"].rearrange("(k p) o -> p k o", p=P), "w_mix")
            sp.wait_ge(S("bd_zero"), 1)
            for q in range(4):
                load(bd[32 * q:32 * q + 32, :, 32 * q:32 * q + 32],
                     A["w_pw"].rearrange("(j p) o -> p j o", p=P)[32 * q:32 * q + 32, :, :], "w_mix")
            load(dw_, A["w_dw"], "w_mix")
            load(bres_, A["b_res"].partition_broadcast(P), "w_mix")
            stage_end(sp, 1)
            table_store(sp, "l0", xn_dram)
            stage_end(sp, 2)
            for h in range(KD):
                sp.dma_start(xe_dram.rearrange("(t p) d -> p t d", p=P)[:, :, h * P:(h + 1) * P],
                             zeros[:, :].rearrange("p (t d) -> p t d", t=1)
                             .to_broadcast((P, SLOTS // P + TOPK, P))).then_inc(S("slots_zero"), 16)
            stage_end(sp, 3)
            load(w1t, A["g0_w1"].rearrange("(k p) o -> p k o", p=P), "w_g0")
            load(w2t, A["g0_w2"].rearrange("(k p) o -> p k o", p=P), "w_g0")
            load(brow_[0:1, 0:D], row(A["g0_b1"]), "w_g0")
            load(brow_[0:1, D:2 * D], row(A["g0_b2"]), "w_g0")
            stage_end(sp, 4)
            load(wr, A["f0_wr"].rearrange("(k p) e -> p k e", p=P), "w_router")
            load(r0[0:1, 0, :], row(A["f0_br"]), "w_router")
            load(gb0[:, 0, :], A["f0_gamma"].partition_broadcast(P), "w_f0n")
            load(gb0[:, 1, :], A["f0_beta"].partition_broadcast(P), "w_f0n")
            sp.wait_ge(S("routed"), 1)
            for k in range(TOPK):
                e = sp.value_load(r0[0:1, 9, k:k + 1].bitcast(I32), min_val=0, max_val=E0 - 1)
                load(f0w1[:, k, :, :], A["f0_w1"].rearrange("e (k p) f -> e p k f", p=P)[ds(e, 1), :, :, :]
                     .rearrange("a p k f -> (a p) k f"), "w_f0")
                load(f0w2[:, k, :, :], A["f0_w2"].rearrange("e (k p) f -> e p k f", p=P)[ds(e, 1), :, :, :]
                     .rearrange("a p k f -> (a p) k f"), "w_f0")
                load(f0b1_[:, 4 * k:4 * k + 4], A["f0_b1"][ds(e, 1), :, :]
                     .rearrange("a p m -> (a p) m"), "w_f0")
                load(f0row_[0:1, k * D:(k + 1) * D], A["f0_b2"][ds(e, 1), :], "w_f0")
            stage_end(sp, 5)
            table_store(sp, "l1", xs_dram)
            stage_end(sp, 6)
            load(g1w1, A["g1_w1"].rearrange("(k p) o -> p k o", p=P), "w_g1")
            load(g1w2, A["g1_w2"].rearrange("(k p) o -> p k o", p=P), "w_g1")
            load(g1b1_, A["g1_b1"], "w_g1")
            load(g1row_[0:1, :], row(A["g1_b2"]), "w_g1")
            load(kwc_[:, 0:2], A["m1_kw"], "w_m1")
            load(kwc_[:, 2:4], A["m1_kb"], "w_m1")
            load(vwb_[:, 0:D], A["m1_vw"].partition_broadcast(P), "w_m1")
            load(vwb_[:, D:2 * D], A["m1_vb"].partition_broadcast(P), "w_m1")
            stage_end(sp, 7)
            stage_end(sp, 8)
            load(gate, A["f1_wg"].rearrange("(k p) e -> p k e", p=P), "w_gate")
            load(grow_[0:1, :], row(A["f1_bg"]), "w_gate")
            load(b2f[0:E1, :], A["f1_b2"], "w_gate")
            load(e_w2[:, WAIT:E1, :, :], A["f1_w2"].rearrange("e (k p) f -> p e k f", p=P)[:, WAIT:E1, :, :], "w_f1")
            stage_end(sp, 9)
            load(b1t, A["f1_b1"].rearrange("e p m -> p e m"), "w_b1")
            load(e_w1, A["f1_w1"].rearrange("e (k p) f -> p e k f", p=P), "w_f1")
            load(e_w2[:, 0:WAIT, :, :], A["f1_w2"].rearrange("e (k p) f -> p e k f", p=P)[:, 0:WAIT, :, :], "w_f1")
            sp.wait_ge(S("f1_scattered"), 1)
            with sp.Fori(0, PAIRS + 1) as i:
                for k in range(2):
                    sp.wait_ge(S("f1_tx"), i * 2 + k + 1)
                    sp.dma_start(xs[:, k, :], xe_dram[ds((i * 2 + k) * P, P), :]).then_inc(S(f"f1_xs{k}"), 16)
            stage_end(sp, 10)
            load(gb1[:, 0, :], A["f1_gamma"].partition_broadcast(P), "w_f1n")
            load(gb1[:, 1, :], A["f1_beta"].partition_broadcast(P), "w_f1n")
            with sp.Fori(0, NI - 1) as i:
                sp.wait_ge(S("x_final"), i + 1)
                sp.dma_start(out[0:(T - U) * P, :].rearrange("(t p) d -> p t d", p=P)[:, ds(i * U, U), :],
                             X[:, ds(i * U, U), :]).then_inc(S("out"), 16)
            sp.wait_ge(S("x_final"), NI)
            sp.dma_start(out[(T - U) * P:(T - 1) * P, :].rearrange("(t p) d -> p t d", p=P),
                         X[:, T - U:T - 1, :]).then_inc(S("out"), 16)
            sp.dma_start(out[(T - 1) * P:N, :], X[0:TAIL, T - 1, :]).then_inc(S("out"), 16)
            sp.wait_ge(S("out"), 16 * (NI + 1))

        @block.gpsimd
        def _(pool):
            nc.gpsimd.memset(srow, 0).then_inc(S("padded"), 1)
            nc.gpsimd.memset(drow, int(BIG)).then_inc(S("padded"), 1)
            nc.gpsimd.memset(wrow, 0.0).then_inc(S("padded"), 1)
            nc.gpsimd.memset(X[:, T - 1, :], 0.0).then_inc(S("padded"), 1)
            nc.gpsimd.memset(bd_, 0.0).then_inc(S("bd_zero"), 1)
            nc.gpsimd.memset(ident[:, :], 0.0).then_inc(S("pool_set"), 1)
            nc.gpsimd.memset(valid[:, :], 1.0).then_inc(S("pool_set"), 1)
            nc.gpsimd.memset(blockones[:, :], 0.0).then_inc(S("pool_set"), 1)
            pool.wait_ge(S("pool_set"), 3)
            nc.gpsimd.affine_select(out=ident[:, :], in_=ident[:, :], compare_op=ALU.not_equal, fill=1.0,
                                    base=0, pattern=[[-1, P]], channel_multiplier=1).then_inc(S("consts"), 1)
            nc.gpsimd.affine_select(out=valid[:, :], in_=valid[:, :], compare_op=ALU.is_ge, fill=0.0,
                                    base=N - 1, pattern=[[-P, T]], channel_multiplier=-1).then_inc(S("consts"), 1)
            for q in range(4):
                pool.wait_ge(S("consts"), q + 2)
                nc.gpsimd.memset(blockones[32 * q:32 * q + 32, 32 * q:32 * q + 32], 1.0).then_inc(S("consts"), 1)
            pool.wait_ge(S("consts"), 6)
            nc.gpsimd.memset(ones[:, :], 1.0).then_inc(S("consts"), 1)
            nc.gpsimd.memset(zeros[:, :], 0.0).then_inc(S("consts"), 1)
            nc.gpsimd.memset(ones16[:, :], 1.0).then_inc(S("consts"), 1)
            nc.gpsimd.iota(iota[:, :], pattern=[[1, W]], base=0, channel_multiplier=0,
                           allow_small_or_imprecise_dtypes=True).then_inc(S("consts"), 1)
            nc.gpsimd.iota(pcol[:, 0:1], pattern=[[0, 1]], base=0, channel_multiplier=1,
                           allow_small_or_imprecise_dtypes=True).then_inc(S("consts"), 1)
            nc.gpsimd.memset(before[:, :], 1.0).then_inc(S("consts"), 1)
            pool.wait_ge(S("consts"), 12)
            nc.gpsimd.affine_select(out=before[:, :], in_=before[:, :], compare_op=ALU.is_ge, fill=0.0,
                                    base=-1, pattern=[[1, P]], channel_multiplier=-1).then_inc(S("consts"), 1)
            nc.gpsimd.memset(rel[:, :, :], -1.0).then_inc(S("consts"), 1)
            nc.gpsimd.memset(ewt[:, :, :], 0.0).then_inc(S("consts"), 1)
            nc.gpsimd.memset(idx[:, G, :], 0).then_inc(S("consts"), 1)
            nc.gpsimd.memset(ACC[:, :, :], 0.0).then_inc(S("consts"), 1)
            nc.gpsimd.memset(H0T[:, :, NP:NP + P], 0.0).then_inc(S("consts"), 1)
            stage_end(pool, 1)
            stage_end(pool, 2)
            gather_pool_all(pool, "g0", xn_dram)
            stage_end(pool, 3)
            stage_end(pool, 4)
            nc.gpsimd.memset(ACC[:, 0:KD, :], 0.0)
            stage_end(pool, 5)
            stage_end(pool, 6)
            gather_pool_all(pool, "g1", xs_dram)
            stage_end(pool, 7)
            stage_end(pool, 8)
            stage_end(pool, 9)
            pool.wait_ge(S("f1_slots"), 1)
            pool.wait_ge(S("slots_zero"), 16 * KD)
            with pool.Fori(0, NI) as i:
                for u in range(U):
                    t = i * U + u
                    pool.wait_ge(S("f1_sct"), t + 1)
                    pool.wait_ge(S(f"f1_rows{u}"), i * (16 * TOPK))
                    nc.gpsimd.tensor_copy(idxs[:, u, 0:TOPK], slots[:, :, ds(t, 1)].rearrange("p k a -> p (k a)"))\
                        .then_inc(S("f1_idxs"), 1)
                    pool.wait_ge(S("f1_idxs"), t + 1)
                    pool.sem_inc(S("idxs_seen"), 1)
                    for k in range(TOPK):
                        nc.gpsimd.indirect_dma_start(
                            out=xe_dram, out_offset=bass.IndirectOffsetOnAxis(ap=idxs[:, u, k:k + 1], axis=0),
                            in_=sct[:, u, :], in_offset=None).then_inc(S(f"f1_rows{u}"), 16)
            for u in range(U):
                pool.wait_ge(S(f"f1_rows{u}"), NI * 16 * TOPK)
            nc.gpsimd.sem_inc(S("f1_scattered"), 1)
            nc.gpsimd.sem_inc(S("f1_ys_free"), 2)
            with pool.Fori(0, PAIRS) as i:
                for k in range(2):
                    pool.wait_ge(S("f1_ys"), i * 2 + k + 1 + 2)
                    pool.sem_inc(S("idxs_seen"), 1)
                    nc.gpsimd.dma_start(xe_dram[ds((i * 2 + k) * P, P), :], ys[:, k, :]).then_inc(S(f"f1_out{k}"), 16)
                for k in range(2):
                    pool.wait_ge(S(f"f1_out{k}"), i * 16 + 16)
                    pool.sem_inc(S("f1_ys_free"), 1)
            stage_end(pool, 10)
            for k in range(2):
                pool.wait_ge(S(f"f1_out{k}"), PAIRS * 16)
            with pool.Fori(0, NI) as i:
                for u in range(U):
                    t = i * U + u
                    pool.wait_ge(S("f1_cmb"), t + 1)
                    nc.gpsimd.tensor_copy(idxs[:, u, 0:TOPK], slots[:, :, ds(t, 1)].rearrange("p k a -> p (k a)"))\
                        .then_inc(S("f1_idxs"), 1)
                    pool.wait_ge(S("f1_idxs"), T + t + 1)
                    pool.sem_inc(S("idxs_seen"), 1)
                    for k in range(TOPK):
                        nc.gpsimd.indirect_dma_start(
                            out=cmb[:, u, k, :], out_offset=None, in_=xe_dram,
                            in_offset=bass.IndirectOffsetOnAxis(ap=idxs[:, u, k:k + 1], axis=0),
                        ).then_inc(S(f"f1_rows{u}"), 16)

        @block.scalar
        def _(act):
            fn = Asked(act, S("asked"), S("answered"))
            root_of(fn, rs[:, :])
            fn.take()
            fn.give(nc.scalar.activation(sc[:, 1, :], sc[:, 0, :], ACT.Sqrt))
            fn.take()
            fn.give(nc.scalar.activation(sc[:, 4, :], sc[:, 3, :], ACT.Ln))
            stage_end(act, 1)
            ln_tiles_act(act, "l0", scaled=True)
            act.wait_ge(S("gram"), 1)
            nc.scalar.activation(gram, PS[:, 5:7, 0:D], ACT.Copy).then_inc(S("gram_sb"), 1)
            root_of(fn, bnu)
            stage_end(act, 2)
            def mixer_relu(t):
                act.wait_ge(S("mix_conv"), t + 1)
                act.wait_ge(S("mix_hh"), t + 1)
                for j in range(KQ):
                    nc.scalar.activation(hh[:, 2 + j, :], PS[:, j // 4, (j % 4) * P:(j % 4 + 1) * P], ACT.Relu,
                                         bias=bnt[:, j:j + 1], scale=bns[:, j:j + 1]).then_inc(S("mix_h"), 1)
                act.wait_ge(S("mix_h"), t * KQ + KQ)
                nc.scalar.activation(hsq, hh[:, 2:8, :], ACT.Square)

            mixer_relu(0)
            nc.scalar.sem_inc(S("mix_read"), 1)
            with act.Fori(0, T) as t:
                act.wait_ge(S("mix_s"), t + 1)
                psf = PS[:, :, :].rearrange("p b n -> p (b n)")[:, 1024:1024 + TD]
                nc.scalar.activation(hh_[:, 0:2 * P], psf[:, 0:2 * P], ACT.Relu)
                nc.scalar.activation(hh_[:, 8 * P:10 * P], psf[:, 4 * P:6 * P], ACT.Copy)
                nc.scalar.activation(ks_, psf[:, 2 * P:4 * P], ACT.Relu)
                nc.scalar.activation(ssq_, psf, ACT.Square).then_inc(S("mix_qv"), 1)
                act.wait_ge(S("mix_f"), t + 1)
                nc.scalar.activation(ff[:, 2, :], ff[:, 0, :], ACT.Sqrt, scale=1e-30).then_inc(S("mix_eps"), 1)
                act.wait_ge(S("mix_o"), t + 1 + 1)
                nc.scalar.activation(osq_, oo_, ACT.Square).then_inc(S("mix_osq"), 1)
                mixer_relu(t + 1)
                act.wait_ge(S("mix_ft"), t + 1 + 1)
                act.sem_inc(S("act_seen"), 1)
                nc.scalar.activation(tile_of(MB, t), PS[:, 7, D:2 * D], ACT.Copy)
                nc.scalar.activation(sc[:, 0:2, ds(t, 1)].rearrange("p k a -> p (k a)"), PS[:, 7, 0:2], ACT.Copy)\
                    .then_inc(S("mix_read"), 1)
            stage_end(act, 3)
            root_of(fn, sc[:, 0, :])
            with act.Fori(0, NI) as i:
                for u in range(U):
                    t = i * U + u
                    act.wait_ge(S("m0_ft"), t + 1)
                    nc.scalar.activation(ust_[:, 0:D], tile_of(MB, t), ACT.Square, accum_out=col(sc[:, 1, :], t))\
                        .then_inc(S("m0_sq"), 1)
                    act.wait_ge(S("m0_sq"), t + 1)
            fn.take()
            nc.scalar.activation(sc[:, 2, :], sc[:, 1, :], ACT.Sqrt).then_inc(S("m0_n4"), 1)
            act.wait_ge(S("m0_n4"), 1)
            fn.give(nc.scalar.activation(sc[:, 3, :], sc[:, 2, :], ACT.Tanh))
            act.wait_ge(S("m0_done"), 1)
            with act.Fori(0, NI) as i:
                for u in range(U):
                    t = i * U + u
                    act.wait_ge(S("n0_mm"), t + 1)
                    nc.scalar.activation(stg[:, u, :, :], XNT[:, :, ds(t * P, P)], ACT.Copy)\
                        .then_inc(S("n0_stg"), 1)
                for u in range(U):
                    t = i * U + u
                    act.wait_ge(S("n0_y"), t + 1)
                    nc.scalar.activation(hb[:, u, :], tile_of(MB, t), ACT.Square,
                                         accum_out=col(sc[:, 1, :], t)).then_inc(S("n0_ss"), 1)
            root_of(fn, sc[:, 1, :])
            stage_end(act, 4)
            root_of(fn, rs[:, :])
            ln_tiles_act(act, "f0")
            for k in range(TOPK + 1):
                fn.take()
                n = E0 if k < 2 else 1
                fn.give(nc.scalar.activation(r0[0:1, 2, 0:n], r0[0:1, 1, 0:n], ACT.Exp))
            nc.scalar.sem_inc(S("f0_upfree"), 4)
            act.wait_ge(S("w_f0"), 16 * 8)
            with act.Fori(0, NCH) as c:
                act.wait_ge(S("f0_dn"), c * U + U)
                for e in range(TOPK):
                    up_act(act, "f0", c, 8, c * 16 + 8 * e, ACT.Gelu,
                           lambda m: f0b1_[:, 4 * e + m:4 * e + m + 1], lambda m: f0h[:, e, m, :])
            root_of(fn, rs[:, :])
            epilogue_act(act, "f0z")
            stage_end(act, 5)
            root_of(fn, ACC[:, KD, 0:NP])
            root_of(fn, rs[:, :])
            act.wait_ge(S("norms"), NORMS.index("l1") + 1)
            ln_tiles_act(act, "l1", table=(sc[:, 0, :], sc[:, 1, :]))
            stage_end(act, 6)
            with act.Fori(0, T) as t:
                act.wait_ge(S("m1_c"), t + 1)
                nc.scalar.activation(csq, zb, ACT.Square).then_inc(S("m1_sq"), 1)
                act.wait_ge(S("m1_ss"), t + 1)
                nc.scalar.activation(hst[:, 2, :], hst[:, 1, :], ACT.Sqrt, scale=1.0 / (HC - 1))\
                    .then_inc(S("m1_std"), 1)
            stage_end(act, 7)
            nc.scalar.sem_inc(S("g1_upfree"), 4)
            act.wait_ge(S("w_g1"), 16 * 4)
            with act.Fori(0, NCH) as c:
                act.wait_ge(S("g1_dn"), c * U + U)
                up_act(act, "g1", c, 16, c * 16, ACT.Gelu, lambda m: g1b1_[:, m:m + 1], lambda m: g1h[:, m, :])
            stage_end(act, 8)
            root_of(fn, rs[:, :])
            ln_tiles_act(act, "f1")
            fn.take()
            fn.give(nc.scalar.activation(sc[:, 1, :], sc[:, 0, :], ACT.Exp))
            stage_end(act, 9)
            with act.Fori(0, NI) as i:
                for u in range(U):
                    act.wait_ge(S(f"f1_rows{u}"), i * (16 * TOPK))
                    act.sem_inc(S("act_seen"), 1)
                    nc.scalar.activation(sct[:, u, :], tile_of(MB, i * U + u), ACT.Copy).then_inc(S("f1_sct"), 1)
            act.wait_ge(S("f1_scattered"), 1)

            def copy_xt(n, k):
                act.wait_ge(S("f1_tx"), n + 1 + 2)
                nc.scalar.activation(xt[:, k, :, :], v3(PS[:, k, 0:D], P), ACT.Copy).then_inc(S("f1_xt"), 1)

            for k in range(2):
                copy_xt(k, k)
            with act.Fori(0, PAIRS) as i:
                for k in range(2):
                    act.wait_ge(S("f1_h"), i * 2 + k + 1)
                    act.wait_ge(S("f1_y"), i * 2 + k + 1)
                    for m in range(4):
                        ins = nc.scalar.activation(ht[:, k, m, :], PS[:, 2 + k, m * P:(m + 1) * P], ACT.Relu,
                                                   bias=b1s[:, k, m:m + 1])
                    ins.then_inc(S("f1_ht"), 1)
                for k in range(2):
                    copy_xt(i * 2 + 2 + k, k)
            stage_end(act, 10)
            root_of(fn, rs[:, :])
            epilogue_act(act, "f1z")

        @block.tensor
        def _(pe):
            pe.wait_ge(S("consts"), 18)
            for q, rows in enumerate((sf, rf, wrow)):
                pe.wait_ge(S("tab_rows"), q + 1)
                for j in range(C):
                    ins = nc.tensor.transpose(PS[:, q, j * P:j * P + G], rows[:, j * P:(j + 1) * P], ident[0:G, 0:G])
                ins.then_inc(S("tab_t"), 1)
            pe.wait_ge(S("tab_rows"), 4)
            nc.tensor.transpose(PS[0:1, 3, 0:G], gb2[:, 0:1], ident[0:G, 0:G])
            nc.tensor.transpose(PS[0:1, 3, P:P + G], gb2[:, 1:2], ident[0:G, 0:G]).then_inc(S("tab_t"), 1)
            stage_end(pe, 1)
            for m in range(KD):
                nc.tensor.matmul(PS[:, 5 + m, 0:P], zeros[:, :], ident[:, :], start=True, stop=False, skip_group_check=True)
                nc.tensor.matmul(PS[:, 5 + m, P:D], zeros[:, :], ident[:, :], start=False, stop=False, skip_group_check=True)
            nc.tensor.matmul(PS[:, 7, 0:KD], zeros[:, :], ident[:, 0:KD], start=True, stop=False, skip_group_check=True)
            ln_tiles_pe(pe, "l0", scaled=True)
            for m in range(KD):
                nc.tensor.matmul(PS[:, 5 + m, 0:P], zeros[:, :], ident[:, :], start=False, stop=True, skip_group_check=True)
            nc.tensor.matmul(PS[:, 7, 0:KD], zeros[:, :], ident[:, 0:KD], start=False, stop=True,
                             skip_group_check=True).then_inc(S("gram"), 1)
            pe.wait_ge(S("w_conv"), 16 * 3)
            pe.wait_ge(S("gram_sb"), 2)
            pe.wait_ge(S("l0_free"), T + U)
            for m in range(KD):
                for h in range(2):
                    for k in range(KD):
                        ins = nc.tensor.matmul(PS[:, 2 * m + h, 0:TD // 2], gram[:, k, m * P:(m + 1) * P],
                                               wc[:, k, h * (TD // 2):(h + 1) * (TD // 2)], start=k == 0, stop=k == KD - 1)
            ins.then_inc(S("bn_cw"), 1)
            for j in range(KQ):
                for k in range(KD):
                    nc.tensor.matmul(PS[:, 7, 8 + j:9 + j], wc[:, k, j * P:(j + 1) * P], sc[:, 7, k:k + 1],
                                     start=k == 0, stop=k == KD - 1)
            pe.wait_ge(S("bn_zz"), 1)
            for j in range(KQ):
                for k in range(KD):
                    ins = nc.tensor.matmul(PS[:, 7, 16 + j:17 + j], zz[:, k, j * P:(j + 1) * P], ones[:, 0:1],
                                           start=k == 0, stop=k == KD - 1)
            ins.then_inc(S("bn_sums"), 1)
            stage_end(pe, 2)

            def mixer_conv(t):
                for j in range(KQ):
                    for k in range(KD):
                        ins = nc.tensor.matmul(PS[:, j // 4, (j % 4) * P:(j % 4 + 1) * P],
                                               wc[:, k, j * P:(j + 1) * P], H0T[:, k, ds(t * P, P)],
                                               start=k == 0, stop=k == KD - 1)
                ins.then_inc(S("mix_conv"), 1)

            def mixer_pe(t, q):
                if q == 0:
                    pe.wait_ge(S("mix_h"), t * KQ + KQ)
                    pe.wait_ge(S("mix_o"), t + 1)
                    for j in range(KQ):
                        nc.tensor.matmul(PS[:, 2 + j // 4, (j % 4) * P:(j % 4 + 1) * P], bd[:, j, :],
                                         hh[:, 2 + j, :], start=True, stop=True)
                    for j in range(2):
                        ins = nc.tensor.matmul(PS[:, 4, j * P:(j + 1) * P], blockones[:, :], hh[:, 4 + j, :],
                                               start=True, stop=True)
                    ins.then_inc(S("mix_s"), 1)
                elif q == 1:
                    pe.wait_ge(S("mix_qv"), t + 1)
                    for j in range(2):
                        nc.tensor.matmul(PS[:, 4, (2 + j) * P:(3 + j) * P], blockones[:, :], ks[:, j, :],
                                         start=True, stop=True)
                    for j in range(2 * KQ):
                        ins = nc.tensor.matmul(PS[:, 3, D:D + P], ones[:, :], (hsq, ssq)[j // KQ][:, j % KQ, :],
                                               start=j == 0, stop=j == 2 * KQ - 1)
                    ins.then_inc(S("mix_sums"), 1)
                elif q == 3:
                    mixer_conv(t + 1)
                    pe.wait_ge(S("mix_o"), t + 1 + 1)
                    pe.wait_ge(S("mix_read"), t + 1)
                    for j in range(4):
                        nc.tensor.matmul(PS[:, 7, D:2 * D], oo[:, j, :], wres[:, j, :], start=j == 0, stop=j == 3)
                    nc.tensor.matmul(PS[:, 7, 1:2], ff[:, 0, :], ident[:, 0:1], start=True, stop=True)
                    pe.wait_ge(S("mix_osq"), t + 1)
                    for j in range(4):
                        ins = nc.tensor.matmul(PS[:, 7, 0:1], osq[:, j, :], ones[:, 0:1], start=j == 0, stop=j == 3)
                    ins.then_inc(S("mix_ft"), 1)

            mixer_conv(0)
            nc.tensor.sem_inc(S("mix_ft"), 1)
            gather_pe_all(pe, "g0", True, mixer_pe)
            stage_end(pe, 3)
            nc.tensor.sem_inc(S("n0_mm"), U)
            pe.wait_ge(S("w_g0"), 16 * 4)
            pe.wait_ge(S("n0_brow"), 1)
            with pe.Fori(0, NI) as i:
                for u in range(U):
                    t = i * U + u
                    pe.wait_ge(S("n0_stg"), t + 1)
                    pe.wait_ge(S("n0_u"), t + 1)
                    pe.wait_ge(S("n0_ps"), t + 1)
                    nc.tensor.matmul(bank(u), ones[0:1, :], brow_[0:1, 2 * D:3 * D], start=True, stop=False)
                    for k in range(KD):
                        nc.tensor.matmul(bank(u), stg[:, u, k, :], w1t[:, k, :], start=False, stop=False)
                    for k in range(KD):
                        ins = nc.tensor.matmul(bank(u), ust[:, u, k, :], w2t[:, k, :], start=False, stop=k == KD - 1)
                    ins.then_inc(S("n0_mm"), 1)
            stage_end(pe, 4)
            ln_tiles_pe(pe, "f0")
            pe.wait_ge(S("f0_ysum"), 1)
            pe.wait_ge(S("w_router"), 32)
            for k in range(KD):
                ins = nc.tensor.matmul(PS[0:1, 5, 0:E0], ysum[:, k:k + 1], wr[:, k, :], start=k == 0, stop=k == KD - 1)
            ins.then_inc(S("route_mm"), 1)
            pe.wait_ge(S("routed"), 1)
            nc.tensor.matmul(PS[:, 3, 0:TOPK], ones[0:1, :], r0[0:1, 8, 0:TOPK], start=True, stop=True)\
                .then_inc(S("route_mm"), 1)
            nc.tensor.sem_inc(S("f0_dn"), U)
            pe.wait_ge(S("w_f0"), 16 * 8)
            with pe.Fori(0, NCH) as c:
                for e in range(TOPK):
                    up_pe(pe, "f0", c, [[f0w1[:, e, k, m * P:(m + 1) * P] for k in range(KD)] for m in range(4)],
                          lambda k, at: XNT[:, k, ds(at, HALF)], c * 16 + 8 * e, 8)
                pe.wait_ge(S("f0_upfree"), c * 16 + 16 + 4)
                pe.wait_ge(S("f0_w2s"), 1)
                for u in range(U):
                    pe.wait_ge(S("f0_dfree"), slot_free(c * U + u, u))
                    nc.tensor.matmul(slot(u), ones[0:1, :], f0row_[0:1, 2 * D:3 * D], start=True, stop=False)
                    for e in range(TOPK):
                        for k in range(4):
                            ins = nc.tensor.matmul(slot(u), f0h[:, e, k, u * P:(u + 1) * P], f0w2[:, e, k, :],
                                                   start=False, stop=(e, k) == (TOPK - 1, 3))
                    ins.then_inc(S("f0_dn"), 1)
            stage_end(pe, 5)
            ln_tiles_pe(pe, "l1")
            stage_end(pe, 6)
            for at in range(0, D, P):
                nc.tensor.matmul(PS[:, 0, at:at + P], zeros[:, :], ident[:, :], start=at == 0, stop=False, skip_group_check=True)
                nc.tensor.matmul(PS[:, 1, at:at + P], zeros[:, :], ident[:, :], start=at == 0, stop=False, skip_group_check=True)
            nc.tensor.matmul(PS[:, 2, 0:KD], zeros[:, :], ident[:, 0:KD], start=True, stop=False, skip_group_check=True)
            nc.tensor.sem_inc(S("m1_mm"), 1)

            def mixer1_pe(t, q):
                if q == 3:
                    pe.wait_ge(S("m1_z"), t + 1)
                    for m in range(KD):
                        nc.tensor.matmul(PS[:, 0, m * P:(m + 1) * P], zb[:, m * P:(m + 1) * P], zb[:, m * P:(m + 1) * P],
                                         start=False, stop=False, skip_group_check=True)
                        nc.tensor.matmul(PS[:, 2, m:m + 1], zb[:, m * P:(m + 1) * P], ones[:, 0:1],
                                         start=False, stop=False, skip_group_check=True)
                    nc.tensor.matmul(PS[:, 1, 0:D], ones[:, :], zb[:, 0:D],
                                     start=False, stop=False, skip_group_check=True).then_inc(S("m1_mm"), 1)

            gather_pe_all(pe, "g1", False, mixer1_pe)
            for b in range(2):
                nc.tensor.matmul(PS[:, b, 0:P], zeros[:, :], ident[:, :], start=False, stop=True, skip_group_check=True)
            nc.tensor.matmul(PS[:, 2, 0:KD], zeros[:, :], ident[:, 0:KD], start=False, stop=True, skip_group_check=True)
            stage_end(pe, 7)
            nc.tensor.sem_inc(S("g1_dn"), U)
            pe.wait_ge(S("w_g1"), 16 * 4)
            pe.wait_ge(S("agg"), 1)
            with pe.Fori(0, NCH) as c:
                up_pe(pe, "g1", c, [[g1w1[:, k, m * P:(m + 1) * P] for k in range(KD)] for m in range(8)],
                      lambda k, at: ACC[:, k, ds(at, HALF)], c * 16, 16)
                pe.wait_ge(S("g1_upfree"), c * 16 + 16 + 4)
                for u in range(U):
                    pe.wait_ge(S("g1_dfree"), slot_free(c * U + u, u))
                    pe.wait_ge(S("g1_stg"), c * U + u + 1)
                    nc.tensor.matmul(slot(u), ones[0:1, :], g1row_[0:1, :], start=True, stop=False)
                    for m in range(KD):
                        nc.tensor.matmul(slot(u)[:, m * P:(m + 1) * P], stg1[:, u, m, :], kv[:, m, :], start=False, stop=False)
                    for k in range(8):
                        ins = nc.tensor.matmul(slot(u), g1h[:, k, u * P:(u + 1) * P], g1w2[:, k, :],
                                               start=False, stop=k == 7)
                    ins.then_inc(S("g1_dn"), 1)
            stage_end(pe, 8)
            nc.tensor.sem_inc(S("f1_gate"), U)
            pe.wait_ge(S("w_gate"), 48)

            def gate_pe(i, u, t):
                pe.wait_ge(S("f1_stg"), t + 1)
                ins = nc.tensor.matmul(PS[:, u, D:D + E1], ones[0:1, :], grow_[0:1, :], start=True, stop=False)
                for k in range(KD):
                    ins = nc.tensor.matmul(PS[:, u, D:D + E1], stg2[:, u, k, :], gate[:, k, :],
                                           start=False, stop=k == KD - 1)
                ins.then_inc(S("f1_gate"), 1)

            ln_tiles_pe(pe, "f1", after=gate_pe)
            pe.wait_ge(S("f1_cnt"), 1)
            nc.tensor.matmul(PS[:, 5, 0:T * E1], before[:, :], cnt_, start=True, stop=True)
            nc.tensor.matmul(PS[:, 6, 0:T * E1], ones[:, :], cnt_, start=True, stop=True).then_inc(S("f1_rank"), 1)
            stage_end(pe, 9)
            pe.wait_ge(S("w_f1"), 48)
            pe.wait_ge(S("f1_b3"), 1)

            def transpose_x(n, k):
                pe.wait_ge(S(f"f1_xs{k}"), 16 + (n - k) * 8)
                for m in range(KD):
                    ins = nc.tensor.transpose(PS[:, k, m * P:(m + 1) * P], xs[:, k, m * P:(m + 1) * P], ident[:, :])
                ins.then_inc(S("f1_tx"), 1)

            nc.tensor.sem_inc(S("f1_tx"), 2)
            nc.tensor.sem_inc(S("f1_y"), 2)
            for k in range(2):
                transpose_x(k, k)
            with pe.Fori(0, PAIRS) as i:
                for k in range(2):
                    n = i * 2 + k
                    pe.wait_ge(S("f1_xt"), n + 1)
                    pe.wait_ge(S("f1_w"), n + 1)
                    for m in range(4):
                        for j in range(KD):
                            ins = nc.tensor.matmul(PS[:, 2 + k, m * P:(m + 1) * P], w1s[:, k, j, m * P:(m + 1) * P],
                                                   xt[:, k, j, :], start=j == 0, stop=j == KD - 1)
                    ins.then_inc(S("f1_h"), 1)
                for k in range(2):
                    transpose_x(i * 2 + 2 + k, k)
                for k in range(2):
                    n = i * 2 + k
                    e = pe.value_load(eji[0:1, ds(n, 1)], min_val=0, max_val=E1 - 1)
                    pe.wait_ge(S("f1_ht"), n + 1)
                    pe.wait_ge(S("f1_sel"), n + 1)
                    pe.wait_ge(S("f1_ys"), n + 1)
                    nc.tensor.matmul(PS[:, 6 + k, 0:D], sel[0:96, k, :], b3[0:96, :], start=True, stop=False)
                    for m in range(4):
                        ins = nc.tensor.matmul(PS[:, 6 + k, 0:D], ht[:, k, m, :],
                                               e_w2[:, ds(e, 1), m, :].rearrange("p a f -> p (a f)"),
                                               start=False, stop=m == 3)
                    ins.then_inc(S("f1_y"), 1)
            stage_end(pe, 10)

        @block.vector
        def _(v):
            ch = Chain(v, S("dve"))
            fn = Asked(v, S("asked"), S("answered"))
            v.wait_ge(S("edges"), 16 * 6)
            nc.vector.tensor_copy(sf, srow).then_inc(S("tab_rows"), 1)
            ch(nc.vector.tensor_copy(df, drow))
            ch(nc.vector.tensor_reduce(out=gb2[:, 0:1], in_=df, axis=AX.X, op=ALU.min))
            ch(nc.vector.tensor_scalar(rf, df, gb2[:, 0:1], None, ALU.subtract))
            ch(nc.vector.scalar_tensor_tensor(out=mf, in0=df, scalar=BIG / 2, in1=rf, op0=ALU.is_lt, op1=ALU.mult))
            v.sem_inc(S("tab_rows"), 2)
            ch(nc.vector.tensor_reduce(out=gb2[:, 1:2], in_=mf, axis=AX.X, op=ALU.max))
            ch(nc.vector.tensor_scalar(gb2[:, 0:1], gb2[:, 0:1], float(N), None, ALU.min))
            v.sem_inc(S("tab_rows"), 1)
            v.wait_ge(S("tab_t"), 4)
            v.wait_ge(S("consts"), 18)
            for q, table in enumerate((idx[:, 0:G, :], rel0[:, :, :], ewt[:, 0:G, :])):
                ch(nc.vector.tensor_copy(table.rearrange("p g c -> p c g"), v3(PS[:, q, :], P)[:, :, 0:G]))
            ch(nc.vector.tensor_copy(rel[:, 0:G, :], rel0[:, :, :]))
            ch(nc.vector.tensor_copy(base0[:, :], PS[0:1, 3, 0:G]))
            ch(nc.vector.tensor_copy(base[:, :], base0[:, :]))
            ch(nc.vector.tensor_reduce(out=farthest[:, :], in_=PS[0:1, 3, P:P + G], axis=AX.X, op=ALU.max))
            ch(nc.vector.tensor_scalar(rounds[:, :], farthest[:, :], 1.0 / W, 1.0 - (W - 1) / 2 / W, ALU.mult, ALU.add))
            v.wait_ge(S("x_in"), 32)
            ln_stats(v, ch, fn, X, 1e-5)
            n2, n, lo, hi, ln, fac = (sc[:, k, :] for k in range(6))
            ch(nc.vector.tensor_tensor(n2, rs[:, :], rs[:, :], ALU.mult))
            ch(nc.vector.tensor_tensor(n2, n2, mv[:, :, 1], ALU.mult))
            fn.ask(nc.vector.tensor_scalar(n2, n2, float(D), TINY, ALU.mult, ALU.max))
            ch(nc.vector.tensor_scalar(lo, n, MAXNORM, None, ALU.min))
            ch(nc.vector.tensor_scalar(hi, lo, 1.0, None, ALU.add))
            ch(nc.vector.tensor_scalar(lo, lo, -1.0, 1.0, ALU.mult, ALU.add))
            ch(nc.vector.reciprocal(lo, lo))
            fn.ask(nc.vector.tensor_tensor(hi, hi, lo, ALU.mult))
            ch(nc.vector.reciprocal(lo, n))
            ch(nc.vector.scalar_tensor_tensor(out=fac, in0=ln, scalar=0.5, in1=lo, op0=ALU.mult, op1=ALU.mult))
            ch(nc.vector.tensor_scalar(lo, n2, 1.0 / 7, 1.0 / 5, ALU.mult, ALU.add))
            ch(nc.vector.tensor_tensor(lo, lo, n2, ALU.mult))
            ch(nc.vector.tensor_scalar(lo, lo, 1.0 / 3, None, ALU.add))
            ch(nc.vector.tensor_tensor(lo, lo, n2, ALU.mult))
            ch(nc.vector.scalar_tensor_tensor(out=lo, in0=lo, scalar=1.0, in1=fac, op0=ALU.add, op1=ALU.subtract))
            ch(nc.vector.scalar_tensor_tensor(out=lo, in0=n, scalar=0.05, in1=lo, op0=ALU.is_lt, op1=ALU.mult))
            ch(nc.vector.tensor_tensor(fac, fac, lo, ALU.add))
            v.sem_inc(S("norms"), 1)
            stage_end(v, 1)
            ln_tiles_dve(v, "l0", scaled=fac)
            v.wait_ge(S("gram"), 1)
            nc.vector.tensor_scalar(sc[:, 7, 0:KD], PS[:, 7, 0:KD], 1.0 / N, None, ALU.mult).then_inc(S("gram_sb"), 1)
            v.wait_ge(S("bn_cw"), 1)
            v.wait_ge(S("w_conv"), 48)
            for m in range(KD):
                ch(nc.vector.tensor_tensor(zz[:, m, :].rearrange("p (h o) -> p h o", h=2),
                                           wc[:, m, :].rearrange("p (h o) -> p h o", h=2),
                                           PS[:, 2 * m:2 * m + 2, 0:TD // 2], ALU.mult))
            v.sem_inc(S("bn_zz"), 1)
            v.wait_ge(S("bn_sums"), 1)
            ch(nc.vector.tensor_copy(bnm, PS[:, 7, 8:8 + KQ]))
            ch(nc.vector.tensor_tensor(bns, bnm, bnm, ALU.mult))
            ch(nc.vector.scalar_tensor_tensor(out=bnu, in0=PS[:, 7, 16:16 + KQ], scalar=1.0 / N, in1=bns,
                                              op0=ALU.mult, op1=ALU.subtract))
            fn.ask(nc.vector.tensor_scalar(bnu, bnu, 0.0, 1e-5, ALU.max, ALU.add))
            ch(nc.vector.reciprocal(bnu, bnu))
            ch(nc.vector.tensor_tensor(bns, bng, bnu, ALU.mult))
            ch(nc.vector.tensor_tensor(bnm, bnm, bns, ALU.mult))
            ch(nc.vector.tensor_tensor(bnt, bnb, bnm, ALU.subtract))
            v.wait_ge(S("w_mix"), 16 * 7)
            ch(nc.vector.tensor_tensor(bd, bd, dw_.rearrange("p (j a) -> p j a", a=1).to_broadcast((P, KQ, P)), ALU.mult))
            stage_end(v, 2)

            A2 = ATANH_MAX * ATANH_MAX

            def mixer_dve(t, q):
                if q == 1:
                    v.wait_ge(S("mix_qv"), t + 1)
                    v.wait_ge(S("mix_ft"), t + 1)
                    nc.vector.tensor_tensor(oo[:, 0:2, :], hh[:, 6:8, :], hh[:, 2:4, :], ALU.mult)
                    nc.vector.tensor_tensor(oo[:, 2:4, :], hh[:, 8:10, :], hh[:, 0:2, :], ALU.mult)\
                        .then_inc(S("mix_r"), 1)
                elif q == 2:
                    v.wait_ge(S("mix_sums"), t + 1)
                    nc.vector.tensor_scalar(ff[:, 0, :], PS[:, 3, D:D + P], 1.0 / A2, 1.0, ALU.mult, ALU.max)\
                        .then_inc(S("mix_f"), 1)
                    v.wait_ge(S("mix_eps"), t + 1)
                    nc.vector.tensor_tensor(rr, hh[:, 6:10, :], ff[:, 2:3, :].to_broadcast((P, 4, P)), ALU.add)\
                        .then_inc(S("mix_hh"), 1)
                    v.wait_ge(S("mix_hh"), t + 1 + 1)
                    nc.vector.reciprocal(rr, rr).then_inc(S("mix_r"), 1)
                    v.wait_ge(S("mix_r"), t * 3 + 2)
                    nc.vector.tensor_tensor(oo, rr, oo, ALU.mult).then_inc(S("mix_r"), 1)
                    v.wait_ge(S("mix_r"), t * 3 + 3)
                    nc.vector.tensor_tensor(oo, oo, PS[:, 4, :].rearrange("p (j n) -> p j n", n=P), ALU.mult)\
                        .then_inc(S("mix_o"), 1)

            nc.vector.sem_inc(S("mix_o"), 1)
            nc.vector.sem_inc(S("mix_hh"), 1)
            gather_dve_all(v, "g0", True, mixer_dve)
            stage_end(v, 3)
            a, b, c4, th, f = (sc[:, k, :] for k in range(5))
            fn.ask(nc.vector.tensor_scalar(a, a, TINY, None, ALU.max))
            ch(nc.vector.reciprocal(a, a))
            ch(nc.vector.reciprocal(b, b))
            ch(nc.vector.scalar_tensor_tensor(out=a, in0=a, scalar=ATANH_MAX, in1=b, op0=ALU.mult, op1=ALU.min))
            with v.Fori(0, NI) as i:
                for u in range(U):
                    t = i * U + u
                    nc.vector.scalar_tensor_tensor(out=tile_of(MB, t), in0=tile_of(MB, t), scalar=col(a, t), in1=bres_,
                                                   op0=ALU.mult, op1=ALU.add).then_inc(S("m0_ft"), 1)
            v.wait_ge(S("m0_sq"), T)
            fn.ask(nc.vector.tensor_scalar(b, b, TINY, None, ALU.max))
            ch(nc.vector.reciprocal(f, c4))
            ch(nc.vector.scalar_tensor_tensor(out=f, in0=th, scalar=MAXNORM, in1=f, op0=ALU.min, op1=ALU.mult))
            with v.Fori(0, NI) as i:
                for u in range(U):
                    t = i * U + u
                    ins = nc.vector.scalar_tensor_tensor(out=tile_of(X, t), in0=tile_of(MB, t), scalar=col(f, t),
                                                         in1=tile_of(X, t), op0=ALU.mult, op1=ALU.add)
                ch.enter(i, 1)
                ch(ins)
            ch.leave(NI)
            v.sem_inc(S("m0_done"), 1)
            v.wait_ge(S("w_g0"), 64)
            nc.vector.tensor_tensor(brow_[0:1, 2 * D:3 * D], brow_[0:1, 0:D], brow_[0:1, D:2 * D], ALU.add)\
                .then_inc(S("n0_brow"), 1)
            nc.vector.sem_inc(S("n0_ps"), U)
            with v.Fori(0, NI) as i:
                for u in range(U):
                    t = i * U + u
                    v.wait_ge(S("n0_mm"), t + 1)
                    nc.vector.scalar_tensor_tensor(out=ust[:, u, :, :], in0=XNT[:, :, ds(t * P, P)], scalar=1.0,
                                                   in1=ACC[:, 0:KD, ds(t * P, P)], op0=ALU.add, op1=ALU.mult)\
                        .then_inc(S("n0_u"), 1)
                for u in range(U):
                    t = i * U + u
                    v.wait_ge(S("n0_mm"), t + 1 + U)
                    nc.vector.tensor_copy(tile_of(MB, t), bank(u)).then_inc(S("n0_ps"), 1)
                    v.wait_ge(S("n0_ps"), t + 1 + U)
                    nc.vector.scalar_tensor_tensor(out=tile_of(MB, t), in0=tile_of(MB, t), scalar=0.2,
                                                   in1=tile_of(MB, t), op0=ALU.mult, op1=ALU.max).then_inc(S("n0_y"), 1)
            v.wait_ge(S("n0_ss"), T)
            fn.ask(nc.vector.tensor_scalar(b, b, 1e-24, None, ALU.max))
            ch(nc.vector.reciprocal(b, b))
            with v.Fori(0, NI) as i:
                for u in range(U):
                    t = i * U + u
                    ins = nc.vector.scalar_tensor_tensor(out=tile_of(X, t), in0=tile_of(MB, t), scalar=col(b, t),
                                                         in1=tile_of(X, t), op0=ALU.mult, op1=ALU.add)
                ch.enter(i, 1)
                ch(ins)
            ch.leave(NI)
            stage_end(v, 4)
            ln_stats(v, ch, fn, X, 1e-5)
            v.sem_inc(S("norms"), 1)
            ln_tiles_dve(v, "f0")
            v.wait_ge(S("f0_free"), T + U)
            ch(nc.vector.tensor_reduce(out=ysum, in_=XNT[:, :, 0:N], axis=AX.X, op=ALU.add))
            nc.vector.tensor_scalar(ysum, ysum, 1.0 / N, None, ALU.mult).then_inc(S("f0_ysum"), 1)
            v.wait_ge(S("route_mm"), 1)
            v.wait_ge(S("w_router"), 32)
            R = lambda k, n=E0: r0[0:1, k, 0:n]
            ch(nc.vector.tensor_tensor(R(3), R(0), PS[0:1, 5, 0:E0], ALU.add))
            for k in range(2):
                ch(nc.vector.tensor_reduce(out=R(5, 1), in_=R(3), axis=AX.X, op=ALU.max))
                fn.ask(nc.vector.tensor_scalar(R(1), R(3), R(5, 1), None, ALU.subtract))
                ch(nc.vector.tensor_reduce(out=R(5, 1), in_=R(2), axis=AX.X, op=ALU.add))
                ch(nc.vector.reciprocal(R(5, 1), R(5, 1)))
                ch(nc.vector.tensor_scalar(R(4), R(2), R(5, 1), None, ALU.mult))
                if k == 0:
                    ch(nc.vector.tensor_scalar(R(6), R(4), float(N), TINY, ALU.mult, ALU.max))
                    ch(nc.vector.reciprocal(R(6), R(6)))
                    ch(nc.vector.tensor_scalar(R(6), R(6), CAPACITY, 1.0, ALU.mult, ALU.min))
                    ch(nc.vector.tensor_tensor(R(3), R(4), R(6), ALU.mult))
            ch(nc.vector.max(out=R(7), in_=R(4)))
            ch(nc.vector.max_index(out=R(9).bitcast(U32), in_max=R(7), in_values=R(4)))
            fn.ask(nc.vector.tensor_tensor(R(1, 1), r0[0:1, 7, 1:2], r0[0:1, 7, 0:1], ALU.subtract))
            ch(nc.vector.tensor_scalar(R(6, 1), R(2, 1), 1.0, None, ALU.add))
            ch(nc.vector.reciprocal(r0[0:1, 8, 0:1], R(6, 1)))
            ch(nc.vector.tensor_tensor(r0[0:1, 8, 1:2], r0[0:1, 8, 0:1], R(2, 1), ALU.mult))
            v.sem_inc(S("routed"), 1)
            v.wait_ge(S("route_mm"), 2)
            ch(nc.vector.tensor_copy(wexp, PS[:, 3, 0:TOPK]))
            v.wait_ge(S("w_f0"), 16 * 8)
            for e in range(TOPK):
                ch(nc.vector.tensor_scalar(f0w2[:, e, :, :], f0w2[:, e, :, :], wexp[:, e:e + 1], None, ALU.mult))
            ch(nc.vector.tensor_scalar(f0row_[0:1, 2 * D:3 * D], f0row_[0:1, 0:D], wexp[0:1, 0:1], None, ALU.mult))
            ch(nc.vector.scalar_tensor_tensor(out=f0row_[0:1, 2 * D:3 * D], in0=f0row_[0:1, D:2 * D],
                                              scalar=wexp[0:1, 1:2], in1=f0row_[0:1, 2 * D:3 * D],
                                              op0=ALU.mult, op1=ALU.add))
            v.sem_inc(S("f0_w2s"), 1)
            nc.vector.sem_inc(S("f0_dfree"), U)
            with v.Fori(0, NCH) as c:
                for u in range(U):
                    t = c * U + u
                    v.wait_ge(S("f0_dn"), t + 1 + U)
                    nc.vector.tensor_tensor(tile_of(MB, t), tile_of(MB, t), slot(u), ALU.add)\
                        .then_inc(S("f0_dfree"), 1)
            v.wait_ge(S("f0_dfree"), T + U)
            ln_stats(v, ch, fn, MB, 1e-5)
            v.sem_inc(S("norms"), 1)
            v.wait_ge(S("w_f0n"), 32)
            epilogue_dve(v, ch, "f0z", gb0)
            stage_end(v, 5)
            nc.vector.tensor_scalar(rel[:, 0:G, :], rel0[:, :, :], 0.0, None, ALU.add)
            nc.vector.tensor_copy(base[:, :], base0[:, :])
            deg = ACC[:, KD, 0:NP]
            pos = mflat[:, 0:NP]
            ch(nc.vector.tensor_scalar(pos, deg, 0.0, None, ALU.is_gt))
            fn.ask(nc.vector.tensor_scalar(deg, deg, 1e-12, None, ALU.max))
            ch(nc.vector.reciprocal(deg, deg))
            ch(nc.vector.tensor_tensor(deg, deg, pos, ALU.mult))
            diag = v3(pos, P)
            ch(nc.vector.tensor_tensor(diag, v3(deg, P), ident[:, :].rearrange("p (a n) -> p a n", a=1)
                                       .to_broadcast((P, T, P)), ALU.mult))
            ch(nc.vector.tensor_reduce(out=dinvc[:, :], in_=diag, axis=AX.X, op=ALU.add))
            ln_stats(v, ch, fn, X, 1e-5)
            ch(nc.vector.tensor_tensor(sc[:, 0, :], rs[:, :], dinvc[:, :], ALU.mult))
            ch(nc.vector.tensor_tensor(sc[:, 1, :], nm[:, :], dinvc[:, :], ALU.mult))
            v.sem_inc(S("norms"), 1)
            ln_tiles_dve(v, "l1")
            stage_end(v, 6)

            c1 = Chain(v, S("dve_mix1"))

            def mixer1_dve(t, q):
                z8 = v3(zb, HC)
                if q == 0:
                    c1.enter(t, 3)
                    v.wait_ge(S("m1_mm"), t + 1)
                    c1(nc.vector.tensor_scalar(zb, tile_of(X, t), col(rs, t), col(nm, t), ALU.mult, ALU.add))
                    c1(nc.vector.tensor_reduce(out=hst[:, 0, :], in_=z8, axis=AX.X, op=ALU.add))
                    c1(nc.vector.tensor_scalar(hst[:, 0, :], hst[:, 0, :], 1.0 / HC, None, ALU.mult))
                    mean = hst[:, 0, :].rearrange("p (h a) -> p h a", a=1).to_broadcast((P, HEADS, HC))
                    nc.vector.tensor_tensor(z8, z8, mean, ALU.subtract).then_inc(S("m1_c"), 1)
                elif q == 1:
                    v.wait_ge(S("m1_sq"), t + 1)
                    nc.vector.tensor_reduce(out=hst[:, 1, :], in_=v3(csq, HC), axis=AX.X, op=ALU.add)\
                        .then_inc(S("m1_ss"), 1)
                elif q == 2:
                    v.wait_ge(S("m1_std"), t + 1)
                    nc.vector.tensor_scalar(hst[:, 2, :], hst[:, 2, :], 1e-5, None, ALU.add).then_inc(S("m1_r"), 1)
                    v.wait_ge(S("m1_r"), t * 3 + 1)
                    nc.vector.reciprocal(hst[:, 3, :], hst[:, 2, :]).then_inc(S("m1_r"), 1)
                    v.wait_ge(S("m1_r"), t * 3 + 2)
                    nc.vector.tensor_scalar(hst[:, 3, :], hst[:, 3, :], col(valid, t), None, ALU.mult)\
                        .then_inc(S("m1_r"), 1)
                    v.wait_ge(S("m1_r"), t * 3 + 3)
                    inv = hst[:, 3, :].rearrange("p (h a) -> p h a", a=1).to_broadcast((P, HEADS, HC))
                    nc.vector.tensor_tensor(z8, z8, inv, ALU.mult).then_inc(S("m1_z"), 1)

            gather_dve_all(v, "g1", False, mixer1_dve)
            stage_end(v, 7)
            v.wait_ge(S("w_m1"), 64)
            for m in range(KD):
                zcol = sc[:, 2, m:m + 1]
                ch(nc.vector.tensor_copy(zcol, PS[:, 2, m:m + 1]))
                ch(nc.vector.tensor_tensor(kt1[:, m, :], vwb[:, m, :], PS[:, 0, m * P:(m + 1) * P], ALU.mult))
                ch(nc.vector.scalar_tensor_tensor(out=kt1[:, m, :], in0=vbb[:, m, :], scalar=zcol, in1=kt1[:, m, :],
                                                  op0=ALU.mult, op1=ALU.add))
                ch(nc.vector.tensor_scalar(kt1[:, m, :], kt1[:, m, :], kwc_[:, m:m + 1], None, ALU.mult))
                ch(nc.vector.tensor_tensor(kt2[:, m, :], vwb[:, m, :], PS[:, 1, m * P:(m + 1) * P], ALU.mult))
                ch(nc.vector.scalar_tensor_tensor(out=kt2[:, m, :], in0=vbb[:, m, :], scalar=float(N), in1=kt2[:, m, :],
                                                  op0=ALU.mult, op1=ALU.add))
                ch(nc.vector.scalar_tensor_tensor(out=kv[:, m, :], in0=kt2[:, m, :], scalar=kwc_[:, 2 + m:3 + m],
                                                  in1=kt1[:, m, :], op0=ALU.mult, op1=ALU.add))
                ch(nc.vector.scalar_tensor_tensor(out=kv[:, m, :], in0=kv[:, m, :], scalar=1.0 / N, in1=blockones[:, :],
                                                  op0=ALU.mult, op1=ALU.mult))
                ch(nc.vector.tensor_tensor(kv[:, m, :], kv[:, m, :], ident[:, :], ALU.add))
            for k in range(KD):
                ch(nc.vector.tensor_tensor(ACC[:, k, 0:NP], ACC[:, k, 0:NP], deg, ALU.mult))
            v.sem_inc(S("agg"), 1)
            nc.vector.sem_inc(S("g1_dfree"), U)
            with v.Fori(0, NCH) as c:
                for u in range(U):
                    t = c * U + u
                    v.wait_ge(S("g1_dn"), t + 1)
                    nc.vector.tensor_copy(stg1[:, u, :, :], XNT[:, :, ds(t * P, P)]).then_inc(S("g1_stg"), 1)
                for u in range(U):
                    t = c * U + u
                    v.wait_ge(S("g1_dn"), t + 1 + U)
                    nc.vector.tensor_tensor(tile_of(X, t), tile_of(X, t), slot(u), ALU.add)\
                        .then_inc(S("g1_dfree"), 1)
            stage_end(v, 8)
            ln_stats(v, ch, fn, X, 1e-5)
            v.sem_inc(S("norms"), 1)

            def gate_dve(i, u, t):
                v.wait_ge(S("f1_free"), t + 1 + U)
                v.wait_ge(S("f1_gate"), t + 1)
                nc.vector.tensor_copy(stg2[:, u, :, :], XNT[:, :, ds(t * P, P)]).then_inc(S("f1_stg"), 1)
                v.wait_ge(S("f1_gate"), t + 1 + U)
                nc.vector.tensor_copy(tile_of(lg, t), PS[:, u, D:D + E1]).then_inc(S("f1_lg"), 1)

            ln_tiles_dve(v, "f1", extra=gate_dve)
            v.wait_ge(S("f1_lg"), T)
            for t in range(T):
                ins = nc.vector.max(out=top[:, t, :], in_=lg[:, t, :])
            ch(ins)
            for t in range(T):
                ins = nc.vector.max_index(out=topi[:, t, :], in_max=top[:, t, :], in_values=lg[:, t, :])
            ch(ins)
            p1, p2, i1, i2 = (sc[:, k, :] for k in (2, 3, 4, 5))
            fn.ask(nc.vector.tensor_tensor(sc[:, 0, :], top[:, :, 1], top[:, :, 0], ALU.subtract))
            ch(nc.vector.tensor_scalar(p1, sc[:, 1, :], 1.0, None, ALU.add))
            ch(nc.vector.reciprocal(p1, p1))
            ch(nc.vector.tensor_tensor(p2, p1, sc[:, 1, :], ALU.mult))
            ch(nc.vector.tensor_copy(i1, topi[:, :, 0]))
            ch(nc.vector.tensor_copy(i2, topi[:, :, 1]))

            def by_node(ap):
                return ap.rearrange("p (t a) -> p t a", a=1).to_broadcast((P, T, E1))

            def by_expert(ap, n=T):
                return ap.rearrange("p (a e) -> p a e", a=1).to_broadcast((P, n, E1))

            for o, i_k in ((o1, i1), (o2, i2)):
                ch(nc.vector.tensor_tensor(o, by_expert(iota[:, 0:E1]), by_node(i_k), ALU.is_equal))
                ch(nc.vector.tensor_tensor(o, o, by_node(valid[:, :]), ALU.mult))
            nc.vector.tensor_tensor(cnt_, o1_, o2_, ALU.add).then_inc(S("f1_cnt"), 1)
            v.wait_ge(S("f1_rank"), 1)
            ch(nc.vector.tensor_copy(rk_, PS[:, 5, 0:T * E1]))
            ch(nc.vector.tensor_copy(cnt_, PS[:, 6, 0:T * E1]))
            for e in range(E1):
                ins = nc.vector.tensor_tensor_scan(out=lg[:, :, e], data0=ones[:, 0:T], data1=cnt[:, :, e],
                                                   initial=0.0, op0=ALU.mult, op1=ALU.add)
            ch(ins)
            ch(nc.vector.tensor_scalar(eji_[:, 0:E1].bitcast(I32), lg[:, T - 1, :], 1.0 / P, 0.498, ALU.mult, ALU.add))
            ch(nc.vector.tensor_copy(nt_, eji_[:, 0:E1].bitcast(I32)))
            ch(nc.vector.tensor_tensor_scan(out=te_, data0=ones[:, 0:E1], data1=nt_, initial=0.0,
                                            op0=ALU.mult, op1=ALU.add))
            ch(nc.vector.tensor_tensor(ts_, te_, nt_, ALU.subtract))
            ch(nc.vector.tensor_scalar(ts_, ts_, float(P), None, ALU.mult))
            ch(nc.vector.tensor_tensor(rk_, rk_, lg_, ALU.add))
            ch(nc.vector.tensor_tensor(rk_, rk_, cnt_, ALU.subtract))
            ch(nc.vector.tensor_tensor(rk, rk, by_expert(ts_), ALU.add))
            for k, o in enumerate((o1, o2)):
                slot_f = sc[:, 4 + k, :]
                ch(nc.vector.tensor_tensor(o, o, rk, ALU.mult))
                ch(nc.vector.tensor_reduce(out=slot_f, in_=o, axis=AX.X, op=ALU.add))
                ch(nc.vector.tensor_scalar(sc[:, 6, :], valid[:, :], -1.0, 1.0, ALU.mult, ALU.add))
                ch(nc.vector.tensor_scalar(sc[:, 7, 0:1], pcol[:, 0:1], float(SLOTS + k * P), None, ALU.add))
                ch(nc.vector.scalar_tensor_tensor(out=slot_f, in0=sc[:, 6, :], scalar=sc[:, 7, 0:1], in1=slot_f,
                                                  op0=ALU.mult, op1=ALU.add))
            v.wait_ge(S("w_gate"), 48)
            stage_end(v, 9)
            for k in range(TOPK):
                ch(nc.vector.tensor_copy(slots[:, k, :], sc[:, 4 + k, :]))
            v.sem_inc(S("f1_slots"), 1)
            jj = iota[:, 0:NTILE + 2].rearrange("p (j a) -> p j a", a=1).to_broadcast((P, NTILE + 2, E1))
            ch(nc.vector.tensor_tensor(wide, by_expert(te_, NTILE + 2), jj, ALU.is_le))
            ch(nc.vector.tensor_reduce(out=ej_[:, 0:NTILE + 2], in_=wide, axis=AX.X, op=ALU.add))
            ch(nc.vector.tensor_scalar(ej_[:, 0:NTILE + 2], ej_[:, 0:NTILE + 2], float(E1 - 1), None, ALU.min))
            ch(nc.vector.tensor_copy(eji[:, 0:NTILE + 2], ej_[:, 0:NTILE + 2]))
            ch(nc.vector.memset(b3[0:96, :], 0.0))
            for k in range(3):
                ch(nc.vector.tensor_copy(b3[32 * k:32 * k + E1, :], b2f[0:E1, :]))
                if k < 2:
                    ch(nc.vector.tensor_copy(b2g[0:E1, :], b3[32 * k:32 * k + E1, :]))
                    ch(nc.vector.tensor_tensor(b2f[0:E1, :], b2f[0:E1, :], b2g[0:E1, :], ALU.subtract))
            ch(nc.vector.tensor_scalar(pcol[:, 1:2], pcol[:, 0:1], 32.0, -32.0, ALU.is_ge, ALU.mult))
            ch(nc.vector.tensor_tensor(sc[:, 7, 0:1], pcol[:, 0:1], pcol[:, 1:2], ALU.add))
            ch(nc.vector.tensor_scalar(pcol[:, 1:2], pcol[:, 0:1], 64.0, -32.0, ALU.is_ge, ALU.mult))
            ch(nc.vector.tensor_tensor(pcol[:, 1:2], pcol[:, 1:2], sc[:, 7, 0:1], ALU.add))
            v.sem_inc(S("f1_b3"), 1)
            v.wait_ge(S("f1_scattered"), 1)
            v.wait_ge(S("w_f1"), 48)
            v.wait_ge(S("w_b1"), 16)

            def expert_weights(n, k):
                e = v.value_load(eji[0:1, ds(n, 1)], min_val=0, max_val=E1 - 1)
                nc.vector.tensor_copy(b1s[:, k, :], tile_of(b1t, e))
                nc.vector.tensor_copy(w1s_[:, k * KD * F1:(k + 1) * KD * F1],
                                      e_w1[:, ds(e, 1), :, :].rearrange("p a k f -> p (a k f)")).then_inc(S("f1_w"), 1)

            def pick_bias(n, k):
                nc.vector.tensor_scalar(sel[0:96, k, :], ej_[0:96, ds(n, 1)].to_broadcast((96, P)),
                                        pcol[0:96, 1:2], None, ALU.is_equal).then_inc(S("f1_sel"), 1)

            for k in range(2):
                expert_weights(k, k)
                pick_bias(k, k)
            nc.vector.sem_inc(S("f1_ys"), 2)
            with v.Fori(0, PAIRS) as i:
                for k in range(2):
                    n = i * 2 + k
                    v.wait_ge(S("f1_h"), n + 1)
                    v.wait_ge(S("f1_ht"), n + 1)
                    expert_weights(n + 2, k)
                for k in range(2):
                    n = i * 2 + k
                    v.wait_ge(S("f1_y"), n + 1 + 2)
                    v.wait_ge(S("f1_ys_free"), n + 1)
                    nc.vector.tensor_copy(ys[:, k, :], PS[:, 6 + k, 0:D]).then_inc(S("f1_ys"), 1)
                    pick_bias(n + 2, k)
            stage_end(v, 10)
            nc.vector.sem_inc(S("f1_cmb"), U)
            with v.Fori(0, NI) as i:
                for k in range(TOPK):
                    for u in range(U):
                        t = i * U + u
                        if k == 0:
                            v.wait_ge(S(f"f1_rows{u}"), (NI + i + 1) * 16 * TOPK)
                        ins = nc.vector.scalar_tensor_tensor(out=tile_of(MB, t), in0=cmb[:, u, k, :],
                                                             scalar=col((p1, p2)[k], t), in1=tile_of(MB, t),
                                                             op0=ALU.mult, op1=ALU.add)
                        ins.then_inc(S("f1_cmb" if k else "f1_cmb0"), 1)
                    if k == 0:
                        v.wait_ge(S("f1_cmb0"), i * U + U)
            v.wait_ge(S("f1_cmb"), T + U)
            ln_stats(v, ch, fn, MB, 1e-5)
            v.sem_inc(S("norms"), 1)
            v.wait_ge(S("w_f1n"), 32)
            epilogue_dve(v, ch, "f1z", gb1)


def kernel(**inputs):
    import concourse.bacc as bacc
    from concourse.bass_utils import run_bass_kernel_spmd

    a = {k: np.asarray(v) for k, v in inputs.items()}
    channels = np.arange(TD).reshape(HEADS, 3, HC).transpose(1, 0, 2).reshape(-1)
    pointwise = a["L0_mix_w_pw"][channels, :, 0].reshape(TD // HC, HC, HC).transpose(0, 2, 1).reshape(TD, HC)

    def by_partition(v):
        return np.swapaxes(v.reshape(*v.shape[:-1], -1, P), -1, -2)

    laid = {
        "x": a["x"], "src": a["src"], "dst": a["dst"], "edge_weight": a["edge_weight"],
        "g0_w1": a["L0_gnn_W1"].T, "g0_b1": a["L0_gnn_b1"], "g0_w2": a["L0_gnn_W2"].T, "g0_b2": a["L0_gnn_b2"],
        "wc": a["L0_mix_w_qkv"][channels, :, 2].T,
        "bn_gamma": by_partition(a["L0_mix_bn_gamma"][channels]), "bn_beta": by_partition(a["L0_mix_bn_beta"][channels]),
        "w_dw": by_partition(a["L0_mix_w_dw"][channels, 0, 2]), "w_pw": pointwise,
        "w_res": a["L0_mix_w_res"][:, :, 0].T, "b_res": a["L0_mix_b_res"],
        "f0_wr": a["L0_ffn_Wr"], "f0_br": a["L0_ffn_br"], "f0_w1": a["L0_ffn_W1"], "f0_b1": by_partition(a["L0_ffn_b1"]),
        "f0_w2": a["L0_ffn_W2"], "f0_b2": a["L0_ffn_b2"], "f0_gamma": a["L0_ffn_gamma"], "f0_beta": a["L0_ffn_beta"],
        "g1_w1": a["L1_gnn_W1"], "g1_b1": by_partition(a["L1_gnn_b1"]), "g1_w2": a["L1_gnn_W2"], "g1_b2": a["L1_gnn_b2"],
        "m1_kw": by_partition(a["L1_mix_kln_weight"].reshape(-1)), "m1_kb": by_partition(a["L1_mix_kln_bias"].reshape(-1)),
        "m1_vw": a["L1_mix_vln_weight"].reshape(-1), "m1_vb": a["L1_mix_vln_bias"].reshape(-1),
        "f1_wg": a["L1_ffn_gate_w"], "f1_bg": a["L1_ffn_gate_b"], "f1_w1": a["L1_ffn_w1"], "f1_b1": by_partition(a["L1_ffn_b1"]),
        "f1_w2": a["L1_ffn_w2"], "f1_b2": a["L1_ffn_b2"], "f1_gamma": a["L1_ffn_gamma"], "f1_beta": a["L1_ffn_beta"],
    }
    laid = {k: np.ascontiguousarray(v) for k, v in laid.items()}
    nc = bacc.Bacc("TRN2", target_bir_lowering=False, num_devices=1)
    dram = {k: nc.dram_tensor(f"in_{k}", v.shape, mybir.dt.from_np(v.dtype), kind="ExternalInput").ap()
            for k, v in laid.items()}
    out = nc.dram_tensor("out_x", (N, D), F32, kind="ExternalOutput").ap()
    bass_gps_kernel(nc, dram, out)
    got = run_bass_kernel_spmd(nc, [{f"in_{k}": v for k, v in laid.items()}], core_ids=[0])
    return got.results[0]["out_x"]
```

```python
import math
from contextlib import ExitStack

import numpy as np
import concourse.bass as bass
from concourse import mybir

F32 = mybir.dt.float32
I32 = mybir.dt.int32
U32 = mybir.dt.uint32
BF16 = mybir.dt.bfloat16
ALU = mybir.AluOpType
ACT = mybir.ActivationFunctionType
AX = mybir.AxisListType
ds = bass.ds

P = 128
N = 3125
D = 256
KD = D // P
E = 50000
U = 5
T = -(-N // P)
NP = T * P
NI = T // U
TAIL = N - (T - 1) * P
assert T % U == 0

C = 4
GE = C * P
B = 4
G = -(-E // (GE * B)) * B
GB = G // B
W = 80
MAXR = -(-N // W)
NA = NP + P
BIG = 16384.0

LN = ("l0", "f0", "l1", "f1")
COPIES = ("l0", "f0", "f1")
COPIED = 2
CH = U * P
HALF = CH // 2
NCH = NP // CH
TD = 3 * D
KQ = TD // P
HID1 = 1024
F0, E0 = 512, 8
F1, E1 = 512, 16
TOPK = 2
TILES1 = (TOPK * N + E1 * (P - 1)) // P
PAIRS = -(-TILES1 // 2)
SLOTS = 2 * PAIRS * P
HC = 32
HEADS = D // HC
CAPACITY = float(math.ceil(N * 1.25 / E0))

MAXNORM = float(np.float32(1.0 - 1e-5))
ATANH_MAX = math.atanh(MAXNORM)
TINY = 1e-30


class Asked:

    def __init__(self, engine, asked, answered):
        self.engine, self.asked, self.answered, self.n = engine, asked, answered, 0

    def ask(self, instruction):
        self.n += 1
        instruction.then_inc(self.asked, 1)
        self.engine.wait_ge(self.answered, self.n)

    def take(self):
        self.n += 1
        self.engine.wait_ge(self.asked, self.n)

    def give(self, instruction):
        instruction.then_inc(self.answered, 1)


class Chain:

    def __init__(self, engine, semaphore):
        self.engine, self.semaphore = engine, semaphore
        self.before, self.n, self.base = 0, 0, None

    def __call__(self, instruction):
        instruction.then_inc(self.semaphore, 1)
        self.n += 1
        at = self.before + self.n
        self.engine.wait_ge(self.semaphore, at if self.base is None else self.base + at)

    def enter(self, i, per):
        self.before, self.n, self.per, self.base = self.before + self.n, 0, per, i * per

    def leave(self, times):
        assert self.n == self.per, (self.n, self.per)
        self.before, self.n, self.base = self.before + self.per * times, 0, None


def bass_gps_kernel(nc, A, out):
    with ExitStack() as ctx:
        def sb(name, shape, dt=F32):
            return ctx.enter_context(nc.sbuf_tensor(name, shape, dt))

        semaphores = {}

        def S(name):
            if name not in semaphores:
                semaphores[name] = ctx.enter_context(nc.semaphore(name))
            return semaphores[name]

        X = sb("X", [P, T, D])
        big = sb("big", [P, KD * NP + (KD + 1) * NA])
        XNT = big[:, 0:KD * NP].rearrange("p (k n) -> p k n", k=KD)
        ACC = big[:, KD * NP:KD * NP + (KD + 1) * NA].rearrange("p (k n) -> p k n", k=KD + 1)
        MB = sb("MB", [P, T, D])
        ident = sb("ident", [P, P])
        iota = sb("iota", [P, W])
        ones = sb("ones", [P, P])
        zeros = sb("zeros", [P, P])
        ones16 = sb("ones16", [P, P], BF16)
        blockones = sb("blockones", [P, P])
        before = sb("before", [P, P])
        pcol = sb("pcol", [P, 2])
        tables = sb("tables", [P, 4, (G + 1) * C])

        def table(k):
            return tables[:, k, :].rearrange("p (g c) -> p g c", c=C)

        idx = table(0).bitcast(I32)
        rel0 = table(1)[:, 0:G, :]
        rel = table(2)
        ewt = table(3)
        base0 = sb("base0", [1, G], I32)
        base = sb("base", [1, G], I32)
        rounds = sb("rounds", [1, 1], I32)
        farthest = sb("farthest", [1, 1])
        idxs = sb("idxs", [P, U, C], I32)
        st = sb("st", [P, T, 6])
        mv = sb("mv", [P, T, 2])
        st5 = sb("st5", [P, U, 6])
        mv5 = sb("mv5", [P, U, 2])
        rs5 = sb("rs5", [P, U])
        nm5 = sb("nm5", [P, U])
        rs = sb("rs", [P, T])
        nm = sb("nm", [P, T])
        sc = sb("sc", [P, 8, T])
        valid = sb("valid", [P, T])
        dinvc = sb("dinvc", [P, T])
        NWORK = 20640
        work = sb("work", [P, NWORK])
        PS = ctx.enter_context(nc.psum_tensor("PS", [P, 8, 512], F32))
        xn_dram = nc.dram_tensor("xn_table", (NP, D), F32).ap()
        xe_dram = nc.dram_tensor("expert_rows", (SLOTS + TOPK * P, D), F32).ap()
        xs_dram = nc.dram_tensor("xs_table", (NP, D), F32).ap()

        def areas(*sizes, start=0):
            at, found = start, []
            for n in sizes:
                found.append(work[:, at:at + n])
                at += n
            assert at <= NWORK, at
            return found

        def v3(ap, b):
            return ap.rearrange("p (a b) -> p a b", b=b)

        gflat, oh_, oh16_ = areas(B * C * D, 2 * C * W, C * W)
        gath = gflat.rearrange("p (s c d) -> p s c d", s=B, c=C)
        oh = oh_.rearrange("p (s c w) -> p s c w", s=2, c=C)
        oh16 = oh16_.bitcast(BF16).rearrange("p (s c w) -> p s c w", s=2, c=C)
        GATHER = B * C * D + 3 * C * W
        xb = v3(gflat[:, 0:U * D], D)
        hb = v3(gflat[:, U * D:2 * U * D], D)
        mflat = MB[:, :, :].rearrange("p t d -> p (t d)")

        srow = mflat[0:G, 0:GE].bitcast(I32)
        drow = mflat[0:G, GE:2 * GE].bitcast(I32)
        wrow = mflat[0:G, 2 * GE:3 * GE]
        sf, df, rf, mf = (mflat[0:G, k * GE:(k + 1) * GE] for k in range(3, 7))
        gb2 = mflat[0:G, 7 * GE:7 * GE + 4]

        H0T_, wc_, bd_, wres_, hh_, ks_, hsq_, ssq_, osq_, oo_, ff_, dw_, bn_, bres_ = areas(
            KD * (NP + P), KD * TD, KQ * P, 4 * D, 10 * P, 2 * P, KQ * P, KQ * P, 4 * P, 4 * P, 3 * P, KQ,
            6 * KQ, D, start=GATHER)
        H0T, wc, bd, wres = v3(H0T_, NP + P), v3(wc_, TD), v3(bd_, P), v3(wres_, D)
        hh = v3(hh_, P)
        ks, hsq, ssq, osq, oo, ff, bn = (
            v3(ks_, P), v3(hsq_, P), v3(ssq_, P), v3(osq_, P), v3(oo_, P), v3(ff_, P), v3(bn_, KQ))
        rr = v3(ssq_[:, 0:4 * P], P)
        bng, bnb, bns, bnt, bnu, bnm = (bn[:, i, :] for i in range(6))
        gram = v3(hh_[:, 0:KD * D], D)
        zz, = areas(KD * TD, start=GATHER + KD * (NP + P) + KD * TD + KQ * P + 4 * D + 10 * P)
        zz = v3(zz, TD)
        w1t_, w2t_, stg_, ust_, brow_ = areas(KD * D, KD * D, U * D, U * D, 3 * D, start=GATHER + T * D)
        Y = v3(areas(T * D, start=GATHER)[0], D)
        w1t, w2t = v3(w1t_, D), v3(w2t_, D)
        stg = stg_.rearrange("p (u k n) -> p u k n", u=U, k=KD)
        ust = ust_.rearrange("p (u k n) -> p u k n", u=U, k=KD)
        f0w1_, f0w2_, f0h_, f0b1_, f0row_, gb0_, f0r_ = areas(
            TOPK * KD * F0, TOPK * 4 * D, TOPK * 4 * CH, TOPK * 4, 3 * D, 2 * D, 200, start=GATHER)
        f0w1 = f0w1_.rearrange("p (e k f) -> p e k f", e=TOPK, k=KD)
        f0w2 = f0w2_.rearrange("p (e k f) -> p e k f", e=TOPK, k=4)
        f0h = f0h_.rearrange("p (e k f) -> p e k f", e=TOPK, k=4)
        gb0 = v3(gb0_, D)
        wr = v3(f0r_[:, 0:KD * E0], E0)
        r0 = v3(f0r_[:, KD * E0:KD * E0 + 10 * E0], E0)
        ysum = f0r_[:, 120:122]
        wexp = f0r_[:, 122:124]
        g1w1_, g1w2_, g1h_, g1b1_, g1row_, kvp_, vwb_, kwc_, z_, = areas(
            KD * HID1, 8 * D, 8 * CH, 8, D, 4 * D, 2 * D, 8, 4 * D, start=GATHER)
        g1w1, g1w2, g1h = v3(g1w1_, HID1), v3(g1w2_, D), v3(g1h_, CH)
        zb, csq = z_[:, 0:D], z_[:, D:2 * D]
        hst = v3(z_[:, 2 * D:2 * D + 4 * HEADS], HEADS)
        kv = v3(kvp_[:, 0:D], P)
        kt1, kt2 = v3(kvp_[:, D:2 * D], P), v3(kvp_[:, 2 * D:3 * D], P)
        vwb, vbb = v3(vwb_[:, 0:D], P), v3(vwb_[:, D:2 * D], P)
        stg1 = gflat[:, 0:U * D].rearrange("p (u k n) -> p u k n", u=U, k=KD)
        stg2 = gflat[:, 2 * U * D:3 * U * D].rearrange("p (u k n) -> p u k n", u=U, k=KD)
        e_w1 = big[:, 0:E1 * KD * F1].rearrange("p (e k f) -> p e k f", e=E1, k=KD)
        e_w2_, = areas(E1 * 4 * D)
        e_w2 = e_w2_.rearrange("p (e k f) -> p e k f", e=E1, k=4)
        FREE1 = E1 * 4 * D
        EARLY1, EARLY2 = -(-KD * NP // (KD * F1)), -(-(GATHER + (KD + 1) * E1) // (4 * D))
        gate_, grow_ = areas(KD * E1, E1, start=GATHER)
        gate = v3(gate_, E1)
        lg_, o1_, o2_, cnt_, rk_, top_, topi_ = areas(*[T * E1] * 5, T * 8, T * 8, start=FREE1)
        lg, o1, o2, cnt, rk = (v3(a, E1) for a in (lg_, o1_, o2_, cnt_, rk_))
        top, topi = v3(top_, 8), v3(topi_, 8).bitcast(U32)
        NTILE = 2 * PAIRS
        xs_, w1s_, ht_, b3_, sel_, eji_, slots_, b1s_, b1t_ = areas(
            2 * D, 2 * KD * F1, 2 * 4 * P, D // 2, P, NTILE + 2, 2 * T, 8, 4 * E1, start=FREE1)
        tflat = tables[:, :, :].rearrange("p a b -> p (a b)")
        b2f, b2g = tflat[:, 0:D], tflat[:, D:2 * D]
        ej_ = tflat[:, 2 * D:2 * D + NTILE + 2]
        xt_, ys_ = tflat[:, 0:2 * D], tflat[:, 2 * D + NTILE + 2:4 * D + NTILE + 2]
        xs, xt, ys = v3(xs_, D), xt_.rearrange("p (s k n) -> p s k n", s=2, k=KD), v3(ys_, D)
        w1s, ht = w1s_.rearrange("p (s k f) -> p s k f", s=2, k=KD), ht_.rearrange("p (s m n) -> p s m n", s=2, m=4)
        b1s, b1t = v3(b1s_, 4), v3(b1t_, 4)
        b3 = b3_.bitcast(BF16)
        sel = v3(sel_.bitcast(BF16), P)
        eji = eji_.bitcast(I32)
        slots = v3(slots_.bitcast(I32), T)
        wide = v3(w1s_[:, 0:(NTILE + 2) * E1], E1)
        nt_, ts_, te_ = (st[:, :, :].rearrange("p a b -> p (a b)")[:, k * E1:(k + 1) * E1] for k in range(3))
        cmb_, gb1_ = areas(U * TOPK * D, 2 * D)
        cmb = cmb_.rearrange("p (u k d) -> p u k d", u=U, k=TOPK)
        gb1 = v3(gb1_, D)

        block = ctx.enter_context(nc.Block())

        def stage_end(eng, k):
            eng.drain().then_inc(S("stages"), 1)
            eng.wait_ge(S("stages"), 5 * k)

        def col(ap, t):
            return ap[:, ds(t, 1)]

        def tile_of(ap, t):
            return ap[:, ds(t, 1), :].rearrange("p a b -> p (a b)")

        def row(ap):
            return ap.rearrange("(a n) -> a n", a=1)

        full_groups, last_group = E // GE, E % GE

        def tiles_stats(src, i):
            nc.vector.sem_inc(S("dve_seen"), 1)
            for u in range(U):
                ins = nc.vector.bn_stats(tile_of(st, i * U + u), tile_of(src, i * U + u))
            return ins

        def ln_stats(v, ch, root, eps):
            for t in range(T):
                ins = nc.vector.bn_aggr(mv[:, t, :], st[:, t, :])
            ch(ins)
            root.ask(nc.vector.tensor_scalar(rs[:, :], mv[:, :, 1], eps, None, ALU.add))
            ch(nc.vector.reciprocal(rs[:, :], rs[:, :]))
            ch(nc.vector.scalar_tensor_tensor(out=nm[:, :], in0=mv[:, :, 0], scalar=-1.0, in1=rs[:, :],
                                              op0=ALU.mult, op1=ALU.mult))

        def root_of(fn, ap, scale=1.0):
            fn.take()
            fn.give(nc.scalar.activation(ap, ap, ACT.Sqrt, scale=scale))

        def ln_tiles_dve(v, s, scaled=None, extra=None):
            with v.Fori(0, NI) as i:
                for u in range(U):
                    t = i * U + u
                    v.wait_ge(S("ln_tp"), LN.index(s) * (T + U) + t + 1)
                    if s != "l1" and u < COPIED:
                        v.wait_ge(S("ln_mb"), COPIES.index(s) * (NI + 1) * COPIED + i * COPIED + u + 1)
                    nc.vector.tensor_scalar(xb[:, u, :], tile_of(X, t), col(rs, t), col(nm, t),
                                            ALU.mult, ALU.add).then_inc(S("ln_xb"), 1)
                    if scaled is not None:
                        v.wait_ge(S("ln_xb"), LN.index(s) * T + t + 1)
                        nc.vector.tensor_scalar(hb[:, u, :], xb[:, u, :], col(scaled, t), None,
                                                ALU.mult).then_inc(S(s + "_hb"), 1)
                if extra is not None:
                    extra(i)

        def ln_tiles_pe(pe, s, scaled=False, after=None):
            if s == "f0":
                nc.tensor.matmul(PS[:, 7, 0:KD], zeros[:, :], ident[:, 0:KD], start=True, stop=False, skip_group_check=True)
            nc.tensor.sem_inc(S("ln_tp"), U)
            with pe.Fori(0, NI) as i:
                for u in range(U):
                    t = i * U + u
                    pe.wait_ge(S("ln_xb"), LN.index(s) * T + t + 1)
                    pe.wait_ge(S("ln_free"), LN.index(s) * (T + U) + t + 1)
                    for k in range(KD):
                        ins = nc.tensor.transpose(PS[:, u, k * P:(k + 1) * P], xb[:, u, k * P:(k + 1) * P], ident[:, :])
                    if s == "f0":
                        for m in range(KD):
                            ins = nc.tensor.matmul(PS[:, 7, m:m + 1], xb[:, u, m * P:(m + 1) * P], ones[:, 0:1],
                                                   start=False, stop=False, skip_group_check=True)
                    if scaled:
                        pe.wait_ge(S(s + "_hb"), t + 1)
                        for k in range(KD):
                            ins = nc.tensor.transpose(PS[:, u, D + k * P:D + (k + 1) * P],
                                                      hb[:, u, k * P:(k + 1) * P], ident[:, :])
                        for m in range(KD):
                            nc.tensor.matmul(PS[:, 5 + m, 0:D], hb[:, u, m * P:(m + 1) * P], hb[:, u, :],
                                             start=False, stop=False, skip_group_check=True)
                            ins = nc.tensor.matmul(PS[:, 7, m:m + 1], hb[:, u, m * P:(m + 1) * P], ones[:, 0:1],
                                                   start=False, stop=False, skip_group_check=True)
                    ins.then_inc(S("ln_tp"), 1)
                if after is not None:
                    for u in range(U):
                        after(i, u, i * U + u)

        def ln_tiles_pool(pool, s):
            nc.gpsimd.sem_inc(S("ln_mb"), COPIED)
            with pool.Fori(0, NI) as i:
                for u in range(COPIED):
                    pool.wait_ge(S("ln_xb"), LN.index(s) * T + i * U + u + 1)
                    pool.sem_inc(S("idxs_seen"), 1)
                    nc.gpsimd.tensor_copy(tile_of(MB, i * U + u), xb[:, u, :]).then_inc(S("ln_mb"), 1)

        def ln_tiles_act(act, s, scaled=False):
            nc.scalar.sem_inc(S("ln_free"), U)
            act.wait_ge(S("norms"), ("l0", "f0", "l1", "f1").index(s) + 1)
            by, plus = (sc[:, 0, :], sc[:, 1, :]) if s == "l1" else (rs, nm)
            with act.Fori(0, NI) as i:
                for u in range(0 if s == "l1" else COPIED, U):
                    t = i * U + u
                    nc.scalar.activation(tile_of(MB, t), tile_of(X, t), ACT.Identity, bias=col(plus, t),
                                         scale=col(by, t)).then_inc(S("ln_mb_act"), 1)
                for u in range(U):
                    t = i * U + u
                    act.wait_ge(S("ln_tp"), LN.index(s) * (T + U) + t + 1 + U)
                    ins = nc.scalar.activation(XNT[:, :, ds(t * P, P)], v3(PS[:, u, 0:D], P), ACT.Copy)
                    if scaled:
                        ins = nc.scalar.activation(H0T[:, :, ds(t * P, P)], v3(PS[:, u, D:2 * D], P), ACT.Copy)
                    ins.then_inc(S("ln_free"), 1)

        def table_store(sp, s, dram):
            with sp.Fori(0, NI) as i:
                if s == "l1":
                    sp.wait_ge(S("ln_mb_act"), 2 * NI * (U - COPIED) + i * U + U)
                else:
                    sp.wait_ge(S("ln_mb_act"), (i + 1) * (U - COPIED))
                    sp.wait_ge(S("ln_mb"), COPIES.index(s) * (NI + 1) * COPIED + i * COPIED + 2 * COPIED)
                sp.dma_start(dram.rearrange("(t p) d -> p t d", p=P)[:, ds(i * U, U), :],
                             MB[:, ds(i * U, U), :]).then_inc(S(s + "_table"), 16)
            sp.wait_ge(S(s + "_table"), 16 * NI)

        def gather_pool(pool, s, dram, r, b):
            for q in range(B):
                n = r * G + b * B + q
                nxt = (q + 1) % B
                pool.wait_ge(S(f"{s}_rows{nxt}"), (r * GB + b + (q + 1) // B) * (16 * C))
                nc.gpsimd.tensor_copy(idxs[:, nxt, :], tile_of(idx, b * B + q + 1)).then_inc(S(s + "_idxs"), 1)
                pool.wait_ge(S(s + "_sum"), n + 1)
                pool.wait_ge(S(s + "_idxs"), n + r + 1)
                nc.gpsimd.sem_inc(S("idxs_seen"), 1)
                for j in range(C):
                    nc.gpsimd.indirect_dma_start(
                        out=gath[:, q, j, :], out_offset=None, in_=dram,
                        in_offset=bass.IndirectOffsetOnAxis(ap=idxs[:, q, j:j + 1], axis=0),
                    ).then_inc(S(f"{s}_rows{q}"), 16)

        def first_indices(pool, s, r):
            if not isinstance(r, int):
                pool.wait_ge(S(s + "_idxs"), r * (G + 1))
                pool.sem_inc(S("idxs_seen"), 1)
            nc.gpsimd.tensor_copy(idxs[:, 0, :], tile_of(idx, 0)).then_inc(S(s + "_idxs"), 1)

        def gather_pe(pe, s, r, b, q, degrees):
            n = r * G + b * B + q
            h = q % 2
            pe.wait_ge(S(s + "_oh"), r * (G + 1) + b * B + q + 1)
            pe.wait_ge(S(f"{s}_rows{q}"), (r * GB + b + 1) * (16 * C))
            pe.wait_ge(S(s + "_added"), n + 1)
            for k in range(KD):
                for j in range(C):
                    ins = nc.tensor.matmul(PS[:, 5 + h, k * W:(k + 1) * W], gath[:, q, j, k * P:(k + 1) * P],
                                           oh[:, h, j, :], start=j == 0, stop=j == C - 1)
            if degrees:
                for j in range(C):
                    ins = nc.tensor.matmul(PS[:, 5 + h, KD * W:(KD + 1) * W], ones16[:, :], oh16[:, h, j, :],
                                           start=j == 0, stop=j == C - 1)
            ins.then_inc(S(s + "_sum"), 1)

        def windows(s, g, h, weighted):
            for j in range(C):
                at = rel[:, ds(g, 1), j:j + 1].rearrange("p a c -> p (a c)")
                wt_j = ewt[:, ds(g, 1), j:j + 1].rearrange("p a c -> p (a c)")
                if weighted:
                    nc.vector.tensor_scalar(oh16[:, h, j, :], iota[:, :], at, None, ALU.is_equal)
                    ins = nc.vector.tensor_scalar(oh[:, h, j, :], iota[:, :], at, wt_j, ALU.is_equal, ALU.mult)
                else:
                    ins = nc.vector.tensor_scalar(oh[:, h, j, :], iota[:, :], at, None, ALU.is_equal)
            ins.then_inc(S(s + "_oh"), 1)

        def gather_dve(v, s, r, b, q, weighted, step=None):
            g = b * B + q
            planes = KD + 1 if weighted else KD
            windows(s, g + 1, (q + 1) % 2, weighted)
            if step:
                step(b, q)
            v.wait_ge(S(s + "_sum"), r * G + g + 1 + B)
            start = v.value_load(base[0:1, ds(g, 1)], min_val=0, max_val=N)
            into = ACC[:, 0:planes, ds(start, W)]
            nc.vector.tensor_tensor(into, into, v3(PS[:, 5 + q % 2, 0:planes * W], W), ALU.add)\
                .then_inc(S(s + "_added"), 1)
            v.wait_ge(S(s + "_added"), r * G + g + 1 + 2)

        def next_round(v, s, r):
            nc.vector.tensor_scalar(rel[:, 0:G, :], rel[:, 0:G, :], -float(W), None, ALU.add)\
                .then_inc(S(s + "_round"), 1)
            nc.vector.tensor_scalar(base[:, :], base[:, :], float(W), float(N), ALU.add, ALU.min)\
                .then_inc(S(s + "_round"), 1)
            v.wait_ge(S(s + "_round"), r * 2 + 2)

        def gather_pool_all(pool, s, dram):
            first_indices(pool, s, 0)
            with pool.Fori(0, GB) as b:
                gather_pool(pool, s, dram, 0, b)
            more = pool.value_load(rounds[0:1, 0:1], min_val=1, max_val=MAXR)
            with pool.If(more > 1):
                with pool.Fori(1, more) as r:
                    first_indices(pool, s, r)
                    with pool.Fori(0, GB) as b:
                        gather_pool(pool, s, dram, r, b)

        def gather_pe_all(pe, s, degrees, step):
            with pe.Fori(0, GB) as b:
                for q in range(B):
                    gather_pe(pe, s, 0, b, q, degrees)
                    step(b, q)
            more = pe.value_load(rounds[0:1, 0:1], min_val=1, max_val=MAXR)
            with pe.If(more > 1):
                with pe.Fori(1, more) as r:
                    with pe.Fori(0, GB) as b:
                        for q in range(B):
                            gather_pe(pe, s, r, b, q, degrees)

        def gather_dve_all(v, s, weighted, step):
            nc.vector.sem_inc(S(s + "_added"), 2)
            windows(s, 0, 0, weighted)
            with v.Fori(0, GB) as b:
                for q in range(B):
                    gather_dve(v, s, 0, b, q, weighted, step)
            next_round(v, s, 0)
            more = v.value_load(rounds[0:1, 0:1], min_val=1, max_val=MAXR)
            with v.If(more > 1):
                with v.Fori(1, more) as r:
                    windows(s, 0, 0, weighted)
                    with v.Fori(0, GB) as b:
                        for q in range(B):
                            gather_dve(v, s, r, b, q, weighted)
                    next_round(v, s, r)

        def slot(u):
            return PS[:, u % 4, 0:D]

        def slot_free(t, u):
            return t + 1 + {0: 4, 4: 1}.get(u, 0)

        def bank(u):
            return PS[:, u, 0:D]

        def up_pe(pe, s, c, weights, rhs, at0, units):
            for m, w in enumerate(weights):
                for h in range(2):
                    n = m * 2 + h
                    pe.wait_ge(S(s + "_upfree"), at0 + n + 1)
                    for k in range(KD):
                        ins = nc.tensor.matmul(PS[:, 4 + n % 4, 0:HALF], w[k], rhs(k, c * CH + h * HALF),
                                               start=k == 0, stop=k == KD - 1)
                    ins.then_inc(S(s + "_up"), 1)

        def up_act(act, s, c, units, at0, func, bias, into):
            for m in range(units // 2):
                for h in range(2):
                    n = m * 2 + h
                    act.wait_ge(S(s + "_up"), at0 + n + 1)
                    nc.scalar.activation(into(m)[:, h * HALF:(h + 1) * HALF], PS[:, 4 + n % 4, 0:HALF], func,
                                         bias=bias(m)).then_inc(S(s + "_upfree"), 1)

        def epilogue_act(act, base, i):
            act.wait_ge(S("ln_var"), base + i + 1)
            nc.scalar.activation(rs5[:, :], rs5[:, :], ACT.Sqrt).then_inc(S("ln_root"), 1)
            act.wait_ge(S("ln_scale"), base + i + 1)
            act.sem_inc(S("act_seen"), 1)
            for u in range(U):
                ins = nc.scalar.activation(tile_of(MB, i * U + u), tile_of(MB, i * U + u), ACT.Identity,
                                           bias=nm5[:, u:u + 1], scale=rs5[:, u:u + 1])
            ins.then_inc(S("mbn"), 1)

        def chunk_stats(v, ch, i):
            v.sem_inc(S("dve_seen"), 1)
            for u in range(U):
                ins = nc.vector.bn_stats(st5[:, u, :], tile_of(MB, i * U + u))
            ch(ins)
            v.sem_inc(S("dve_seen"), 1)
            for u in range(U):
                ins = nc.vector.bn_aggr(mv5[:, u, :], st5[:, u, :])
            ch(ins)

        def chunk_var(v):
            nc.vector.tensor_scalar(rs5[:, :], mv5[:, :, 1], 1e-5, None, ALU.add).then_inc(S("ln_var"), 1)

        def chunk_scale(v, ch, base, i):
            v.wait_ge(S("ln_root"), base + i + 1)
            ch(nc.vector.reciprocal(rs5[:, :], rs5[:, :]))
            nc.vector.scalar_tensor_tensor(out=nm5[:, :], in0=mv5[:, :, 0], scalar=-1.0, in1=rs5[:, :],
                                           op0=ALU.mult, op1=ALU.mult).then_inc(S("ln_scale"), 1)

        def chunk_add(v, ch, i, gb, last):
            mb = MB[:, ds(i * U, U), :]
            xx = X[:, ds(i * U, U), :]
            ch(nc.vector.tensor_tensor(mb, mb, gb[:, 0:1, :].to_broadcast((P, U, D)), ALU.mult))
            if last:
                ch(nc.vector.tensor_tensor(mb, mb, gb[:, 1:2, :].to_broadcast((P, U, D)), ALU.add))
            ch(nc.vector.tensor_tensor(xx, xx, mb, ALU.add))
            if last:
                v.sem_inc(S("x_final"), 1)
            else:
                ch(tiles_stats(X, i))

        EPILOGUE = 6

        @block.sync
        def _(sp):
            def load(dst, src, name):
                sp.dma_start(dst, src).then_inc(S(name), 16)

            sp.wait_ge(S("padded"), 4)
            load(X[:, 0:T - 1, :], A["x"][0:(T - 1) * P, :].rearrange("(t p) d -> p t d", p=P), "x_in")
            load(X[0:TAIL, T - 1, :], A["x"][(T - 1) * P:N, :], "x_in")
            for dst, src in ((srow, A["src"]), (drow, A["dst"]), (wrow, A["edge_weight"])):
                load(dst[0:full_groups, :], src[0:full_groups * GE].rearrange("(g e) -> g e", e=GE), "edges")
                load(dst[full_groups:full_groups + 1, 0:last_group], row(src[full_groups * GE:E]), "edges")
            load(wc, A["wc"].rearrange("(k p) o -> p k o", p=P), "w_conv")
            load(bng, A["bn_gamma"], "w_conv")
            load(bnb, A["bn_beta"], "w_conv")
            load(wres, A["w_res"].rearrange("(k p) o -> p k o", p=P), "w_mix")
            sp.wait_ge(S("bd_zero"), 1)
            for q in range(4):
                load(bd[32 * q:32 * q + 32, :, 32 * q:32 * q + 32],
                     A["w_pw"].rearrange("(j p) o -> p j o", p=P)[32 * q:32 * q + 32, :, :], "w_mix")
            load(dw_, A["w_dw"], "w_mix")
            load(bres_, A["b_res"].partition_broadcast(P), "w_mix")
            stage_end(sp, 1)
            table_store(sp, "l0", xn_dram)
            stage_end(sp, 2)
            stage_end(sp, 3)
            load(w1t, A["g0_w1"].rearrange("(k p) o -> p k o", p=P), "w_g0")
            load(w2t, A["g0_w2"].rearrange("(k p) o -> p k o", p=P), "w_g0")
            load(brow_[0:1, 0:D], row(A["g0_b1"]), "w_g0")
            load(brow_[0:1, D:2 * D], row(A["g0_b2"]), "w_g0")
            stage_end(sp, 4)
            load(wr, A["f0_wr"].rearrange("(k p) e -> p k e", p=P), "w_router")
            load(r0[0:1, 0, :], row(A["f0_br"]), "w_router")
            load(gb0[:, 0, :], A["f0_gamma"].partition_broadcast(P), "w_f0n")
            load(gb0[:, 1, :], A["f0_beta"].partition_broadcast(P), "w_f0n")
            sp.wait_ge(S("routed"), 1)
            for k in range(TOPK):
                e = sp.value_load(r0[0:1, 9, k:k + 1].bitcast(I32), min_val=0, max_val=E0 - 1)
                load(f0w1[:, k, :, :], A["f0_w1"].rearrange("e (k p) f -> e p k f", p=P)[ds(e, 1), :, :, :]
                     .rearrange("a p k f -> (a p) k f"), "w_f0")
                load(f0w2[:, k, :, :], A["f0_w2"].rearrange("e (k p) f -> e p k f", p=P)[ds(e, 1), :, :, :]
                     .rearrange("a p k f -> (a p) k f"), "w_f0")
                load(f0b1_[:, 4 * k:4 * k + 4], A["f0_b1"][ds(e, 1), :, :]
                     .rearrange("a p m -> (a p) m"), "w_f0")
                load(f0row_[0:1, k * D:(k + 1) * D], A["f0_b2"][ds(e, 1), :], "w_f0")
            for h in range(KD):
                sp.dma_start(xe_dram.rearrange("(t p) d -> p t d", p=P)[:, :, h * P:(h + 1) * P],
                             zeros[:, :].rearrange("p (t d) -> p t d", t=1)
                             .to_broadcast((P, SLOTS // P + TOPK, P))).then_inc(S("slots_zero"), 16)
            stage_end(sp, 5)
            table_store(sp, "l1", xs_dram)
            stage_end(sp, 6)
            load(g1w1, A["g1_w1"].rearrange("(k p) o -> p k o", p=P), "w_g1")
            load(g1w2, A["g1_w2"].rearrange("(k p) o -> p k o", p=P), "w_g1")
            load(g1b1_, A["g1_b1"], "w_g1")
            load(g1row_, A["g1_b2"].partition_broadcast(P), "w_g1")
            load(kwc_[:, 0:2], A["m1_kw"], "w_m1")
            load(kwc_[:, 2:4], A["m1_kb"], "w_m1")
            load(vwb_[:, 0:D], A["m1_vw"].partition_broadcast(P), "w_m1")
            load(vwb_[:, D:2 * D], A["m1_vb"].partition_broadcast(P), "w_m1")
            stage_end(sp, 7)
            stage_end(sp, 8)
            load(gate, A["f1_wg"].rearrange("(k p) e -> p k e", p=P), "w_gate")
            load(grow_[0:1, :], row(A["f1_bg"]), "w_gate")
            load(b2f[0:E1, :], A["f1_b2"], "w_gate")
            f1_w1, f1_w2 = (A[k].rearrange("e (k p) f -> p e k f", p=P) for k in ("f1_w1", "f1_w2"))
            load(e_w1[:, EARLY1:E1, :, :], f1_w1[:, EARLY1:E1, :, :], "w_f1")
            load(e_w2[:, EARLY2:E1, :, :], f1_w2[:, EARLY2:E1, :, :], "w_f1")
            stage_end(sp, 9)
            load(b1t, A["f1_b1"].rearrange("e p m -> p e m"), "w_b1")
            load(e_w1[:, 0:EARLY1, :, :], f1_w1[:, 0:EARLY1, :, :], "w_f1")
            load(e_w2[:, 0:EARLY2, :, :], f1_w2[:, 0:EARLY2, :, :], "w_f1")
            sp.wait_ge(S("f1_scattered"), 1)
            with sp.Fori(0, PAIRS + 1) as i:
                for k in range(2):
                    sp.wait_ge(S("f1_tx"), i * 2 + k + 1)
                    sp.dma_start(xs[:, k, :], xe_dram[ds((i * 2 + k) * P, P), :]).then_inc(S(f"f1_xs{k}"), 16)
            stage_end(sp, 10)
            load(gb1[:, 0, :], A["f1_gamma"].partition_broadcast(P), "w_f1n")
            load(gb1[:, 1, :], A["f1_beta"].partition_broadcast(P), "w_f1n")
            with sp.Fori(0, NI - 1) as i:
                sp.wait_ge(S("x_final"), i + 1)
                sp.dma_start(out[0:(T - U) * P, :].rearrange("(t p) d -> p t d", p=P)[:, ds(i * U, U), :],
                             X[:, ds(i * U, U), :]).then_inc(S("out"), 16)
            sp.wait_ge(S("x_final"), NI)
            sp.dma_start(out[(T - U) * P:(T - 1) * P, :].rearrange("(t p) d -> p t d", p=P),
                         X[:, T - U:T - 1, :]).then_inc(S("out"), 16)
            sp.dma_start(out[(T - 1) * P:N, :], X[0:TAIL, T - 1, :]).then_inc(S("out"), 16)
            sp.wait_ge(S("out"), 16 * (NI + 1))

        @block.gpsimd
        def _(pool):
            nc.gpsimd.memset(srow, 0).then_inc(S("padded"), 1)
            nc.gpsimd.memset(drow, int(BIG)).then_inc(S("padded"), 1)
            nc.gpsimd.memset(wrow, 0.0).then_inc(S("padded"), 1)
            nc.gpsimd.memset(X[:, T - 1, :], 0.0).then_inc(S("padded"), 1)
            nc.gpsimd.memset(bd_, 0.0).then_inc(S("bd_zero"), 1)
            nc.gpsimd.memset(ident[:, :], 0.0).then_inc(S("pool_set"), 1)
            nc.gpsimd.memset(valid[:, :], 1.0).then_inc(S("pool_set"), 1)
            nc.gpsimd.memset(blockones[:, :], 0.0).then_inc(S("pool_set"), 1)
            pool.wait_ge(S("pool_set"), 3)
            nc.gpsimd.affine_select(out=ident[:, :], in_=ident[:, :], compare_op=ALU.not_equal, fill=1.0,
                                    base=0, pattern=[[-1, P]], channel_multiplier=1).then_inc(S("consts"), 1)
            nc.gpsimd.affine_select(out=valid[:, :], in_=valid[:, :], compare_op=ALU.is_ge, fill=0.0,
                                    base=N - 1, pattern=[[-P, T]], channel_multiplier=-1).then_inc(S("consts"), 1)
            for q in range(4):
                pool.wait_ge(S("consts"), q + 2)
                nc.gpsimd.memset(blockones[32 * q:32 * q + 32, 32 * q:32 * q + 32], 1.0).then_inc(S("consts"), 1)
            pool.wait_ge(S("consts"), 6)
            nc.gpsimd.memset(ones[:, :], 1.0).then_inc(S("consts"), 1)
            nc.gpsimd.memset(zeros[:, :], 0.0).then_inc(S("consts"), 1)
            nc.gpsimd.memset(ones16[:, :], 1.0).then_inc(S("consts"), 1)
            nc.gpsimd.iota(iota[:, :], pattern=[[1, W]], base=0, channel_multiplier=0,
                           allow_small_or_imprecise_dtypes=True).then_inc(S("consts"), 1)
            nc.gpsimd.iota(pcol[:, 0:1], pattern=[[0, 1]], base=0, channel_multiplier=1,
                           allow_small_or_imprecise_dtypes=True).then_inc(S("consts"), 1)
            nc.gpsimd.memset(before[:, :], 1.0).then_inc(S("consts"), 1)
            pool.wait_ge(S("consts"), 12)
            nc.gpsimd.affine_select(out=before[:, :], in_=before[:, :], compare_op=ALU.is_ge, fill=0.0,
                                    base=-1, pattern=[[1, P]], channel_multiplier=-1).then_inc(S("consts"), 1)
            nc.gpsimd.memset(rel[:, :, :], -1.0).then_inc(S("consts"), 1)
            nc.gpsimd.memset(ewt[:, :, :], 0.0).then_inc(S("consts"), 1)
            nc.gpsimd.memset(idx[:, G, :], 0).then_inc(S("consts"), 1)
            nc.gpsimd.memset(ACC[:, :, :], 0.0).then_inc(S("consts"), 1)
            nc.gpsimd.memset(H0T[:, :, NP:NP + P], 0.0).then_inc(S("consts"), 1)
            stage_end(pool, 1)
            ln_tiles_pool(pool, "l0")
            stage_end(pool, 2)
            gather_pool_all(pool, "g0", xn_dram)
            stage_end(pool, 3)
            stage_end(pool, 4)
            ln_tiles_pool(pool, "f0")
            nc.gpsimd.memset(ACC[:, 0:KD, :], 0.0)
            pool.wait_ge(S("f0_brow"), 2)
            pool.wait_ge(S("ln_mb_act"), 2 * NI * (U - COPIED))
            pool.wait_ge(S("ln_mb"), 2 * (NI + 1) * COPIED)
            with pool.Fori(0, NI) as i:
                mb = MB[:, ds(i * U, U), :]
                nc.gpsimd.tensor_tensor(mb, mb, f0row_[:, 0:D].rearrange("p (a d) -> p a d", a=1)
                                        .to_broadcast((P, U, D)), ALU.add).then_inc(S("x_beta"), 1)
            pool.wait_ge(S("w_f0n"), 32)
            pool.wait_ge(S("ln_xb"), 2 * T)
            with pool.Fori(0, NI) as i:
                xx = X[:, ds(i * U, U), :]
                nc.gpsimd.tensor_tensor(xx, xx, gb0[:, 1:2, :].to_broadcast((P, U, D)), ALU.add)\
                    .then_inc(S("x_beta"), 1)
            stage_end(pool, 5)
            stage_end(pool, 6)
            gather_pool_all(pool, "g1", xs_dram)
            stage_end(pool, 7)
            pool.wait_ge(S("w_g1"), 16 * 4)
            with pool.Fori(0, NI) as i:
                xx = X[:, ds(i * U, U), :]
                nc.gpsimd.tensor_tensor(xx, xx, g1row_.rearrange("p (a d) -> p a d", a=1).to_broadcast((P, U, D)), ALU.add)\
                    .then_inc(S("x_beta"), 1)
            stage_end(pool, 8)
            ln_tiles_pool(pool, "f1")
            stage_end(pool, 9)
            pool.wait_ge(S("f1_slots"), 1)
            pool.wait_ge(S("slots_zero"), 16 * KD)
            for t in range(T):
                for k in range(TOPK):
                    nc.gpsimd.indirect_dma_start(
                        out=xe_dram, out_offset=bass.IndirectOffsetOnAxis(ap=slots[:, k, t:t + 1], axis=0),
                        in_=MB[:, t, :], in_offset=None).then_inc(S("f1_put"), 16)
            pool.wait_ge(S("f1_put"), T * TOPK * 16)
            nc.gpsimd.sem_inc(S("f1_scattered"), 1)
            nc.gpsimd.sem_inc(S("f1_ys_free"), 2)
            with pool.Fori(0, PAIRS) as i:
                for k in range(2):
                    pool.wait_ge(S("f1_ys"), i * 2 + k + 1 + 2)
                    pool.sem_inc(S("idxs_seen"), 1)
                    nc.gpsimd.dma_start(xe_dram[ds((i * 2 + k) * P, P), :], ys[:, k, :]).then_inc(S(f"f1_out{k}"), 16)
                for k in range(2):
                    pool.wait_ge(S(f"f1_out{k}"), i * 16 + 16)
                    pool.sem_inc(S("f1_ys_free"), 1)
            stage_end(pool, 10)
            for k in range(2):
                pool.wait_ge(S(f"f1_out{k}"), PAIRS * 16)
            with pool.Fori(0, NI) as i:
                for u in range(U):
                    t = i * U + u
                    pool.wait_ge(S("f1_cmb"), t + 1)
                    nc.gpsimd.tensor_copy(idxs[:, u, 0:TOPK], slots[:, :, ds(t, 1)].rearrange("p k a -> p (k a)"))\
                        .then_inc(S("f1_idxs"), 1)
                    pool.wait_ge(S("f1_idxs"), t + 1)
                    pool.sem_inc(S("idxs_seen"), 1)
                    for k in range(TOPK):
                        nc.gpsimd.indirect_dma_start(
                            out=cmb[:, u, k, :], out_offset=None, in_=xe_dram,
                            in_offset=bass.IndirectOffsetOnAxis(ap=idxs[:, u, k:k + 1], axis=0),
                        ).then_inc(S(f"f1_rows{u}"), 16)

        @block.scalar
        def _(act):
            fn = Asked(act, S("asked"), S("answered"))
            root_of(fn, rs[:, :])
            fn.take()
            fn.give(nc.scalar.activation(sc[:, 1, :], sc[:, 0, :], ACT.Sqrt))
            fn.take()
            fn.give(nc.scalar.activation(sc[:, 4, :], sc[:, 3, :], ACT.Ln))
            stage_end(act, 1)
            ln_tiles_act(act, "l0", scaled=True)
            act.wait_ge(S("gram"), 1)
            nc.scalar.activation(gram, PS[:, 5:7, 0:D], ACT.Copy).then_inc(S("gram_sb"), 1)
            root_of(fn, bnu)
            stage_end(act, 2)
            def mixer_relu(t):
                act.wait_ge(S("mix_conv"), t + 1)
                act.wait_ge(S("mix_hh"), t + 1)
                for j in range(KQ):
                    nc.scalar.activation(hh[:, 2 + j, :], PS[:, j // 4, (j % 4) * P:(j % 4 + 1) * P], ACT.Relu,
                                         bias=bnt[:, j:j + 1], scale=bns[:, j:j + 1]).then_inc(S("mix_h"), 1)
                act.wait_ge(S("mix_h"), t * KQ + KQ)
                nc.scalar.activation(hsq, hh[:, 2:8, :], ACT.Square)

            mixer_relu(0)
            nc.scalar.sem_inc(S("mix_read"), 1)
            with act.Fori(0, T) as t:
                act.wait_ge(S("mix_s"), t + 1)
                psf = PS[:, :, :].rearrange("p b n -> p (b n)")[:, 1024:1024 + TD]
                nc.scalar.activation(hh_[:, 0:2 * P], psf[:, 0:2 * P], ACT.Relu)
                nc.scalar.activation(hh_[:, 8 * P:10 * P], psf[:, 4 * P:6 * P], ACT.Copy)
                nc.scalar.activation(ks_, psf[:, 2 * P:4 * P], ACT.Relu)
                nc.scalar.activation(ssq_, psf, ACT.Square).then_inc(S("mix_qv"), 1)
                act.wait_ge(S("mix_f"), t + 1)
                nc.scalar.activation(ff[:, 2, :], ff[:, 0, :], ACT.Sqrt, scale=1e-30).then_inc(S("mix_eps"), 1)
                act.wait_ge(S("mix_o"), t + 1 + 1)
                nc.scalar.activation(osq_, oo_, ACT.Square).then_inc(S("mix_osq"), 1)
                mixer_relu(t + 1)
                act.wait_ge(S("mix_ft"), t + 1 + 1)
                act.sem_inc(S("act_seen"), 1)
                nc.scalar.activation(tile_of(MB, t), PS[:, 7, D:2 * D], ACT.Copy)
                nc.scalar.activation(sc[:, 0:2, ds(t, 1)].rearrange("p k a -> p (k a)"), PS[:, 7, 0:2], ACT.Copy)\
                    .then_inc(S("mix_read"), 1)
            stage_end(act, 3)
            root_of(fn, sc[:, 0, :])
            with act.Fori(0, NI) as i:
                for u in range(U):
                    t = i * U + u
                    act.wait_ge(S("n0_mm"), t + 1)
                    nc.scalar.activation(stg[:, u, :, :], XNT[:, :, ds(t * P, P)], ACT.Copy)\
                        .then_inc(S("n0_stg"), 1)
                for u in range(U):
                    t = i * U + u
                    act.wait_ge(S("m0_ft"), t + 1)
                    act.wait_ge(S("n0_ss"), i * 2 * U + u)
                    act.sem_inc(S("act_seen"), 1)
                    nc.scalar.activation(hb[:, u, :], tile_of(MB, t), ACT.Square, accum_out=col(sc[:, 1, :], t))\
                        .then_inc(S("n0_ss"), 1)
                for u in range(U):
                    t = i * U + u
                    act.wait_ge(S("n0_ps"), t + 1 + U)
                    act.wait_ge(S("n0_ss"), i * 2 * U + U + u)
                    act.sem_inc(S("act_seen"), 1)
                    nc.scalar.activation(hb[:, u, :], tile_of(Y, t), ACT.Square, accum_out=col(sc[:, 5, :], t))\
                        .then_inc(S("n0_ss"), 1)
            fn.take()
            nc.scalar.activation(sc[:, 5, :], sc[:, 5, :], ACT.Sqrt)
            nc.scalar.activation(sc[:, 2, :], sc[:, 1, :], ACT.Sqrt).then_inc(S("m0_n4"), 1)
            act.wait_ge(S("m0_n4"), 1)
            fn.give(nc.scalar.activation(sc[:, 3, :], sc[:, 2, :], ACT.Tanh))
            stage_end(act, 4)
            root_of(fn, rs[:, :])
            ln_tiles_act(act, "f0")
            for k in range(TOPK + 1):
                fn.take()
                n = E0 if k < 2 else 1
                fn.give(nc.scalar.activation(r0[0:1, 2, 0:n], r0[0:1, 1, 0:n], ACT.Exp))
            nc.scalar.sem_inc(S("f0_upfree"), 4)
            act.wait_ge(S("w_f0"), 16 * 8)

            def f0_up(c):
                act.wait_ge(S("f0_dn"), c * U + U)
                for e in range(TOPK):
                    up_act(act, "f0", c, 8, c * 16 + 8 * e, ACT.Gelu,
                           lambda m: f0b1_[:, 4 * e + m:4 * e + m + 1], lambda m: f0h[:, e, m, :])

            f0_up(0)
            with act.Fori(1, NCH) as c:
                f0_up(c)
                epilogue_act(act, 0, c - 1)
            epilogue_act(act, 0, NCH - 1)
            stage_end(act, 5)
            root_of(fn, dinvc[:, :])
            root_of(fn, rs[:, :])
            ln_tiles_act(act, "l1")
            stage_end(act, 6)
            for c in range(-(-T // 4)):
                act.wait_ge(S("dinv_mm"), c + 1)
                n = min(4 * P, NP - c * 4 * P)
                nc.scalar.activation(ACC[:, KD, c * 4 * P:c * 4 * P + n], PS[:, 3 + c % 2, 0:n], ACT.Copy)\
                    .then_inc(S("dinv_row"), 1)
            with act.Fori(0, T) as t:
                act.wait_ge(S("m1_c"), t + 1)
                nc.scalar.activation(csq, zb, ACT.Square).then_inc(S("m1_sq"), 1)
                act.wait_ge(S("m1_ss"), t + 1)
                nc.scalar.activation(hst[:, 2, :], hst[:, 1, :], ACT.Sqrt, scale=1.0 / (HC - 1))\
                    .then_inc(S("m1_std"), 1)
            stage_end(act, 7)
            nc.scalar.sem_inc(S("g1_upfree"), 4)
            act.wait_ge(S("w_g1"), 16 * 4)
            with act.Fori(0, NCH) as c:
                act.wait_ge(S("g1_dn"), c * U + U)
                up_act(act, "g1", c, 16, c * 16, ACT.Gelu, lambda m: g1b1_[:, m:m + 1], lambda m: g1h[:, m, :])
            stage_end(act, 8)
            root_of(fn, rs[:, :])
            ln_tiles_act(act, "f1")
            fn.take()
            fn.give(nc.scalar.activation(sc[:, 1, :], sc[:, 0, :], ACT.Exp))
            stage_end(act, 9)
            act.wait_ge(S("f1_scattered"), 1)

            def copy_xt(n, k):
                act.wait_ge(S("f1_tx"), n + 1 + 2)
                nc.scalar.activation(xt[:, k, :, :], v3(PS[:, k, 0:D], P), ACT.Copy).then_inc(S("f1_xt"), 1)

            for k in range(2):
                copy_xt(k, k)
            with act.Fori(0, PAIRS) as i:
                for k in range(2):
                    act.wait_ge(S("f1_h"), i * 2 + k + 1)
                    act.wait_ge(S("f1_y"), i * 2 + k + 1)
                    for m in range(4):
                        ins = nc.scalar.activation(ht[:, k, m, :], PS[:, 2 + k, m * P:(m + 1) * P], ACT.Relu,
                                                   bias=b1s[:, k, m:m + 1])
                    ins.then_inc(S("f1_ht"), 1)
                for k in range(2):
                    copy_xt(i * 2 + 2 + k, k)
            stage_end(act, 10)
            with act.Fori(0, NI) as i:
                epilogue_act(act, NCH, i)

        @block.tensor
        def _(pe):
            pe.wait_ge(S("consts"), 18)
            for q, rows in enumerate((sf, rf, wrow)):
                pe.wait_ge(S("tab_rows"), q + 1)
                for j in range(C):
                    ins = nc.tensor.transpose(PS[:, q, j * P:j * P + G], rows[:, j * P:(j + 1) * P], ident[0:G, 0:G])
                ins.then_inc(S("tab_t"), 1)
            pe.wait_ge(S("tab_rows"), 4)
            nc.tensor.transpose(PS[0:1, 3, 0:G], gb2[:, 0:1], ident[0:G, 0:G])
            nc.tensor.transpose(PS[0:1, 3, P:P + G], gb2[:, 1:2], ident[0:G, 0:G]).then_inc(S("tab_t"), 1)
            stage_end(pe, 1)
            for m in range(KD):
                nc.tensor.matmul(PS[:, 5 + m, 0:P], zeros[:, :], ident[:, :], start=True, stop=False, skip_group_check=True)
                nc.tensor.matmul(PS[:, 5 + m, P:D], zeros[:, :], ident[:, :], start=False, stop=False, skip_group_check=True)
            nc.tensor.matmul(PS[:, 7, 0:KD], zeros[:, :], ident[:, 0:KD], start=True, stop=False, skip_group_check=True)
            ln_tiles_pe(pe, "l0", scaled=True)
            for m in range(KD):
                nc.tensor.matmul(PS[:, 5 + m, 0:P], zeros[:, :], ident[:, :], start=False, stop=True, skip_group_check=True)
            nc.tensor.matmul(PS[:, 7, 0:KD], zeros[:, :], ident[:, 0:KD], start=False, stop=True,
                             skip_group_check=True).then_inc(S("gram"), 1)
            pe.wait_ge(S("w_conv"), 16 * 3)
            pe.wait_ge(S("gram_sb"), 2)
            pe.wait_ge(S("ln_free"), T + U)
            for m in range(KD):
                for h in range(2):
                    for k in range(KD):
                        ins = nc.tensor.matmul(PS[:, 2 * m + h, 0:TD // 2], gram[:, k, m * P:(m + 1) * P],
                                               wc[:, k, h * (TD // 2):(h + 1) * (TD // 2)], start=k == 0, stop=k == KD - 1)
            ins.then_inc(S("bn_cw"), 1)
            for j in range(KQ):
                for k in range(KD):
                    nc.tensor.matmul(PS[:, 7, 8 + j:9 + j], wc[:, k, j * P:(j + 1) * P], sc[:, 7, k:k + 1],
                                     start=k == 0, stop=k == KD - 1)
            pe.wait_ge(S("bn_zz"), 1)
            for j in range(KQ):
                for k in range(KD):
                    ins = nc.tensor.matmul(PS[:, 7, 16 + j:17 + j], zz[:, k, j * P:(j + 1) * P], ones[:, 0:1],
                                           start=k == 0, stop=k == KD - 1)
            ins.then_inc(S("bn_sums"), 1)
            stage_end(pe, 2)

            def mixer_conv(t):
                for j in range(KQ):
                    for k in range(KD):
                        ins = nc.tensor.matmul(PS[:, j // 4, (j % 4) * P:(j % 4 + 1) * P],
                                               wc[:, k, j * P:(j + 1) * P], H0T[:, k, ds(t * P, P)],
                                               start=k == 0, stop=k == KD - 1)
                ins.then_inc(S("mix_conv"), 1)

            def mixer_pe(t, q):
                if q == 0:
                    pe.wait_ge(S("mix_h"), t * KQ + KQ)
                    pe.wait_ge(S("mix_o"), t + 1)
                    for j in range(KQ):
                        nc.tensor.matmul(PS[:, 2 + j // 4, (j % 4) * P:(j % 4 + 1) * P], bd[:, j, :],
                                         hh[:, 2 + j, :], start=True, stop=True)
                    for j in range(2):
                        ins = nc.tensor.matmul(PS[:, 4, j * P:(j + 1) * P], blockones[:, :], hh[:, 4 + j, :],
                                               start=True, stop=True)
                    ins.then_inc(S("mix_s"), 1)
                elif q == 1:
                    pe.wait_ge(S("mix_qv"), t + 1)
                    for j in range(2):
                        nc.tensor.matmul(PS[:, 4, (2 + j) * P:(3 + j) * P], blockones[:, :], ks[:, j, :],
                                         start=True, stop=True)
                    for j in range(2 * KQ):
                        ins = nc.tensor.matmul(PS[:, 3, D:D + P], ones[:, :], (hsq, ssq)[j // KQ][:, j % KQ, :],
                                               start=j == 0, stop=j == 2 * KQ - 1)
                    ins.then_inc(S("mix_sums"), 1)
                elif q == 3:
                    mixer_conv(t + 1)
                    pe.wait_ge(S("mix_o"), t + 1 + 1)
                    pe.wait_ge(S("mix_read"), t + 1)
                    for j in range(4):
                        nc.tensor.matmul(PS[:, 7, D:2 * D], oo[:, j, :], wres[:, j, :], start=j == 0, stop=j == 3)
                    nc.tensor.matmul(PS[:, 7, 1:2], ff[:, 0, :], ident[:, 0:1], start=True, stop=True)
                    pe.wait_ge(S("mix_osq"), t + 1)
                    for j in range(4):
                        ins = nc.tensor.matmul(PS[:, 7, 0:1], osq[:, j, :], ones[:, 0:1], start=j == 0, stop=j == 3)
                    ins.then_inc(S("mix_ft"), 1)

            mixer_conv(0)
            nc.tensor.sem_inc(S("mix_ft"), 1)
            nc.tensor.sem_inc(S("g0_sum"), B)
            gather_pe_all(pe, "g0", True, mixer_pe)
            stage_end(pe, 3)
            nc.tensor.sem_inc(S("n0_mm"), U)
            pe.wait_ge(S("w_g0"), 16 * 4)
            pe.wait_ge(S("n0_brow"), 1)
            with pe.Fori(0, NI) as i:
                for u in range(U):
                    t = i * U + u
                    pe.wait_ge(S("n0_stg"), t + 1)
                    pe.wait_ge(S("n0_u"), t + 1)
                    pe.wait_ge(S("n0_ps"), t + 1)
                    nc.tensor.matmul(bank(u), ones[0:1, :], brow_[0:1, 2 * D:3 * D], start=True, stop=False)
                    for k in range(KD):
                        nc.tensor.matmul(bank(u), stg[:, u, k, :], w1t[:, k, :], start=False, stop=False)
                    for k in range(KD):
                        ins = nc.tensor.matmul(bank(u), ust[:, u, k, :], w2t[:, k, :], start=False, stop=k == KD - 1)
                    ins.then_inc(S("n0_mm"), 1)
            stage_end(pe, 4)
            ln_tiles_pe(pe, "f0")
            nc.tensor.matmul(PS[:, 7, 0:KD], zeros[:, :], ident[:, 0:KD], start=False, stop=True,
                             skip_group_check=True).then_inc(S("route_mm"), 1)
            pe.wait_ge(S("f0_ysum"), 1)
            pe.wait_ge(S("w_router"), 32)
            for k in range(KD):
                ins = nc.tensor.matmul(PS[0:1, 5, 0:E0], ysum[:, k:k + 1], wr[:, k, :], start=k == 0, stop=k == KD - 1)
            ins.then_inc(S("route_mm"), 1)
            pe.wait_ge(S("routed"), 1)
            nc.tensor.matmul(PS[:, 3, 0:TOPK], ones[0:1, :], r0[0:1, 8, 0:TOPK], start=True, stop=True)\
                .then_inc(S("route_mm"), 1)
            nc.tensor.sem_inc(S("f0_dn"), U)
            pe.wait_ge(S("w_f0"), 16 * 8)
            pe.wait_ge(S("f0_brow"), 1)
            nc.tensor.matmul(PS[:, 2, 0:D], ones[0:1, :], f0row_[0:1, 2 * D:3 * D], start=True, stop=True)\
                .then_inc(S("route_mm"), 1)
            with pe.Fori(0, NCH) as c:
                for e in range(TOPK):
                    up_pe(pe, "f0", c, [[f0w1[:, e, k, m * P:(m + 1) * P] for k in range(KD)] for m in range(4)],
                          lambda k, at: XNT[:, k, ds(at, HALF)], c * 16 + 8 * e, 8)
                pe.wait_ge(S("f0_upfree"), c * 16 + 16 + 4)
                pe.wait_ge(S("f0_w2s"), 1)
                for u in range(U):
                    pe.wait_ge(S("f0_dfree"), slot_free(c * U + u, u))
                    for e in range(TOPK):
                        for k in range(4):
                            ins = nc.tensor.matmul(slot(u), f0h[:, e, k, u * P:(u + 1) * P], f0w2[:, e, k, :],
                                                   start=(e, k) == (0, 0), stop=(e, k) == (TOPK - 1, 3))
                    ins.then_inc(S("f0_dn"), 1)
            stage_end(pe, 5)
            ln_tiles_pe(pe, "l1")
            stage_end(pe, 6)
            for at in range(0, D, P):
                nc.tensor.matmul(PS[:, 0, at:at + P], zeros[:, :], ident[:, :], start=at == 0, stop=False, skip_group_check=True)
                nc.tensor.matmul(PS[:, 1, at:at + P], zeros[:, :], ident[:, :], start=at == 0, stop=False, skip_group_check=True)
            nc.tensor.matmul(PS[:, 2, 0:KD], zeros[:, :], ident[:, 0:KD], start=True, stop=False, skip_group_check=True)
            nc.tensor.sem_inc(S("m1_mm"), 1)

            def mixer1_pe(t, q):
                if q == 3:
                    pe.wait_ge(S("m1_z"), t + 1)
                    for m in range(KD):
                        nc.tensor.matmul(PS[:, 0, m * P:(m + 1) * P], zb[:, m * P:(m + 1) * P], zb[:, m * P:(m + 1) * P],
                                         start=False, stop=False, skip_group_check=True)
                        nc.tensor.matmul(PS[:, 2, m:m + 1], zb[:, m * P:(m + 1) * P], ones[:, 0:1],
                                         start=False, stop=False, skip_group_check=True)
                    nc.tensor.matmul(PS[:, 1, 0:D], ones[:, :], zb[:, 0:D],
                                     start=False, stop=False, skip_group_check=True).then_inc(S("m1_mm"), 1)

            nc.tensor.sem_inc(S("g1_sum"), B)
            pe.wait_ge(S("dinv_diag"), 1)
            for c in range(-(-T // 4)):
                if c >= 2:
                    pe.wait_ge(S("dinv_row"), c - 1)
                n = min(4 * P, NP - c * 4 * P)
                nc.tensor.matmul(PS[:, 3 + c % 2, 0:n], ones[:, :], mflat[:, c * 4 * P:c * 4 * P + n],
                                 start=True, stop=True).then_inc(S("dinv_mm"), 1)
            gather_pe_all(pe, "g1", False, mixer1_pe)
            for b in range(2):
                nc.tensor.matmul(PS[:, b, 0:P], zeros[:, :], ident[:, :], start=False, stop=True, skip_group_check=True)
            nc.tensor.matmul(PS[:, 2, 0:KD], zeros[:, :], ident[:, 0:KD], start=False, stop=True, skip_group_check=True)
            stage_end(pe, 7)
            nc.tensor.sem_inc(S("g1_dn"), U)
            pe.wait_ge(S("w_g1"), 16 * 4)
            with pe.Fori(0, NCH) as c:
                pe.wait_ge(S("agg"), c + 1)
                up_pe(pe, "g1", c, [[g1w1[:, k, m * P:(m + 1) * P] for k in range(KD)] for m in range(8)],
                      lambda k, at: ACC[:, k, ds(at, HALF)], c * 16, 16)
                pe.wait_ge(S("g1_upfree"), c * 16 + 16 + 4)
                pe.wait_ge(S("kv"), 1)
                for u in range(U):
                    pe.wait_ge(S("g1_dfree"), slot_free(c * U + u, u))
                    pe.wait_ge(S("g1_stg"), c * U + u + 1)
                    for k in range(8):
                        ins = nc.tensor.matmul(slot(u), g1h[:, k, u * P:(u + 1) * P], g1w2[:, k, :],
                                               start=k == 0, stop=k == 7)
                        for m in range(KD if k == 0 else 0):
                            nc.tensor.matmul(slot(u)[:, m * P:(m + 1) * P], stg1[:, u, m, :], kv[:, m, :],
                                             start=False, stop=False)
                    ins.then_inc(S("g1_dn"), 1)
            stage_end(pe, 8)
            nc.tensor.sem_inc(S("f1_gate"), U)
            pe.wait_ge(S("w_gate"), 48)

            def gate_pe(i, u, t):
                pe.wait_ge(S("f1_stg"), t + 1)
                ins = nc.tensor.matmul(PS[:, u, D:D + E1], ones[0:1, :], grow_[0:1, :], start=True, stop=False)
                for k in range(KD):
                    ins = nc.tensor.matmul(PS[:, u, D:D + E1], stg2[:, u, k, :], gate[:, k, :],
                                           start=False, stop=k == KD - 1)
                ins.then_inc(S("f1_gate"), 1)

            ln_tiles_pe(pe, "f1", after=gate_pe)
            pe.wait_ge(S("f1_cnt"), 1)
            nc.tensor.matmul(PS[:, 5, 0:T * E1], before[:, :], cnt_, start=True, stop=True)
            nc.tensor.matmul(PS[:, 6, 0:T * E1], ones[:, :], cnt_, start=True, stop=True).then_inc(S("f1_rank"), 1)
            stage_end(pe, 9)
            pe.wait_ge(S("w_f1"), 64)
            pe.wait_ge(S("f1_b3"), 1)

            def transpose_x(n, k):
                pe.wait_ge(S(f"f1_xs{k}"), 16 + (n - k) * 8)
                for m in range(KD):
                    ins = nc.tensor.transpose(PS[:, k, m * P:(m + 1) * P], xs[:, k, m * P:(m + 1) * P], ident[:, :])
                ins.then_inc(S("f1_tx"), 1)

            nc.tensor.sem_inc(S("f1_tx"), 2)
            nc.tensor.sem_inc(S("f1_y"), 2)
            for k in range(2):
                transpose_x(k, k)
            with pe.Fori(0, PAIRS) as i:
                for k in range(2):
                    n = i * 2 + k
                    pe.wait_ge(S("f1_xt"), n + 1)
                    pe.wait_ge(S("f1_w"), n + 1)
                    for m in range(4):
                        for j in range(KD):
                            ins = nc.tensor.matmul(PS[:, 2 + k, m * P:(m + 1) * P], w1s[:, k, j, m * P:(m + 1) * P],
                                                   xt[:, k, j, :], start=j == 0, stop=j == KD - 1)
                    ins.then_inc(S("f1_h"), 1)
                for k in range(2):
                    transpose_x(i * 2 + 2 + k, k)
                for k in range(2):
                    n = i * 2 + k
                    e = pe.value_load(eji[0:1, ds(n, 1)], min_val=0, max_val=E1 - 1)
                    pe.wait_ge(S("f1_ht"), n + 1)
                    pe.wait_ge(S("f1_sel"), n + 1)
                    pe.wait_ge(S("f1_ys"), n + 1)
                    nc.tensor.matmul(PS[:, 6 + k, 0:D], sel[0:96, k, :], b3[0:96, :], start=True, stop=False)
                    for m in range(4):
                        ins = nc.tensor.matmul(PS[:, 6 + k, 0:D], ht[:, k, m, :],
                                               e_w2[:, ds(e, 1), m, :].rearrange("p a f -> p (a f)"),
                                               start=False, stop=m == 3)
                    ins.then_inc(S("f1_y"), 1)
            stage_end(pe, 10)

        @block.vector
        def _(v):
            ch = Chain(v, S("dve"))
            fn = Asked(v, S("asked"), S("answered"))
            v.wait_ge(S("edges"), 16 * 6)
            nc.vector.tensor_copy(sf, srow).then_inc(S("tab_rows"), 1)
            ch(nc.vector.tensor_copy(df, drow))
            ch(nc.vector.tensor_reduce(out=gb2[:, 0:1], in_=df, axis=AX.X, op=ALU.min))
            ch(nc.vector.tensor_scalar(rf, df, gb2[:, 0:1], None, ALU.subtract))
            ch(nc.vector.scalar_tensor_tensor(out=mf, in0=df, scalar=BIG / 2, in1=rf, op0=ALU.is_lt, op1=ALU.mult))
            v.sem_inc(S("tab_rows"), 2)
            ch(nc.vector.tensor_reduce(out=gb2[:, 1:2], in_=mf, axis=AX.X, op=ALU.max))
            ch(nc.vector.tensor_scalar(gb2[:, 0:1], gb2[:, 0:1], float(N), None, ALU.min))
            v.sem_inc(S("tab_rows"), 1)
            v.wait_ge(S("tab_t"), 4)
            v.wait_ge(S("consts"), 18)
            for q, table in enumerate((idx[:, 0:G, :], rel0[:, :, :], ewt[:, 0:G, :])):
                ch(nc.vector.tensor_copy(table.rearrange("p g c -> p c g"), v3(PS[:, q, :], P)[:, :, 0:G]))
            ch(nc.vector.tensor_copy(rel[:, 0:G, :], rel0[:, :, :]))
            ch(nc.vector.tensor_copy(base0[:, :], PS[0:1, 3, 0:G]))
            ch(nc.vector.tensor_copy(base[:, :], base0[:, :]))
            ch(nc.vector.tensor_reduce(out=farthest[:, :], in_=PS[0:1, 3, P:P + G], axis=AX.X, op=ALU.max))
            ch(nc.vector.tensor_scalar(rounds[:, :], farthest[:, :], 1.0 / W, 1.0 - (W - 1) / 2 / W, ALU.mult, ALU.add))
            v.wait_ge(S("x_in"), 32)
            with v.Fori(0, NI) as i:
                ch.enter(i, 1)
                ch(tiles_stats(X, i))
            ch.leave(NI)
            ln_stats(v, ch, fn, 1e-5)
            n2, n, lo, hi, ln, fac = (sc[:, k, :] for k in range(6))
            ch(nc.vector.tensor_tensor(n2, rs[:, :], rs[:, :], ALU.mult))
            ch(nc.vector.tensor_tensor(n2, n2, mv[:, :, 1], ALU.mult))
            fn.ask(nc.vector.tensor_scalar(n2, n2, float(D), TINY, ALU.mult, ALU.max))
            ch(nc.vector.tensor_scalar(lo, n, MAXNORM, None, ALU.min))
            ch(nc.vector.tensor_scalar(hi, lo, 1.0, None, ALU.add))
            ch(nc.vector.tensor_scalar(lo, lo, -1.0, 1.0, ALU.mult, ALU.add))
            ch(nc.vector.reciprocal(lo, lo))
            fn.ask(nc.vector.tensor_tensor(hi, hi, lo, ALU.mult))
            ch(nc.vector.reciprocal(lo, n))
            ch(nc.vector.scalar_tensor_tensor(out=fac, in0=ln, scalar=0.5, in1=lo, op0=ALU.mult, op1=ALU.mult))
            ch(nc.vector.tensor_scalar(lo, n2, 1.0 / 7, 1.0 / 5, ALU.mult, ALU.add))
            ch(nc.vector.tensor_tensor(lo, lo, n2, ALU.mult))
            ch(nc.vector.tensor_scalar(lo, lo, 1.0 / 3, None, ALU.add))
            ch(nc.vector.tensor_tensor(lo, lo, n2, ALU.mult))
            ch(nc.vector.scalar_tensor_tensor(out=lo, in0=lo, scalar=1.0, in1=fac, op0=ALU.add, op1=ALU.subtract))
            ch(nc.vector.scalar_tensor_tensor(out=lo, in0=n, scalar=0.05, in1=lo, op0=ALU.is_lt, op1=ALU.mult))
            ch(nc.vector.tensor_tensor(fac, fac, lo, ALU.add))
            v.sem_inc(S("norms"), 1)
            stage_end(v, 1)
            ln_tiles_dve(v, "l0", scaled=fac)
            v.wait_ge(S("gram"), 1)
            nc.vector.tensor_scalar(sc[:, 7, 0:KD], PS[:, 7, 0:KD], 1.0 / N, None, ALU.mult).then_inc(S("gram_sb"), 1)
            v.wait_ge(S("bn_cw"), 1)
            v.wait_ge(S("w_conv"), 48)
            for m in range(KD):
                ch(nc.vector.tensor_tensor(zz[:, m, :].rearrange("p (h o) -> p h o", h=2),
                                           wc[:, m, :].rearrange("p (h o) -> p h o", h=2),
                                           PS[:, 2 * m:2 * m + 2, 0:TD // 2], ALU.mult))
            v.sem_inc(S("bn_zz"), 1)
            v.wait_ge(S("bn_sums"), 1)
            ch(nc.vector.tensor_copy(bnm, PS[:, 7, 8:8 + KQ]))
            ch(nc.vector.tensor_tensor(bns, bnm, bnm, ALU.mult))
            ch(nc.vector.scalar_tensor_tensor(out=bnu, in0=PS[:, 7, 16:16 + KQ], scalar=1.0 / N, in1=bns,
                                              op0=ALU.mult, op1=ALU.subtract))
            fn.ask(nc.vector.tensor_scalar(bnu, bnu, 0.0, 1e-5, ALU.max, ALU.add))
            ch(nc.vector.reciprocal(bnu, bnu))
            ch(nc.vector.tensor_tensor(bns, bng, bnu, ALU.mult))
            ch(nc.vector.tensor_tensor(bnm, bnm, bns, ALU.mult))
            ch(nc.vector.tensor_tensor(bnt, bnb, bnm, ALU.subtract))
            v.wait_ge(S("w_mix"), 16 * 7)
            ch(nc.vector.tensor_tensor(bd, bd, dw_.rearrange("p (j a) -> p j a", a=1).to_broadcast((P, KQ, P)), ALU.mult))
            stage_end(v, 2)

            A2 = ATANH_MAX * ATANH_MAX

            def mixer_dve(t, q):
                if q == 1:
                    v.wait_ge(S("mix_qv"), t + 1)
                    v.wait_ge(S("mix_ft"), t + 1)
                    nc.vector.tensor_tensor(oo[:, 0:2, :], hh[:, 6:8, :], hh[:, 2:4, :], ALU.mult)
                    nc.vector.tensor_tensor(oo[:, 2:4, :], hh[:, 8:10, :], hh[:, 0:2, :], ALU.mult)\
                        .then_inc(S("mix_r"), 1)
                elif q == 2:
                    v.wait_ge(S("mix_sums"), t + 1)
                    nc.vector.tensor_scalar(ff[:, 0, :], PS[:, 3, D:D + P], 1.0 / A2, 1.0, ALU.mult, ALU.max)\
                        .then_inc(S("mix_f"), 1)
                    v.wait_ge(S("mix_eps"), t + 1)
                    nc.vector.tensor_tensor(rr, hh[:, 6:10, :], ff[:, 2:3, :].to_broadcast((P, 4, P)), ALU.add)\
                        .then_inc(S("mix_hh"), 1)
                    v.wait_ge(S("mix_hh"), t + 1 + 1)
                    nc.vector.reciprocal(rr, rr).then_inc(S("mix_r"), 1)
                    v.wait_ge(S("mix_r"), t * 3 + 2)
                    nc.vector.tensor_tensor(oo, rr, oo, ALU.mult).then_inc(S("mix_r"), 1)
                    v.wait_ge(S("mix_r"), t * 3 + 3)
                    nc.vector.tensor_tensor(oo, oo, PS[:, 4, :].rearrange("p (j n) -> p j n", n=P), ALU.mult)\
                        .then_inc(S("mix_o"), 1)

            nc.vector.sem_inc(S("mix_o"), 1)
            nc.vector.sem_inc(S("mix_hh"), 1)
            gather_dve_all(v, "g0", True, mixer_dve)
            stage_end(v, 3)
            a, b, c4, th, f = (sc[:, k, :] for k in range(5))
            fn.ask(nc.vector.tensor_scalar(a, a, TINY, None, ALU.max))
            ch(nc.vector.reciprocal(a, a))
            ch(nc.vector.reciprocal(b, b))
            ch(nc.vector.scalar_tensor_tensor(out=a, in0=a, scalar=ATANH_MAX, in1=b, op0=ALU.mult, op1=ALU.min))
            v.wait_ge(S("w_g0"), 64)
            nc.vector.tensor_tensor(brow_[0:1, 2 * D:3 * D], brow_[0:1, 0:D], brow_[0:1, D:2 * D], ALU.add)\
                .then_inc(S("n0_brow"), 1)
            nc.vector.sem_inc(S("n0_ps"), U)
            with v.Fori(0, NI) as i:
                for u in range(U):
                    t = i * U + u
                    v.wait_ge(S("n0_mm"), t + 1)
                    nc.vector.scalar_tensor_tensor(out=ust[:, u, :, :], in0=XNT[:, :, ds(t * P, P)], scalar=1.0,
                                                   in1=ACC[:, 0:KD, ds(t * P, P)], op0=ALU.add, op1=ALU.mult)\
                        .then_inc(S("n0_u"), 1)
                for u in range(U):
                    t = i * U + u
                    nc.vector.scalar_tensor_tensor(out=tile_of(MB, t), in0=tile_of(MB, t), scalar=col(a, t), in1=bres_,
                                                   op0=ALU.mult, op1=ALU.add).then_inc(S("m0_ft"), 1)
                for u in range(U):
                    t = i * U + u
                    v.wait_ge(S("n0_mm"), t + 1 + U)
                    nc.vector.tensor_scalar(tile_of(Y, t), bank(u), 0.2, None, ALU.mult).then_inc(S("n0_y"), 1)
                    v.wait_ge(S("n0_y"), t + 1)
                    nc.vector.tensor_tensor(tile_of(Y, t), tile_of(Y, t), bank(u), ALU.max).then_inc(S("n0_ps"), 1)
            ysq = sc[:, 5, :]
            v.wait_ge(S("n0_ss"), 2 * T)
            ch(nc.vector.tensor_scalar(ysq, ysq, 1e-24, None, ALU.max))
            fn.ask(nc.vector.tensor_scalar(b, b, TINY, None, ALU.max))
            ch(nc.vector.reciprocal(ysq, ysq))
            ch(nc.vector.reciprocal(f, c4))
            ch(nc.vector.scalar_tensor_tensor(out=f, in0=th, scalar=MAXNORM, in1=f, op0=ALU.min, op1=ALU.mult))
            with v.Fori(0, NI) as i:
                ch.enter(i, 3)
                for rows, by in ((MB, f), (Y, ysq)):
                    for u in range(U):
                        t = i * U + u
                        ins = nc.vector.scalar_tensor_tensor(out=tile_of(X, t), in0=tile_of(rows, t), scalar=col(by, t),
                                                             in1=tile_of(X, t), op0=ALU.mult, op1=ALU.add)
                    ch(ins)
                ch(tiles_stats(X, i))
            ch.leave(NI)
            stage_end(v, 4)
            ln_stats(v, ch, fn, 1e-5)
            v.sem_inc(S("norms"), 1)
            ln_tiles_dve(v, "f0")
            v.wait_ge(S("route_mm"), 1)
            nc.vector.tensor_scalar(ysum, PS[:, 7, 0:KD], 1.0 / N, None, ALU.mult).then_inc(S("f0_ysum"), 1)
            v.wait_ge(S("route_mm"), 2)
            v.wait_ge(S("w_router"), 32)
            R = lambda k, n=E0: r0[0:1, k, 0:n]
            ch(nc.vector.tensor_tensor(R(3), R(0), PS[0:1, 5, 0:E0], ALU.add))
            for k in range(2):
                ch(nc.vector.tensor_reduce(out=R(5, 1), in_=R(3), axis=AX.X, op=ALU.max))
                fn.ask(nc.vector.tensor_scalar(R(1), R(3), R(5, 1), None, ALU.subtract))
                ch(nc.vector.tensor_reduce(out=R(5, 1), in_=R(2), axis=AX.X, op=ALU.add))
                ch(nc.vector.reciprocal(R(5, 1), R(5, 1)))
                ch(nc.vector.tensor_scalar(R(4), R(2), R(5, 1), None, ALU.mult))
                if k == 0:
                    ch(nc.vector.tensor_scalar(R(6), R(4), float(N), TINY, ALU.mult, ALU.max))
                    ch(nc.vector.reciprocal(R(6), R(6)))
                    ch(nc.vector.tensor_scalar(R(6), R(6), CAPACITY, 1.0, ALU.mult, ALU.min))
                    ch(nc.vector.tensor_tensor(R(3), R(4), R(6), ALU.mult))
            ch(nc.vector.max(out=R(7), in_=R(4)))
            ch(nc.vector.max_index(out=R(9).bitcast(U32), in_max=R(7), in_values=R(4)))
            fn.ask(nc.vector.tensor_tensor(R(1, 1), r0[0:1, 7, 1:2], r0[0:1, 7, 0:1], ALU.subtract))
            ch(nc.vector.tensor_scalar(R(6, 1), R(2, 1), 1.0, None, ALU.add))
            ch(nc.vector.reciprocal(r0[0:1, 8, 0:1], R(6, 1)))
            ch(nc.vector.tensor_tensor(r0[0:1, 8, 1:2], r0[0:1, 8, 0:1], R(2, 1), ALU.mult))
            v.sem_inc(S("routed"), 1)
            v.wait_ge(S("route_mm"), 3)
            ch(nc.vector.tensor_copy(wexp, PS[:, 3, 0:TOPK]))
            v.wait_ge(S("w_f0"), 16 * 8)
            ch(nc.vector.tensor_scalar(f0row_[0:1, 2 * D:3 * D], f0row_[0:1, 0:D], wexp[0:1, 0:1], None, ALU.mult))
            nc.vector.scalar_tensor_tensor(out=f0row_[0:1, 2 * D:3 * D], in0=f0row_[0:1, D:2 * D],
                                           scalar=wexp[0:1, 1:2], in1=f0row_[0:1, 2 * D:3 * D],
                                           op0=ALU.mult, op1=ALU.add).then_inc(S("f0_brow"), 1)
            for e in range(TOPK):
                ins = nc.vector.tensor_scalar(f0w2[:, e, :, :], f0w2[:, e, :, :], wexp[:, e:e + 1], None, ALU.mult)
            ch(ins)
            v.sem_inc(S("f0_w2s"), 1)
            v.wait_ge(S("route_mm"), 4)
            nc.vector.tensor_copy(f0row_[:, 0:D], PS[:, 2, 0:D]).then_inc(S("f0_brow"), 1)
            v.wait_ge(S("ln_mb"), 2 * (NI + 1) * COPIED)
            diag = v3(gflat[:, 0:NP], P)
            eye = ident[:, :].rearrange("p (a n) -> p a n", a=1).to_broadcast((P, T, P))
            ch(nc.vector.tensor_tensor(diag, v3(ACC[:, KD, 0:NP], P), eye, ALU.mult))
            ch(nc.vector.tensor_reduce(out=dinvc[:, :], in_=diag, axis=AX.X, op=ALU.add))
            nc.vector.sem_inc(S("f0_dfree"), U)
            v.wait_ge(S("w_f0n"), 32)
            v.wait_ge(S("x_beta"), NI)
            with v.Fori(0, NCH) as c:
                for u in range(U):
                    t = c * U + u
                    v.wait_ge(S("f0_dn"), t + 1 + U)
                    nc.vector.tensor_tensor(tile_of(MB, t), tile_of(MB, t), slot(u), ALU.add)\
                        .then_inc(S("f0_dfree"), 1)
                v.wait_ge(S("f0_dfree"), c * U + 2 * U)
                ch.enter(c, EPILOGUE)
                v.wait_ge(S("x_beta"), NI + c + 1)
                chunk_stats(v, ch, c)
                chunk_var(v)
                chunk_scale(v, ch, 0, c)
                v.wait_ge(S("mbn"), c + 1)
                chunk_add(v, ch, c, gb0, False)
            ch.leave(NCH)
            stage_end(v, 5)
            nc.vector.tensor_scalar(rel[:, 0:G, :], rel0[:, :, :], 0.0, None, ALU.add)
            nc.vector.tensor_copy(base[:, :], base0[:, :])
            dinv, some = dinvc[:, :], sc[:, 2, :]
            ch(nc.vector.tensor_scalar(some, dinv, 0.0, None, ALU.is_gt))
            fn.ask(nc.vector.tensor_scalar(dinv, dinv, 1e-12, None, ALU.max))
            ch(nc.vector.reciprocal(dinv, dinv))
            ch(nc.vector.tensor_tensor(dinv, dinv, some, ALU.mult))
            ln_stats(v, ch, fn, 1e-5)
            ch(nc.vector.tensor_tensor(sc[:, 0, :], rs[:, :], dinvc[:, :], ALU.mult))
            ch(nc.vector.tensor_tensor(sc[:, 1, :], nm[:, :], dinvc[:, :], ALU.mult))
            v.sem_inc(S("norms"), 1)
            ln_tiles_dve(v, "l1")
            stage_end(v, 6)

            c1 = Chain(v, S("dve_mix1"))

            def mixer1_dve(t, q):
                z8 = v3(zb, HC)
                if q == 0:
                    c1.enter(t, 3)
                    v.wait_ge(S("m1_mm"), t + 1)
                    c1(nc.vector.tensor_scalar(zb, tile_of(X, t), col(rs, t), col(nm, t), ALU.mult, ALU.add))
                    c1(nc.vector.tensor_reduce(out=hst[:, 0, :], in_=z8, axis=AX.X, op=ALU.add))
                    c1(nc.vector.tensor_scalar(hst[:, 0, :], hst[:, 0, :], 1.0 / HC, None, ALU.mult))
                    mean = hst[:, 0, :].rearrange("p (h a) -> p h a", a=1).to_broadcast((P, HEADS, HC))
                    nc.vector.tensor_tensor(z8, z8, mean, ALU.subtract).then_inc(S("m1_c"), 1)
                elif q == 1:
                    v.wait_ge(S("m1_sq"), t + 1)
                    nc.vector.tensor_reduce(out=hst[:, 1, :], in_=v3(csq, HC), axis=AX.X, op=ALU.add)\
                        .then_inc(S("m1_ss"), 1)
                elif q == 2:
                    v.wait_ge(S("m1_std"), t + 1)
                    nc.vector.tensor_scalar(hst[:, 2, :], hst[:, 2, :], 1e-5, None, ALU.add).then_inc(S("m1_r"), 1)
                    v.wait_ge(S("m1_r"), t * 3 + 1)
                    nc.vector.reciprocal(hst[:, 3, :], hst[:, 2, :]).then_inc(S("m1_r"), 1)
                    v.wait_ge(S("m1_r"), t * 3 + 2)
                    nc.vector.tensor_scalar(hst[:, 3, :], hst[:, 3, :], col(valid, t), None, ALU.mult)\
                        .then_inc(S("m1_r"), 1)
                    v.wait_ge(S("m1_r"), t * 3 + 3)
                    inv = hst[:, 3, :].rearrange("p (h a) -> p h a", a=1).to_broadcast((P, HEADS, HC))
                    nc.vector.tensor_tensor(z8, z8, inv, ALU.mult).then_inc(S("m1_z"), 1)

            spread = v3(mflat[:, 0:NP], P)
            nc.vector.tensor_tensor(spread, eye, dinvc[:, :].rearrange("p (t a) -> p t a", a=1)
                                    .to_broadcast((P, T, P)), ALU.mult).then_inc(S("dinv_diag"), 1)
            gather_dve_all(v, "g1", False, mixer1_dve)
            stage_end(v, 7)
            for c in range(NCH):
                acc = ACC[:, 0:KD, c * CH:(c + 1) * CH]
                nc.vector.tensor_tensor(acc, acc, ACC[:, KD:KD + 1, c * CH:(c + 1) * CH].to_broadcast((P, KD, CH)),
                                        ALU.mult).then_inc(S("agg"), 1)
            v.wait_ge(S("w_m1"), 64)
            for m in range(KD):
                zcol = sc[:, 2, m:m + 1]
                ch(nc.vector.tensor_copy(zcol, PS[:, 2, m:m + 1]))
                ch(nc.vector.tensor_tensor(kt1[:, m, :], vwb[:, m, :], PS[:, 0, m * P:(m + 1) * P], ALU.mult))
                ch(nc.vector.scalar_tensor_tensor(out=kt1[:, m, :], in0=vbb[:, m, :], scalar=zcol, in1=kt1[:, m, :],
                                                  op0=ALU.mult, op1=ALU.add))
                ch(nc.vector.tensor_scalar(kt1[:, m, :], kt1[:, m, :], kwc_[:, m:m + 1], None, ALU.mult))
                ch(nc.vector.tensor_tensor(kt2[:, m, :], vwb[:, m, :], PS[:, 1, m * P:(m + 1) * P], ALU.mult))
                ch(nc.vector.scalar_tensor_tensor(out=kt2[:, m, :], in0=vbb[:, m, :], scalar=float(N), in1=kt2[:, m, :],
                                                  op0=ALU.mult, op1=ALU.add))
                ch(nc.vector.scalar_tensor_tensor(out=kv[:, m, :], in0=kt2[:, m, :], scalar=kwc_[:, 2 + m:3 + m],
                                                  in1=kt1[:, m, :], op0=ALU.mult, op1=ALU.add))
                ch(nc.vector.scalar_tensor_tensor(out=kv[:, m, :], in0=kv[:, m, :], scalar=1.0 / N, in1=blockones[:, :],
                                                  op0=ALU.mult, op1=ALU.mult))
                ch(nc.vector.tensor_tensor(kv[:, m, :], kv[:, m, :], ident[:, :], ALU.add))
            v.sem_inc(S("kv"), 1)
            nc.vector.sem_inc(S("g1_dfree"), U)
            v.wait_ge(S("x_beta"), 3 * NI)
            with v.Fori(0, NCH) as c:
                for u in range(U):
                    t = c * U + u
                    v.wait_ge(S("g1_dn"), t + 1)
                    nc.vector.tensor_copy(stg1[:, u, :, :], XNT[:, :, ds(t * P, P)]).then_inc(S("g1_stg"), 1)
                for u in range(U):
                    t = c * U + u
                    v.wait_ge(S("g1_dn"), t + 1 + U)
                    nc.vector.tensor_tensor(tile_of(X, t), tile_of(X, t), slot(u), ALU.add)\
                        .then_inc(S("g1_dfree"), 1)
                v.wait_ge(S("g1_dfree"), c * U + 2 * U)
                ch.enter(c, 1)
                ch(tiles_stats(X, c))
            ch.leave(NCH)
            stage_end(v, 8)
            ln_stats(v, ch, fn, 1e-5)

            v.sem_inc(S("norms"), 1)

            def gate_dve(i):
                for u in range(U):
                    t = i * U + u
                    v.wait_ge(S("ln_free"), 3 * (T + U) + t + 1 + U)
                    v.wait_ge(S("f1_gate"), t + 1)
                    nc.vector.tensor_copy(stg2[:, u, :, :], XNT[:, :, ds(t * P, P)]).then_inc(S("f1_stg"), 1)
                for u in range(U):
                    t = i * U + u
                    v.wait_ge(S("f1_gate"), t + 1 + U)
                    nc.vector.tensor_copy(tile_of(lg, t), PS[:, u, D:D + E1]).then_inc(S("f1_lg"), 1)

            ln_tiles_dve(v, "f1", extra=gate_dve)
            v.wait_ge(S("f1_lg"), T)
            for t in range(T):
                ins = nc.vector.max(out=top[:, t, :], in_=lg[:, t, :])
            ch(ins)
            for t in range(T):
                ins = nc.vector.max_index(out=topi[:, t, :], in_max=top[:, t, :], in_values=lg[:, t, :])
            ch(ins)
            p1, p2, i1, i2 = (sc[:, k, :] for k in (2, 3, 4, 5))
            fn.ask(nc.vector.tensor_tensor(sc[:, 0, :], top[:, :, 1], top[:, :, 0], ALU.subtract))
            ch(nc.vector.tensor_scalar(p1, sc[:, 1, :], 1.0, None, ALU.add))
            ch(nc.vector.reciprocal(p1, p1))
            ch(nc.vector.tensor_tensor(p2, p1, sc[:, 1, :], ALU.mult))
            ch(nc.vector.tensor_copy(i1, topi[:, :, 0]))
            ch(nc.vector.tensor_copy(i2, topi[:, :, 1]))

            def by_node(ap):
                return ap.rearrange("p (t a) -> p t a", a=1).to_broadcast((P, T, E1))

            def by_expert(ap, n=T):
                return ap.rearrange("p (a e) -> p a e", a=1).to_broadcast((P, n, E1))

            for o, i_k in ((o1, i1), (o2, i2)):
                ch(nc.vector.tensor_tensor(o, by_expert(iota[:, 0:E1]), by_node(i_k), ALU.is_equal))
                ch(nc.vector.tensor_tensor(o, o, by_node(valid[:, :]), ALU.mult))
            nc.vector.tensor_tensor(cnt_, o1_, o2_, ALU.add).then_inc(S("f1_cnt"), 1)
            v.wait_ge(S("f1_rank"), 1)
            ch(nc.vector.tensor_copy(rk_, PS[:, 5, 0:T * E1]))
            ch(nc.vector.tensor_copy(cnt_, PS[:, 6, 0:T * E1]))
            for e in range(E1):
                ins = nc.vector.tensor_tensor_scan(out=lg[:, :, e], data0=ones[:, 0:T], data1=cnt[:, :, e],
                                                   initial=0.0, op0=ALU.mult, op1=ALU.add)
            ch(ins)
            ch(nc.vector.tensor_scalar(eji_[:, 0:E1].bitcast(I32), lg[:, T - 1, :], 1.0 / P, 0.498, ALU.mult, ALU.add))
            ch(nc.vector.tensor_copy(nt_, eji_[:, 0:E1].bitcast(I32)))
            ch(nc.vector.tensor_tensor_scan(out=te_, data0=ones[:, 0:E1], data1=nt_, initial=0.0,
                                            op0=ALU.mult, op1=ALU.add))
            ch(nc.vector.tensor_tensor(ts_, te_, nt_, ALU.subtract))
            ch(nc.vector.tensor_scalar(ts_, ts_, float(P), None, ALU.mult))
            ch(nc.vector.tensor_tensor(rk_, rk_, lg_, ALU.add))
            ch(nc.vector.tensor_tensor(rk_, rk_, cnt_, ALU.subtract))
            ch(nc.vector.tensor_tensor(rk, rk, by_expert(ts_), ALU.add))
            for k, o in enumerate((o1, o2)):
                slot_f = sc[:, 4 + k, :]
                ch(nc.vector.tensor_tensor(o, o, rk, ALU.mult))
                ch(nc.vector.tensor_reduce(out=slot_f, in_=o, axis=AX.X, op=ALU.add))
                ch(nc.vector.tensor_scalar(sc[:, 6, :], valid[:, :], -1.0, 1.0, ALU.mult, ALU.add))
                ch(nc.vector.tensor_scalar(sc[:, 7, 0:1], pcol[:, 0:1], float(SLOTS + k * P), None, ALU.add))
                ch(nc.vector.scalar_tensor_tensor(out=slot_f, in0=sc[:, 6, :], scalar=sc[:, 7, 0:1], in1=slot_f,
                                                  op0=ALU.mult, op1=ALU.add))
            v.wait_ge(S("w_gate"), 48)
            stage_end(v, 9)
            for k in range(TOPK):
                ch(nc.vector.tensor_copy(slots[:, k, :], sc[:, 4 + k, :]))
            v.sem_inc(S("f1_slots"), 1)
            jj = iota[:, 0:NTILE + 2].rearrange("p (j a) -> p j a", a=1).to_broadcast((P, NTILE + 2, E1))
            ch(nc.vector.tensor_tensor(wide, by_expert(te_, NTILE + 2), jj, ALU.is_le))
            ch(nc.vector.tensor_reduce(out=ej_[:, 0:NTILE + 2], in_=wide, axis=AX.X, op=ALU.add))
            ch(nc.vector.tensor_scalar(ej_[:, 0:NTILE + 2], ej_[:, 0:NTILE + 2], float(E1 - 1), None, ALU.min))
            ch(nc.vector.tensor_copy(eji[:, 0:NTILE + 2], ej_[:, 0:NTILE + 2]))
            ch(nc.vector.memset(b3[0:96, :], 0.0))
            for k in range(3):
                ch(nc.vector.tensor_copy(b3[32 * k:32 * k + E1, :], b2f[0:E1, :]))
                if k < 2:
                    ch(nc.vector.tensor_copy(b2g[0:E1, :], b3[32 * k:32 * k + E1, :]))
                    ch(nc.vector.tensor_tensor(b2f[0:E1, :], b2f[0:E1, :], b2g[0:E1, :], ALU.subtract))
            ch(nc.vector.tensor_scalar(pcol[:, 1:2], pcol[:, 0:1], 32.0, -32.0, ALU.is_ge, ALU.mult))
            ch(nc.vector.tensor_tensor(sc[:, 7, 0:1], pcol[:, 0:1], pcol[:, 1:2], ALU.add))
            ch(nc.vector.tensor_scalar(pcol[:, 1:2], pcol[:, 0:1], 64.0, -32.0, ALU.is_ge, ALU.mult))
            ch(nc.vector.tensor_tensor(pcol[:, 1:2], pcol[:, 1:2], sc[:, 7, 0:1], ALU.add))
            v.sem_inc(S("f1_b3"), 1)
            v.wait_ge(S("f1_scattered"), 1)
            v.wait_ge(S("w_f1"), 64)
            v.wait_ge(S("w_b1"), 16)

            def expert_weights(n, k):
                e = v.value_load(eji[0:1, ds(n, 1)], min_val=0, max_val=E1 - 1)
                nc.vector.tensor_copy(b1s[:, k, :], tile_of(b1t, e))
                nc.vector.tensor_copy(w1s_[:, k * KD * F1:(k + 1) * KD * F1],
                                      e_w1[:, ds(e, 1), :, :].rearrange("p a k f -> p (a k f)")).then_inc(S("f1_w"), 1)

            def pick_bias(n, k):
                nc.vector.tensor_scalar(sel[0:96, k, :], ej_[0:96, ds(n, 1)].to_broadcast((96, P)),
                                        pcol[0:96, 1:2], None, ALU.is_equal).then_inc(S("f1_sel"), 1)

            for k in range(2):
                expert_weights(k, k)
                pick_bias(k, k)
            nc.vector.sem_inc(S("f1_ys"), 2)
            with v.Fori(0, PAIRS) as i:
                for k in range(2):
                    n = i * 2 + k
                    v.wait_ge(S("f1_h"), n + 1)
                    v.wait_ge(S("f1_ht"), n + 1)
                    expert_weights(n + 2, k)
                for k in range(2):
                    n = i * 2 + k
                    v.wait_ge(S("f1_y"), n + 1 + 2)
                    v.wait_ge(S("f1_ys_free"), n + 1)
                    nc.vector.tensor_copy(ys[:, k, :], PS[:, 6 + k, 0:D]).then_inc(S("f1_ys"), 1)
                    pick_bias(n + 2, k)
            stage_end(v, 10)
            v.wait_ge(S("w_f1n"), 32)
            nc.vector.sem_inc(S("f1_cmb"), U)

            def add_row(i, u, k, done):
                t = i * U + u
                nc.vector.scalar_tensor_tensor(out=tile_of(MB, t), in0=cmb[:, u, k, :], scalar=col((p1, p2)[k], t),
                                               in1=tile_of(MB, t), op0=ALU.mult, op1=ALU.add).then_inc(S(done), 1)

            def combine(i):
                for u in range(U + 1):
                    if u < U:
                        v.wait_ge(S(f"f1_rows{u}"), (i + 1) * 16 * TOPK)
                        add_row(i, u, 0, "f1_cmb0")
                    if u > 0:
                        v.wait_ge(S("f1_cmb0"), i * U + u)
                        add_row(i, u - 1, 1, "f1_cmb")
                v.wait_ge(S("f1_cmb"), i * U + 2 * U)
                chunk_stats(v, ch, i)

            combine(0)
            chunk_var(v)
            chunk_scale(v, ch, NCH, 0)
            with v.Fori(1, NI) as i:
                ch.enter(i - 1, EPILOGUE)
                combine(i)
                v.wait_ge(S("mbn"), NCH + i)
                chunk_var(v)
                chunk_add(v, ch, i - 1, gb1, True)
                chunk_scale(v, ch, NCH, i)
            ch.leave(NI - 1)
            v.wait_ge(S("mbn"), NCH + NI)
            chunk_add(v, ch, NI - 1, gb1, True)


def kernel(**inputs):
    import concourse.bacc as bacc
    from concourse.bass_utils import run_bass_kernel_spmd

    a = {k: np.asarray(v) for k, v in inputs.items()}
    channels = np.arange(TD).reshape(HEADS, 3, HC).transpose(1, 0, 2).reshape(-1)
    pointwise = a["L0_mix_w_pw"][channels, :, 0].reshape(TD // HC, HC, HC).transpose(0, 2, 1).reshape(TD, HC)

    def by_partition(v):
        return np.swapaxes(v.reshape(*v.shape[:-1], -1, P), -1, -2)

    laid = {
        "x": a["x"], "src": a["src"], "dst": a["dst"], "edge_weight": a["edge_weight"],
        "g0_w1": a["L0_gnn_W1"].T, "g0_b1": a["L0_gnn_b1"], "g0_w2": a["L0_gnn_W2"].T, "g0_b2": a["L0_gnn_b2"],
        "wc": a["L0_mix_w_qkv"][channels, :, 2].T,
        "bn_gamma": by_partition(a["L0_mix_bn_gamma"][channels]), "bn_beta": by_partition(a["L0_mix_bn_beta"][channels]),
        "w_dw": by_partition(a["L0_mix_w_dw"][channels, 0, 2]), "w_pw": pointwise,
        "w_res": a["L0_mix_w_res"][:, :, 0].T, "b_res": a["L0_mix_b_res"],
        "f0_wr": a["L0_ffn_Wr"], "f0_br": a["L0_ffn_br"], "f0_w1": a["L0_ffn_W1"], "f0_b1": by_partition(a["L0_ffn_b1"]),
        "f0_w2": a["L0_ffn_W2"], "f0_b2": a["L0_ffn_b2"], "f0_gamma": a["L0_ffn_gamma"], "f0_beta": a["L0_ffn_beta"],
        "g1_w1": a["L1_gnn_W1"], "g1_b1": by_partition(a["L1_gnn_b1"]), "g1_w2": a["L1_gnn_W2"], "g1_b2": a["L1_gnn_b2"],
        "m1_kw": by_partition(a["L1_mix_kln_weight"].reshape(-1)), "m1_kb": by_partition(a["L1_mix_kln_bias"].reshape(-1)),
        "m1_vw": a["L1_mix_vln_weight"].reshape(-1), "m1_vb": a["L1_mix_vln_bias"].reshape(-1),
        "f1_wg": a["L1_ffn_gate_w"], "f1_bg": a["L1_ffn_gate_b"], "f1_w1": a["L1_ffn_w1"], "f1_b1": by_partition(a["L1_ffn_b1"]),
        "f1_w2": a["L1_ffn_w2"], "f1_b2": a["L1_ffn_b2"], "f1_gamma": a["L1_ffn_gamma"], "f1_beta": a["L1_ffn_beta"],
    }
    laid = {k: np.ascontiguousarray(v) for k, v in laid.items()}
    nc = bacc.Bacc("TRN2", target_bir_lowering=False, num_devices=1)
    dram = {k: nc.dram_tensor(f"in_{k}", v.shape, mybir.dt.from_np(v.dtype), kind="ExternalInput").ap()
            for k, v in laid.items()}
    out = nc.dram_tensor("out_x", (N, D), F32, kind="ExternalOutput").ap()
    bass_gps_kernel(nc, dram, out)
    got = run_bass_kernel_spmd(nc, [{f"in_{k}": v for k, v in laid.items()}], core_ids=[0])
    return got.results[0]["out_x"]
```
